# Optimizing a Trainium2 kernel written in Bass

```python
import numpy as np
import jax
import jax.numpy as jnp

def _softmax(x, axis=-1):
    return jax.nn.softmax(x, axis=axis)

def _gelu(x):
    return jax.nn.gelu(x, approximate=True)

def _silu(x):
    return jax.nn.silu(x)

def _sigmoid(x):
    return jax.nn.sigmoid(x)

def _layernorm(x, axis=-1, eps=1e-05):
    m = jnp.mean(x, axis=axis, keepdims=True)
    v = jnp.var(x, axis=axis, keepdims=True)
    return (x - m) / jnp.sqrt(v + eps)

def _scatter_add(tgt, idx, src, axis=0):
    return tgt.at[idx].add(src)

def _segment_sum(src, seg, n):
    return jax.ops.segment_sum(src, seg, n)
kernel_name = 'mk_gnn_preln_d4_gnn_r32_75b07d'

def setup_inputs(seed: int=0):
    np.random.seed(seed)
    _w = jnp.asarray

    def _rec_inputs():
        import jax
        import jax.numpy as jnp
        _gk = jax.random.key(seed)
        x = -0.0002117 + 1 * jax.random.normal(jax.random.fold_in(_gk, 1), (3125, 256), jnp.float32)
        src = jax.random.randint(jax.random.fold_in(_gk, 2), (50000,), 0, 3125, jnp.int32)
        dst = jnp.minimum((3125 * jax.random.uniform(jax.random.fold_in(_gk, 3), (50000,)) ** 2.0).astype(jnp.int32), 99999)
        _o = jnp.argsort(dst, stable=True)
        src = src[_o]
        dst = dst[_o]
        edge_attr_3 = 0.000279007 + 1.00013 * jax.random.normal(jax.random.fold_in(_gk, 12), (50000, 3), jnp.float32)
        edge_attr_64 = 0.000279952 + 1.00013 * jax.random.normal(jax.random.fold_in(_gk, 13), (50000, 64), jnp.float32)
        edge_weight = jax.random.uniform(jax.random.fold_in(_gk, 15), (50000,), jnp.float32, 0.0, 1)
        return (x, src, dst, edge_attr_3, edge_attr_64, edge_weight)
    x, src, dst, edge_attr_3, edge_attr_64, edge_weight = _rec_inputs()

    def _L0_gnn_setup():
        import jax, jax.numpy as jnp
        import numpy as np
        N_NODES = 3125
        N_EDGES = 50000
        IN_FEATS = 256
        OUT_FEATS = 64
        NHEAD = 4
        ALPHA = 0.2
        key = jax.random.key(seed)
        k1, k2, k3, k4, k5, k6 = jax.random.split(key, 6)
        stdv_w = np.sqrt(6.0 / (IN_FEATS + OUT_FEATS * NHEAD))
        stdv_a = np.sqrt(6.0 / (NHEAD + OUT_FEATS))
        return {'x': jax.random.normal(k1, (N_NODES, IN_FEATS), dtype=jnp.float32), 'W': jax.random.uniform(k2, (IN_FEATS, OUT_FEATS * NHEAD), minval=-stdv_w, maxval=stdv_w, dtype=jnp.float32), 'a_l': jax.random.uniform(k3, (1, NHEAD, OUT_FEATS), minval=-stdv_a, maxval=stdv_a, dtype=jnp.float32), 'a_r': jax.random.uniform(k4, (1, NHEAD, OUT_FEATS), minval=-stdv_a, maxval=stdv_a, dtype=jnp.float32), 'row': jax.random.randint(k5, (N_EDGES,), 0, N_NODES, dtype=jnp.int32), 'col': jax.random.randint(k6, (N_EDGES,), 0, N_NODES, dtype=jnp.int32)}
    _L0_gnn_all = _L0_gnn_setup()
    _L0_gnn_in = {k: v for k, v in _L0_gnn_all.items() if k in ('W', 'a_l', 'a_r')}
    del _L0_gnn_all

    def _L1_gnn_setup():
        import jax, jax.numpy as jnp
        import numpy as np
        N_NODES = 3125
        N_EDGES = 100000
        DIM = 256
        PRESERVE = 0.1

        def _gcn_conv(x, W, b, src, dst, ew, n_nodes):
            loop = jnp.arange(n_nodes, dtype=src.dtype)
            src2 = jnp.concatenate([src, loop])
            dst2 = jnp.concatenate([dst, loop])
            ew2 = jnp.concatenate([ew, jnp.ones((n_nodes,), dtype=ew.dtype)])
            deg = jax.ops.segment_sum(ew2, dst2, num_segments=n_nodes)
            dinv = jnp.where(deg > 0, jax.lax.rsqrt(jnp.maximum(deg, 1e-30)), 0.0)
            norm = dinv[src2] * ew2 * dinv[dst2]
            xw = x @ W
            msg = xw[src2] * norm[:, None]
            out = jax.ops.segment_sum(msg, dst2, num_segments=n_nodes)
            return out + b
        key = jax.random.key(seed)
        k = jax.random.split(key, 8)
        skill_embed = jax.random.normal(k[0], (N_NODES, DIM), dtype=jnp.float32)
        adj_list = jax.random.randint(k[1], (2, N_EDGES), 0, N_NODES, dtype=jnp.int64)
        edge_attr = jax.random.uniform(k[2], (N_EDGES,), dtype=jnp.float32)
        s = 1.0 / np.sqrt(DIM)
        W1 = jax.random.uniform(k[3], (DIM, DIM), dtype=jnp.float32, minval=-s, maxval=s)
        b1 = jnp.zeros((DIM,), dtype=jnp.float32)
        W2 = jax.random.uniform(k[4], (DIM, DIM), dtype=jnp.float32, minval=-s, maxval=s)
        b2 = jnp.zeros((DIM,), dtype=jnp.float32)
        return {'skill_embed': skill_embed, 'adj_list': adj_list, 'edge_attr': edge_attr, 'W1': W1, 'b1': b1, 'W2': W2, 'b2': b2}
    _L1_gnn_all = _L1_gnn_setup()
    _L1_gnn_in = {k: v for k, v in _L1_gnn_all.items() if k in ('W1', 'b1', 'W2', 'b2')}
    del _L1_gnn_all

    def _L2_gnn_setup():
        import jax, jax.numpy as jnp
        import numpy as np
        N, E = (625, 10000)
        IN, OUT, EC = (256, 256, 64)
        BN_EPS = 1e-05
        key = jax.random.key(seed)
        ks = jax.random.split(key, 8)

        def lin(k, fan_in, fan_out):
            bound = 1.0 / np.sqrt(fan_in)
            return jax.random.uniform(k, (fan_in, fan_out), jnp.float32, -bound, bound)
        return {'x': jax.random.normal(ks[0], (N, IN), jnp.float32), 'edge_index': jax.random.randint(ks[1], (2, E), 0, N), 'edge_attr': jax.random.normal(ks[2], (E, EC), jnp.float32), 'W_edge': lin(ks[3], EC, IN), 'W_rel': lin(ks[4], IN, OUT), 'b_rel': jnp.zeros((OUT,), jnp.float32), 'W_root': lin(ks[5], IN, OUT), 'gamma': jnp.ones((OUT,), jnp.float32), 'beta': jnp.zeros((OUT,), jnp.float32), 'W_res': lin(ks[6], IN, OUT)}
    _L2_gnn_all = _L2_gnn_setup()
    _L2_gnn_in = {k: v for k, v in _L2_gnn_all.items() if k in ('W_edge', 'W_rel', 'b_rel', 'W_root', 'gamma', 'beta', 'W_res')}
    del _L2_gnn_all

    def _L3_gnn_setup():
        import jax, jax.numpy as jnp
        import numpy as np
        N_SPATIAL = 65160
        N_SPHERE = 40962
        N = N_SPATIAL + N_SPHERE
        E = 12500
        D = 256
        S = 3
        EPS = 1e-05

        def _layer_norm(x, g, o):
            mu = jnp.mean(x, axis=-1, keepdims=True)
            var = jnp.mean(jnp.square(x - mu), axis=-1, keepdims=True)
            return (x - mu) * jax.lax.rsqrt(var + EPS) * g + o
        key = jax.random.key(seed)
        ks = jax.random.split(key, 12)
        sc = 0.02
        edge_in = 3 + 2 * D
        node_in = 2 * D
        return {'nodes': jax.random.normal(ks[0], (N, D), jnp.float32), 'edges': jax.random.normal(ks[1], (E, 3), jnp.float32), 'senders': jax.random.randint(ks[2], (E,), 0, N_SPATIAL, jnp.int32), 'receivers': jax.random.randint(ks[3], (E,), N_SPATIAL, N, jnp.int32), 'W1e': jax.random.normal(ks[4], (S, edge_in, D), jnp.float32) * sc, 'b1e': jnp.zeros((S, D), jnp.float32), 'ge': jnp.ones((S, D), jnp.float32), 'oe': jnp.zeros((S, D), jnp.float32), 'W2e': jax.random.normal(ks[5], (S, D, D), jnp.float32) * sc, 'b2e': jnp.zeros((S, D), jnp.float32), 'W1n': jax.random.normal(ks[6], (S, node_in, D), jnp.float32) * sc, 'b1n': jnp.zeros((S, D), jnp.float32), 'gn': jnp.ones((S, D), jnp.float32), 'on': jnp.zeros((S, D), jnp.float32), 'W2n': jax.random.normal(ks[7], (S, D, D), jnp.float32) * sc, 'b2n': jnp.zeros((S, D), jnp.float32)}
    _L3_gnn_all = _L3_gnn_setup()
    _L3_gnn_in = {k: v for k, v in _L3_gnn_all.items() if k in ('W1e', 'b1e', 'ge', 'oe', 'W2e', 'b2e', 'W1n', 'b1n', 'gn', 'on', 'W2n', 'b2n')}
    del _L3_gnn_all
    return {'x': x, 'src': src, 'dst': dst, 'edge_attr_3': edge_attr_3, 'edge_attr_64': edge_attr_64, 'edge_weight': edge_weight, 'L0_gnn_W': _L0_gnn_in['W'], 'L0_gnn_a_l': _L0_gnn_in['a_l'], 'L0_gnn_a_r': _L0_gnn_in['a_r'], 'L1_gnn_W1': _L1_gnn_in['W1'], 'L1_gnn_b1': _L1_gnn_in['b1'], 'L1_gnn_W2': _L1_gnn_in['W2'], 'L1_gnn_b2': _L1_gnn_in['b2'], 'L2_gnn_W_edge': _L2_gnn_in['W_edge'], 'L2_gnn_W_rel': _L2_gnn_in['W_rel'], 'L2_gnn_b_rel': _L2_gnn_in['b_rel'], 'L2_gnn_W_root': _L2_gnn_in['W_root'], 'L2_gnn_gamma': _L2_gnn_in['gamma'], 'L2_gnn_beta': _L2_gnn_in['beta'], 'L2_gnn_W_res': _L2_gnn_in['W_res'], 'L3_gnn_W1e': _L3_gnn_in['W1e'], 'L3_gnn_b1e': _L3_gnn_in['b1e'], 'L3_gnn_ge': _L3_gnn_in['ge'], 'L3_gnn_oe': _L3_gnn_in['oe'], 'L3_gnn_W2e': _L3_gnn_in['W2e'], 'L3_gnn_b2e': _L3_gnn_in['b2e'], 'L3_gnn_W1n': _L3_gnn_in['W1n'], 'L3_gnn_b1n': _L3_gnn_in['b1n'], 'L3_gnn_gn': _L3_gnn_in['gn'], 'L3_gnn_on': _L3_gnn_in['on'], 'L3_gnn_W2n': _L3_gnn_in['W2n'], 'L3_gnn_b2n': _L3_gnn_in['b2n']}

def reference(x, src, dst, edge_attr_3, edge_attr_64, edge_weight, L0_gnn_W, L0_gnn_a_l, L0_gnn_a_r, L1_gnn_W1, L1_gnn_b1, L1_gnn_W2, L1_gnn_b2, L2_gnn_W_edge, L2_gnn_W_rel, L2_gnn_b_rel, L2_gnn_W_root, L2_gnn_gamma, L2_gnn_beta, L2_gnn_W_res, L3_gnn_W1e, L3_gnn_b1e, L3_gnn_ge, L3_gnn_oe, L3_gnn_W2e, L3_gnn_b2e, L3_gnn_W1n, L3_gnn_b1n, L3_gnn_gn, L3_gnn_on, L3_gnn_W2n, L3_gnn_b2n):
    import jax
    import jax.numpy as jnp

    def _L0_gnn_ref(x, W, a_l, a_r, row, col):
        import jax, jax.numpy as jnp
        import numpy as np
        N_NODES = 3125
        N_EDGES = 50000
        IN_FEATS = 256
        OUT_FEATS = 64
        NHEAD = 4
        ALPHA = 0.2
        n = x.shape[0]
        h = (x @ W).reshape(n, NHEAD, OUT_FEATS)
        h = jnp.where(jnp.isnan(h), 0.0, h)
        h_l = (a_l * h).sum(-1)
        h_r = (a_r * h).sum(-1)
        e = h_l[row] + h_r[col]
        e = jnp.where(e > 0, e, ALPHA * e)
        m = jax.ops.segment_max(e, row, num_segments=n)
        m = jnp.where(jnp.isfinite(m), m, 0.0)
        ex = jnp.exp(e - m[row])
        denom = jax.ops.segment_sum(ex, row, num_segments=n)
        att = ex / (denom[row] + 1e-16)
        msg = att[:, :, None] * h[col]
        out = jax.ops.segment_sum(msg, row, num_segments=n)
        return out.reshape(n, NHEAD * OUT_FEATS)

    def _L1_gnn_ref(skill_embed, adj_list, edge_attr, W1, b1, W2, b2):
        import jax, jax.numpy as jnp
        import numpy as np
        N_NODES = 3125
        N_EDGES = 100000
        DIM = 256
        PRESERVE = 0.1

        def _gcn_conv(x, W, b, src, dst, ew, n_nodes):
            loop = jnp.arange(n_nodes, dtype=src.dtype)
            src2 = jnp.concatenate([src, loop])
            dst2 = jnp.concatenate([dst, loop])
            ew2 = jnp.concatenate([ew, jnp.ones((n_nodes,), dtype=ew.dtype)])
            deg = jax.ops.segment_sum(ew2, dst2, num_segments=n_nodes)
            dinv = jnp.where(deg > 0, jax.lax.rsqrt(jnp.maximum(deg, 1e-30)), 0.0)
            norm = dinv[src2] * ew2 * dinv[dst2]
            xw = x @ W
            msg = xw[src2] * norm[:, None]
            out = jax.ops.segment_sum(msg, dst2, num_segments=n_nodes)
            return out + b
        src, dst = (adj_list[0], adj_list[1])
        n = skill_embed.shape[0]
        temp = skill_embed
        out = _gcn_conv(skill_embed, W1, b1, src, dst, edge_attr, n)
        temp = (1.0 - PRESERVE) * out + PRESERVE * temp
        out = _gcn_conv(temp, W2, b2, src, dst, edge_attr, n)
        temp = (1.0 - PRESERVE) * out + PRESERVE * temp
        return temp

    def _L2_gnn_ref(x, edge_index, edge_attr, W_edge, W_rel, b_rel, W_root, gamma, beta, W_res):
        import jax, jax.numpy as jnp
        import numpy as np
        N, E = (625, 10000)
        IN, OUT, EC = (256, 256, 64)
        BN_EPS = 1e-05
        src, dst = (edge_index[0], edge_index[1])
        e = edge_attr @ W_edge
        msg = x[src] * e
        agg = jax.ops.segment_sum(msg, dst, num_segments=x.shape[0])
        h = agg @ W_rel + b_rel + x @ W_root
        h = jax.nn.relu(h)
        mean = h.mean(axis=0)
        var = ((h - mean) ** 2).mean(axis=0)
        h = (h - mean) * jax.lax.rsqrt(var + BN_EPS) * gamma + beta
        return h + x @ W_res

    def _L3_gnn_ref(nodes, edges, senders, receivers, W1e, b1e, ge, oe, W2e, b2e, W1n, b1n, gn, on, W2n, b2n):
        import jax, jax.numpy as jnp
        import numpy as np
        N_SPATIAL = 65160
        N_SPHERE = 40962
        N = N_SPATIAL + N_SPHERE
        E = 12500
        D = 256
        S = 3
        EPS = 1e-05

        def _layer_norm(x, g, o):
            mu = jnp.mean(x, axis=-1, keepdims=True)
            var = jnp.mean(jnp.square(x - mu), axis=-1, keepdims=True)
            return (x - mu) * jax.lax.rsqrt(var + EPS) * g + o
        n_nodes = nodes.shape[0]
        n_steps = W1e.shape[0]
        for s in range(n_steps):
            sn = nodes[senders]
            rn = nodes[receivers]
            edge_inputs = jnp.concatenate([edges, sn, rn], axis=1)
            h = jax.nn.relu(edge_inputs @ W1e[s] + b1e[s])
            h = _layer_norm(h, ge[s], oe[s])
            messages = h @ W2e[s] + b2e[s]
            agg = jax.ops.segment_sum(messages, receivers, num_segments=n_nodes)
            node_inputs = jnp.concatenate([nodes, agg], axis=1)
            h2 = jax.nn.relu(node_inputs @ W1n[s] + b1n[s])
            h2 = _layer_norm(h2, gn[s], on[s])
            nodes = h2 @ W2n[s] + b2n[s]
        return nodes
    edge_index = jnp.stack([src, dst])
    h = jnp.maximum(_layernorm(x, axis=-1), 0.0)
    x = x + _L0_gnn_ref(h, L0_gnn_W, L0_gnn_a_l, L0_gnn_a_r, src, dst)
    h = jnp.maximum(_layernorm(x, axis=-1), 0.0)
    x = x + _L1_gnn_ref(h, edge_index, edge_weight, L1_gnn_W1, L1_gnn_b1, L1_gnn_W2, L1_gnn_b2)
    h = jnp.maximum(_layernorm(x, axis=-1), 0.0)
    x = x + _L2_gnn_ref(h, edge_index, edge_attr_64, L2_gnn_W_edge, L2_gnn_W_rel, L2_gnn_b_rel, L2_gnn_W_root, L2_gnn_gamma, L2_gnn_beta, L2_gnn_W_res)
    h = jnp.maximum(_layernorm(x, axis=-1), 0.0)
    x = x + _L3_gnn_ref(h, edge_attr_3, src, dst, L3_gnn_W1e, L3_gnn_b1e, L3_gnn_ge, L3_gnn_oe, L3_gnn_W2e, L3_gnn_b2e, L3_gnn_W1n, L3_gnn_b1n, L3_gnn_gn, L3_gnn_on, L3_gnn_W2n, L3_gnn_b2n)
    return x

_drawn_inputs = setup_inputs


def setup_inputs(seed=0):
    import zlib

    import numpy as np

    out = dict(_drawn_inputs(seed))
    spreads = {'L1_gnn_b1': (0.0, 0.1),
     'L1_gnn_b2': (0.0, 0.1),
     'L2_gnn_b_rel': (0.0, 0.1),
     'L2_gnn_gamma': (1.0, 0.2),
     'L2_gnn_beta': (0.0, 0.1),
     'L3_gnn_b1e': (0.0, 0.1),
     'L3_gnn_ge': (1.0, 0.2),
     'L3_gnn_oe': (0.0, 0.1),
     'L3_gnn_b2e': (0.0, 0.1),
     'L3_gnn_b1n': (0.0, 0.1),
     'L3_gnn_gn': (1.0, 0.2),
     'L3_gnn_on': (0.0, 0.1),
     'L3_gnn_b2n': (0.0, 0.1)}
    factors = {'edge_attr_3': 2.675, 'edge_weight': 3.465}
    for name, (base, spread) in spreads.items():
        noise = np.random.default_rng([zlib.crc32(name.encode()), seed]).standard_normal(out[name].shape)
        drawn = base * np.exp(spread * noise) if base else spread * noise
        out[name] = jnp.asarray(drawn.astype(out[name].dtype))
    for name, factor in factors.items():
        out[name] = (out[name] * factor).astype(out[name].dtype)
    return out
```

```python
from contextlib import ExitStack

import concourse.bass as bass
from concourse import mybir

F32 = mybir.dt.float32
I32 = mybir.dt.int32
ALU = mybir.AluOpType
ACT = mybir.ActivationFunctionType
AX_X = mybir.AxisListType.X

N, D, E = 3125, 256, 50000
P = 125
T = N // P
HEADS = 4
HD = D // HEADS
G = 2
RING = 4
CAP = G * 128
MOST = (E + T * (CAP - 1)) // CAP
UNITS = -(-MOST // RING) * RING
BLOCKS = UNITS * G
EC = E // P
HW = 8
EA = 64
REC = HW + EA
CH = 8
AW = D + 4
BIG = 1e30
ALPHA = 0.2
EPS = 1e-5
S3 = 3


def turns(eng, total, ring, head, depth, step):
    assert head % ring == 0 and head >= depth
    end = total - total % ring
    for v in range(head):
        step(v, v % ring, lambda lag: v >= lag)
    with eng.Fori(head // ring, end // ring) as lap:
        for r in range(ring):
            step(lap * ring + r, r, lambda lag: True)
    for v in range(end, total + depth):
        step(v, v % ring, lambda lag: 0 <= v - lag < total)


def wait_past(eng, sem, value):
    if isinstance(value, int) and value <= 0:
        return
    eng.wait_ge(sem, value)


class Chain:

    def __init__(self, eng, sem):
        self.eng, self.sem, self.n = eng, sem, 0

    def link(self, ins):
        ins.then_inc(self.sem, 1)
        self.n = self.n + 1
        self.eng.wait_ge(self.sem, self.n)

    def at(self, n):
        self.n = n

    def loop(self, end, per, body):
        base = self.n
        with self.eng.Fori(0, end) as i:
            self.n = base + i * per
            body(i)
        self.n = base + per * end


def build(nc, x, src, dst, edge_attr_3, edge_attr_64, edge_weight, L0_gnn_W, L0_gnn_a_l, L0_gnn_a_r,
          L1_gnn_W1, L1_gnn_b1, L1_gnn_W2, L1_gnn_b2, L2_gnn_W_edge, L2_gnn_W_rel, L2_gnn_b_rel,
          L2_gnn_W_root, L2_gnn_gamma, L2_gnn_beta, L2_gnn_W_res, L3_gnn_W1e, L3_gnn_b1e, L3_gnn_ge,
          L3_gnn_oe, L3_gnn_W2e, L3_gnn_b2e, L3_gnn_W1n, L3_gnn_b1n, L3_gnn_gn, L3_gnn_on, L3_gnn_W2n,
          L3_gnn_b2n, out):
    by_dst = nc.dram_tensor("by_dst", (128 * BLOCKS, REC), F32, kind="Internal").ap()
    by_src = nc.dram_tensor("by_src", (128 * BLOCKS, 2), F32, kind="Internal").ap()
    rows_h = nc.dram_tensor("rows_h", (N, AW), F32, kind="Internal").ap()
    rows_hr = nc.dram_tensor("rows_hr", (N, HEADS), F32, kind="Internal").ap()
    rows = nc.dram_tensor("rows", (N, D), F32, kind="Internal").ap()

    with ExitStack() as ctx:
        def sb(name, shape, dt=F32):
            return ctx.enter_context(nc.sbuf_tensor(name, shape, dt))

        def sem(name):
            return ctx.enter_context(nc.semaphore(name))

        X = sb("X", [P, T * D])
        KEEP = sb("KEEP", [P, T * D])
        Y = sb("Y", [P, T * D])
        ACC = sb("ACC", [P, T * AW])
        BT = sb("BT", [128, T * D])
        HL = sb("HL", [P, T * HEADS])
        MX = sb("MX", [P, T * HEADS])
        HM = sb("HM", [P, T * 2 * HEADS])
        CNT = sb("CNT", [P, T * 2])
        DINV = sb("DINV", [P, T])
        RDEN = sb("RDEN", [P, T * HEADS])
        MV = sb("MV", [P, T * 2])
        SD = sb("SD", [P, T])
        RS = sb("RS", [P, T])
        ST = sb("ST", [P, 6])
        AG = sb("AG", [P, 2])
        EPSC = sb("EPSC", [128, 1])

        DH = sb("DH", [128, BLOCKS * HW])
        SH = sb("SH", [128, BLOCKS * 2])
        DIDX = sb("DIDX", [128, BLOCKS], I32)
        SIDX = sb("SIDX", [128, BLOCKS], I32)
        DTILE = sb("DTILE", [1, UNITS], I32)
        STILE = sb("STILE", [1, UNITS], I32)

        IOTA = sb("IOTA", [128, UNITS])
        IDENT = sb("IDENT", [128, 128])
        ONES = sb("ONES", [128, 128])
        LTRI = sb("LTRI", [128, 128])

        W0 = sb("W0", [128, 2 * D])
        WA = sb("WA", [128, 2 * D])
        WB = sb("WB", [128, 2 * D])
        WC = sb("WC", [128, 2 * D])
        WD = sb("WD", [128, 2 * D])
        WF = sb("WF", [128, 2 * D])
        WE = sb("WE", [128, D])
        BIAS = sb("BIAS", [P, 8 * D])
        ALR = BIAS[:, 0:2 * D]

        gidx = sb("gidx", [128, RING * G], I32)
        gat = sb("gat", [128, RING, G, AW])
        oh = sb("oh", [128, RING, G, 128])
        ohw = sb("ohw", [128, 2, G, P])
        ohT = sb("ohT", [128, RING, G * 128])
        msg = sb("msg", [128, RING, G, AW])
        small = sb("small", [128, 64])
        wide = sb("wide", [P, 4, AW])
        staged = sb("staged", [P, 2, D])
        cand = msg[:, :, :, :].rearrange("p r g c -> p (r g c)")[:, 0:2 * HEADS * G * P].rearrange(
            "p (s h g n) -> p s h g n", s=2, h=HEADS, g=G)
        hT = ohT[:, 0:2, 0:2 * P]

        psum = [ctx.enter_context(nc.psum_tensor(f"ps{k}", [128, 512], F32)) for k in range(8)]

        key_of = {"dst": Y[:, 0:EC], "src": Y[:, EC:2 * EC]}
        bucket = Y[:, 2 * EC:3 * EC]
        rank = Y[:, 3 * EC:4 * EC]
        mask = Y[:, 4 * EC:5 * EC]
        prefix = Y[:, 5 * EC:6 * EC]
        ones_row = Y[:, 6 * EC:7 * EC]
        raw = {"dst": Y[:, 7 * EC:8 * EC].bitcast(I32), "src": Y[:, 8 * EC:9 * EC].bitcast(I32)}
        weight_in = Y[:, 9 * EC:10 * EC]
        attr_in = Y[:, 10 * EC:13 * EC]
        place_i = Y[:, 13 * EC:14 * EC].bitcast(I32)
        place_j = Y[:, 14 * EC:15 * EC].bitcast(I32)
        header = BT[0:P, 0:HW * EC]
        pair = BT[0:P, HW * EC:(HW + 2) * EC]
        place_of = {"dst": BT[0:P, 10 * EC:11 * EC].bitcast(I32), "src": BT[0:P, 11 * EC:12 * EC].bitcast(I32)}
        record = BT[0:P, 12 * EC:12 * EC + 2 * CH * REC].rearrange("p (s j c) -> p s j c", s=2, c=REC)
        AT = 12 * EC + 2 * CH * REC
        place_now = BT[0:P, AT:AT + 2 * CH].bitcast(I32)
        AT += 2 * CH
        pair_now = BT[0:P, AT:AT + 4 * CH].rearrange("p (s j c) -> p s j c", s=2, c=2)
        AT += 4 * CH
        threshold = sb("threshold", [128, T])
        count = sb("count", [P, T])
        units_i = sb("units_i", [128, T], I32)
        units = sb("units", [128, T])
        unit_end = sb("unit_end", [128, T])
        unit_start = sb("unit_start", [128, T])
        base = sb("base", [P, T])
        tile_f = Y[0:1, 15 * EC:15 * EC + UNITS]

        inputs_in = sem("inputs_in")
        consts = sem("consts")
        threshold_ready = sem("threshold_ready")
        counted = sem("counted")
        prefixed = sem("prefixed")
        blanked = sem("blanked")
        blank_out = sem("blank_out")
        placed = sem("placed")
        attr_landed = [sem(f"attr_landed{r}") for r in range(2)]
        scattered = [sem(f"scattered{r}") for r in range(2)]
        pairs_out = [sem(f"pairs_out{r}") for r in range(2)]
        turn_ready = sem("turn_ready")
        apart = sem("apart")
        lists_in = {"dst": sem("dst_list_in"), "src": sem("src_list_in")}
        lists_ready = {"dst": sem("dst_list_ready"), "src": sem("src_list_ready")}
        weights_in = sem("weights_in")
        chain_a = sem("chain_a")
        chain_b = sem("chain_b")
        chain_u = sem("chain_u")
        accs_clear = sem("accs_clear")
        moments = sem("moments")
        rooted = sem("rooted")
        made = sem("made")
        staged_in = sem("staged_in")
        turned = sem("turned")
        turned_in = sem("turned_in")
        projected = sem("projected")
        drawn = sem("drawn")
        rows_out = [sem(f"rows_out{r}") for r in range(2)]
        gidx_ready = sem("gidx_ready")
        landed = [sem(f"landed{r}") for r in range(RING)]
        oh_ready = sem("oh_ready")
        part_ready = sem("part_ready")
        acc_done = sem("acc_done")
        max_oh = sem("max_oh")
        max_neg = sem("max_neg")
        max_rows = sem("max_rows")
        max_done = sem("max_done")
        oh_turned = sem("oh_turned")
        ohT_ready = sem("ohT_ready")
        mid_ready = sem("mid_ready")
        scores = sem("scores")
        probs = sem("probs")
        msgs = sem("msgs")
        msg_relu = sem("msg_relu")
        msg_stats = sem("msg_stats")
        msg_sd = sem("msg_sd")
        attrs_in = [sem(f"attrs_in{r}") for r in range(RING)]
        bn_sum = sem("bn_sum")
        bn_sq = sem("bn_sq")
        bn_sqsum = sem("bn_sqsum")
        hm_ready = sem("hm_ready")
        recip = sem("recip")
        ohw_ready = sem("ohw_ready")
        finished = sem("finished")
        out_done = sem("out_done")

        PHASES = ["l0", "l1a", "l1b", "l2in", "l2out", "l3in"]
        for s in range(S3):
            PHASES += [f"agg{s}", f"mix{s}", f"node{s}"] + ([f"next{s}"] if s < S3 - 1 else [])
        MAKES = [p for p in PHASES if p not in ("l2out",) and not p.startswith(("mix", "next"))]
        ROWS = ["l0", "l0", "l1a", "l1b", "l2in", "l3in", "next0", "next1"]
        SCATTERS = ["deg", "l0", "l1a", "l1b", "l2", "e0", "e1", "e2"]
        GATHERS = ["max", "l0", "l1a", "l1b", "l2", "e0", "e1", "e2"]

        def laps(v, r, ring):
            return v // ring if isinstance(v, int) else (v - r) // ring

        def row_dmas(names, r):
            return 16 * names * ((T + 1 - r) // 2)

        def await_rows(eng, phase):
            k = len(ROWS) - 1 - ROWS[::-1].index(phase) + 1
            for r in range(2):
                eng.wait_ge(rows_out[r], row_dmas(k, r))

        def tile(A, t, lo=0, hi=None, w=D):
            return A[:, bass.ds(t * w + lo, (w if hi is None else hi) - lo)]

        def Wc(W, c):
            return W[:, c * D:(c + 1) * D]

        def bias(k):
            return BIAS[:, k * D:(k + 1) * D]

        def hold(eng, s, value):
            wait_past(eng, s, value)
            eng.sem_inc(apart, 1)

        def attr_slot(r):
            return ohT[:, r, 128:128 + G * EA]

        USERS = {"max": (max_rows, 0), "l0": (msgs, 0), "l1a": (part_ready, 2 * UNITS),
                 "l1b": (part_ready, 3 * UNITS), "l2": (msgs, UNITS)}
        USERS.update({f"e{s}": (msgs, (2 + s) * UNITS) for s in range(S3)})
        TURNS_BEFORE_E = MSGS_BEFORE_E = 2 * UNITS
        LAST = 2
        ROWS_TOTAL = [row_dmas(len(ROWS), r) for r in range(2)]

        block = ctx.enter_context(nc.Block())

        def kcn(W):
            return W.rearrange("(c k) n -> k c n", k=128)

        def two(W):
            return W[:, :].rearrange("p (c n) -> p c n", c=2)

        def row(v):
            return v.partition_broadcast(P)

        INIT = [(two(W0), kcn(L0_gnn_W)), (two(WA), kcn(L1_gnn_W1)), (two(WB), kcn(L1_gnn_W2)),
                (two(WC), kcn(L2_gnn_W_root)), (two(WD), kcn(L2_gnn_W_res)), (two(WF), kcn(L2_gnn_W_rel)),
                (WE[0:EA, :], L2_gnn_W_edge), (WE[EA:2 * EA, :], L2_gnn_W_edge),
                (ALR[:, 0:D], row(L0_gnn_a_l.rearrange("a h f -> (a h f)"))),
                (ALR[:, D:2 * D], row(L0_gnn_a_r.rearrange("a h f -> (a h f)"))),
                (bias(2), row(L1_gnn_b1)), (bias(3), row(L1_gnn_b2)), (bias(4), row(L2_gnn_b_rel)),
                (bias(5), row(L2_gnn_gamma)), (bias(6), row(L2_gnn_beta))]

        def table_loads(s):
            return [(two(W0), kcn(L3_gnn_W1e[s, 3:3 + D, :])), (two(WA), kcn(L3_gnn_W1e[s, 3 + D:3 + 2 * D, :])),
                    (two(WB), kcn(L3_gnn_W1n[s, 0:D, :])), (bias(0), row(L3_gnn_b1e[s, :])),
                    (bias(1), row(L3_gnn_b1n[s, :]))]

        def net_loads(s):
            return [(two(WC), kcn(L3_gnn_W2e[s])), (two(WD), kcn(L3_gnn_W1n[s, D:2 * D, :])),
                    (two(WF), kcn(L3_gnn_W2n[s])), (bias(2), row(L3_gnn_ge[s, :])),
                    (bias(3), row(L3_gnn_oe[s, :])), (bias(4), row(L3_gnn_b2e[s, :])),
                    (bias(5), row(L3_gnn_gn[s, :])), (bias(6), row(L3_gnn_on[s, :])),
                    (bias(7), row(L3_gnn_b2n[s, :]))]

        def await_init(eng):
            eng.wait_ge(weights_in, 16 * len(INIT))

        def await_tables(eng, s):
            eng.wait_ge(tables_in, 16 * len(table_loads(s)) * (s + 1))

        def await_nets(eng, s):
            eng.wait_ge(nets_in, 16 * len(net_loads(s)) * (s + 1))

        edge_rows_in = sem("edge_rows_in")
        tables_in = sem("tables_in")
        nets_in = sem("nets_in")

        @block.sync
        def _(sp):
            def load(out_, in_, s):
                sp.dma_start(out_, in_).then_inc(s, 16)

            load(raw["dst"], dst.rearrange("(p j) -> p j", p=P), inputs_in)
            load(raw["src"], src.rearrange("(p j) -> p j", p=P), inputs_in)
            load(weight_in, edge_weight.rearrange("(p j) -> p j", p=P), inputs_in)
            load(attr_in, edge_attr_3.rearrange("(p j) c -> p (j c)", p=P), inputs_in)
            load(X[:, :].rearrange("p (t n) -> p t n", t=T), x.rearrange("(t p) n -> p t n", p=P), inputs_in)
            for a, b in INIT:
                load(a, b, weights_in)
            sp.wait_ge(blanked, 4)
            nb = 22
            for k in range(BLOCKS // nb):
                load(by_dst.rearrange("(p b) c -> p (b c)", p=128)[:, k * nb * REC:(k + 1) * nb * REC],
                     msg[:, :, :, :].rearrange("p r g c -> p (r g c)")[:, 0:nb * REC], blank_out)
            load(by_src.rearrange("(p b) c -> p (b c)", p=128), SH[:, :], blank_out)

            def attrs(v, r, on):
                wait_past(sp, scattered[r], laps(v, r, 2) * 16 * CH)
                sp.dma_start(record[:, r, :, HW:REC],
                             edge_attr_64.rearrange("(p j) c -> p j c", p=P)[:, bass.ds(v * CH, CH), :]
                             ).then_inc(attr_landed[r], 16)
            turns(sp, EC // CH, 2, 2, 0, attrs)
            for r in range(2):
                sp.wait_ge(scattered[r], EC // CH // 2 * 16 * CH)
            load(DH[:, :].rearrange("p (b c) -> p b c", c=HW),
                 by_dst.rearrange("(p b) c -> p b c", p=128)[:, :, 0:HW], lists_in["dst"])
            for r in range(2):
                sp.wait_ge(pairs_out[r], EC // CH // 2 * 16 * CH)
            load(SH[:, :], by_src.rearrange("(p b) c -> p (b c)", p=128), lists_in["src"])
            sp.wait_ge(lists_ready["src"], 1)
            load(BT[P:128, :].rearrange("p (t n) -> p t n", t=T),
                 L3_gnn_W1e[0, 0:3, :].unsqueeze(1).broadcast_to([3, T, D]), edge_rows_in)
            sp.wait_ge(projected, T * (PHASES.index("l1b") + 1))
            for a, b in table_loads(0):
                load(a, b, tables_in)

            def unit_attrs(v, r, on):
                if not isinstance(v, int) or v >= RING:
                    sp.wait_ge(oh_turned, UNITS + v - RING + 1)
                sp.dma_start(attr_slot(r).rearrange("p (g c) -> p g c", g=G), by_dst.rearrange("(p b) c -> p b c", p=128)
                             [:, bass.ds(v * G, G), HW:REC]).then_inc(attrs_in[r], 16)
            sp.wait_ge(projected, T * (PHASES.index("l2in") + 1))
            turns(sp, UNITS, RING, RING, 0, unit_attrs)
            for s in range(S3):
                if s == 0:
                    sp.wait_ge(finished, 1)
                else:
                    sp.wait_ge(drawn, T * (PHASES.index(f"node{s - 1}") + 1))
                for a, b in net_loads(s):
                    load(a, b, nets_in)
                if s < S3 - 1:
                    sp.wait_ge(acc_done, UNITS * (SCATTERS.index(f"e{s}") + 1))
                    load(BT[P:128, :].rearrange("p (t n) -> p t n", t=T),
                         L3_gnn_W1e[s + 1, 0:3, :].unsqueeze(1).broadcast_to([3, T, D]), edge_rows_in)
                    for a, b in table_loads(s + 1):
                        load(a, b, tables_in)
            sp.wait_ge(finished, LAST)
            sp.dma_start(out.rearrange("(t p) n -> p t n", p=P),
                         X[:, :].rearrange("p (t n) -> p t n", t=T)).then_inc(out_done, 16)
            sp.wait_ge(out_done, 16)
            for r in range(2):
                sp.wait_ge(rows_out[r], ROWS_TOTAL[r])

        @block.gpsimd
        def _(pool):
            pool.iota(IOTA[:, :], pattern=[[1, UNITS]], base=0, channel_multiplier=0,
                      allow_small_or_imprecise_dtypes=True).then_inc(consts, 1)
            pool.memset(ONES[:, :], 1.0).then_inc(consts, 1)
            pool.memset(IDENT[:, :], 0.0).then_inc(consts, 1)
            pool.memset(EPSC[:, :], EPS).then_inc(consts, 1)
            pool.wait_ge(consts, 4)
            pool.affine_select(out=IDENT[:, :], in_=IDENT[:, :], compare_op=ALU.not_equal, fill=1.0, base=0,
                               pattern=[[-1, 128]], channel_multiplier=1).then_inc(consts, 1)
            pool.affine_select(out=LTRI[:, :], in_=ONES[:, :], compare_op=ALU.is_ge, fill=0.0, base=-1,
                               pattern=[[1, 128]], channel_multiplier=-1).then_inc(consts, 1)

            def copies_done(n):
                pool.wait_ge(turn_ready, n)
                pool.sem_inc(apart, 1)

            pool.wait_ge(placed, 1)
            pool.wait_ge(blank_out, 16 * (BLOCKS // 22 + 1))

            def to_dst(v, r, on):
                if not isinstance(v, int) or v >= 2:
                    pool.wait_ge(scattered[r], laps(v, r, 2) * 16 * CH)
                pool.wait_ge(attr_landed[r], (laps(v, r, 2) + 1) * 16)
                pool.sem_inc(apart, 1)
                pool.tensor_copy(record[:, r, :, 0:HW], header[:, bass.ds(v * CH * HW, CH * HW)]
                                 .rearrange("p (j c) -> p j c", c=HW)).then_inc(turn_ready, 1)
                pool.tensor_copy(place_now[:, r * CH:(r + 1) * CH], place_of["dst"][:, bass.ds(v * CH, CH)]
                                 ).then_inc(turn_ready, 1)
                copies_done((v + 1) * 2)
                for j in range(CH):
                    pool.indirect_dma_start(
                        by_dst, bass.IndirectOffsetOnAxis(ap=place_now[:, r * CH + j:r * CH + j + 1], axis=0),
                        record[:, r, j, :], None).then_inc(scattered[r], 16)
            turns(pool, EC // CH, 2, 2, 0, to_dst)
            for r in range(2):
                pool.wait_ge(scattered[r], EC // CH // 2 * 16 * CH)
            pool.wait_ge(placed, 2)

            def to_src(v, r, on):
                wait_past(pool, pairs_out[r], laps(v, r, 2) * 16 * CH)
                pool.sem_inc(apart, 1)
                pool.tensor_copy(pair_now[:, r, :, :], pair[:, bass.ds(v * CH * 2, CH * 2)]
                                 .rearrange("p (j c) -> p j c", c=2)).then_inc(turn_ready, 1)
                pool.tensor_copy(place_now[:, r * CH:(r + 1) * CH], place_of["src"][:, bass.ds(v * CH, CH)]
                                 ).then_inc(turn_ready, 1)
                copies_done(EC // CH * 2 + (v + 1) * 2)
                for j in range(CH):
                    pool.indirect_dma_start(
                        by_src, bass.IndirectOffsetOnAxis(ap=place_now[:, r * CH + j:r * CH + j + 1], axis=0),
                        pair_now[:, r, j, :], None).then_inc(pairs_out[r], 16)
            turns(pool, EC // CH, 2, 2, 0, to_src)

            def gather(name, table, width, index):
                q = GATHERS.index(name)
                used, before = USERS[name]
                if q:
                    last, n = USERS[GATHERS[q - 1]]
                    pool.wait_ge(last, n + UNITS)

                def unit(v, r, on):
                    if not isinstance(v, int) or v >= RING:
                        pool.wait_ge(used, before + v - RING + 1)
                    pool.sem_inc(apart, 1)
                    pool.tensor_copy(gidx[:, r * G:(r + 1) * G], index[:, bass.ds(v * G, G)]
                                     ).then_inc(gidx_ready, 1)
                    pool.wait_ge(gidx_ready, q * UNITS + v + 1)
                    pool.sem_inc(apart, 1)
                    for g in range(G):
                        pool.indirect_dma_start(
                            gat[:, r, g, AW - width:AW] if width == HEADS else gat[:, r, g, 0:width], None, table,
                            bass.IndirectOffsetOnAxis(ap=gidx[:, r * G + g:r * G + g + 1], axis=0)
                            ).then_inc(landed[r], 16)
                turns(pool, UNITS, RING, RING, 0, unit)

            pool.wait_ge(lists_ready["src"], 1)
            await_rows(pool, "l0")
            gather("max", rows_hr, HEADS, SIDX)
            gather("l0", rows_h, AW, SIDX)
            for name in ("l1a", "l1b"):
                await_rows(pool, name)
                gather(name, rows, D, DIDX)
            await_rows(pool, "l2in")
            gather("l2", rows, D, DIDX)
            for s in range(S3):
                await_rows(pool, "l3in" if s == 0 else f"next{s - 1}")
                gather(f"e{s}", rows, D, DIDX)

        @block.scalar
        def _(act):
            def roots(k):
                act.wait_ge(moments, k)
                act.activation(SD[:, :], MV[:, :].rearrange("p (t c) -> p t c", c=2)[:, :, 1], ACT.Sqrt,
                               bias=EPSC[0:P, :]).then_inc(rooted, 1)

            def project(name, A=KEEP, w=D, func=ACT.Copy, row_source=None):
                k = PHASES.index(name) * T
                km = MAKES.index(name) * T if name in MAKES else 0

                def step(t, r, on):
                    if on(0):
                        if name in MAKES:
                            act.wait_ge(made, km + t + 1)
                        hold(act, turned, k + t - 1)
                        act.activation(staged[:, r, :], tile(A, t, 0, D, w), func).then_inc(staged_in, 1)
                    if on(1):
                        o = (r + 1) % 2
                        act.wait_ge(turned, k + t)
                        wait_past(act, projected, k + t - 2)
                        act.activation(hT[:, o, :], psum[o][:, 0:2 * P], ACT.Copy).then_inc(turned_in, 1)
                    if row_source is not None and on(3):
                        act.wait_ge(drawn, k + t - 2)
                        row_source(t - 3, (r + 1) % 2)
                turns(act, T, 2, 4, 3, step)

            def rows_from(A, w=D):
                def go(t, r):
                    act.dma_start(rows[bass.ds(t * P, P), :], tile(A, t, 0, D, w)).then_inc(rows_out[r], 16)
                return go

            def rows_h_from(t, r):
                act.dma_start(rows_h[bass.ds(t * P, P), :], wide[:, r, :]).then_inc(rows_out[r], 16)
                act.dma_start(rows_hr[bass.ds(t * P, P), :], wide[:, r, D:AW]).then_inc(rows_out[r], 16)

            def rows_staged(t, r):
                act.dma_start(rows[bass.ds(t * P, P), :], wide[:, r, 0:D]).then_inc(rows_out[r], 16)

            act.wait_ge(consts, 6)
            roots(1)
            project("l0", func=ACT.Relu, row_source=rows_h_from)

            def candidates(v, r, on):
                act.wait_ge(max_oh, v + 1)
                act.wait_ge(landed[r], (laps(v, r, RING) + 1) * 16 * G)
                wait_past(act, max_rows, v - 1)
                for h in range(HEADS):
                    for g in range(G):
                        ins = act.activation(cand[:, r % 2, h, g, :], oh[:, r, g, 0:P], ACT.Identity,
                                             bias=gat[:, r, g, D + h:D + h + 1])
                ins.then_inc(max_neg, 1)
            turns(act, UNITS, RING, RING, 0, candidates)

            def attend(v, r, on):
                if on(1):
                    o = (r + 3) % RING
                    act.wait_ge(oh_turned, v)
                    act.activation(ohT[0:P, o, :], psum[o % 2][0:P, 0:G * 128], ACT.Copy).then_inc(ohT_ready, 1)
                if on(2):
                    o = (r + 2) % RING
                    act.wait_ge(scores, v - 1)
                    act.activation(msg[:, o, :, D:AW], small[:, o * 8:o * 8 + 8].rearrange("p (g h) -> p g h", g=G),
                                   ACT.Exp).then_inc(probs, 1)
            turns(act, UNITS, RING, 2 * RING, 2, attend)
            act.wait_ge(hm_ready, 2)
            act.activation(DINV[:, :], CNT[:, :].rearrange("p (t c) -> p t c", c=2)[:, :, 0], ACT.Sqrt
                           ).then_inc(rooted, 1)
            roots(2)
            project("l1a", func=ACT.Relu, row_source=rows_from(Y))
            project("l1b", row_source=rows_from(Y))
            roots(3)
            project("l2in", func=ACT.Relu, row_source=rows_from(KEEP))

            def attrs_in_sbuf(v, r, on):
                act.wait_ge(oh_turned, UNITS + v + 1)
                act.activation(ohT[:, r, 0:128], psum[r % 2][:, 0:128], ACT.Copy).then_inc(ohT_ready, 1)
            turns(act, UNITS, RING, RING, 0, attrs_in_sbuf)
            act.wait_ge(acc_done, UNITS * (SCATTERS.index("l2") + 1))
            project("l2out", ACC, AW)
            act.wait_ge(bn_sqsum, 2)
            act.activation(wide[:, 1, 0:D], wide[:, 1, 0:D], ACT.Sqrt, bias=EPSC[0:P, :]).then_inc(rooted, 1)
            roots(4)
            project("l3in", func=ACT.Relu, row_source=rows_staged)
            for s in range(S3):
                q = TURNS_BEFORE_E + s * UNITS

                def edge_net(v, r, on):
                    if on(1):
                        o = (r + 3) % RING
                        act.wait_ge(oh_turned, q + v)
                        act.activation(ohT[:, o, :], psum[o % 2][:, 0:G * 128], ACT.Copy).then_inc(ohT_ready, 1)
                    if on(3):
                        o = (r + 1) % RING
                        act.wait_ge(msg_stats, (s * UNITS + v - 2) * 2)
                        act.activation(small[:, o * 2:o * 2 + 2], msg[:, o, :, D + 1], ACT.Sqrt,
                                       bias=EPSC[:, :]).then_inc(msg_sd, 1)
                    if on(2):
                        o = (r + 2) % RING
                        act.wait_ge(msgs, MSGS_BEFORE_E + s * UNITS + v - 1)
                        act.activation(msg[:, o, :, 0:D], msg[:, o, :, 0:D], ACT.Relu).then_inc(msg_relu, 1)
                turns(act, UNITS, RING, 2 * RING, 3, edge_net)
                project(f"agg{s}")
                act.wait_ge(drawn, T * PHASES.index(f"mix{s}"))
                project(f"mix{s}", ACC, AW)
                roots(5 + s)
                project(f"node{s}")
                if s < S3 - 1:
                    act.wait_ge(drawn, T * PHASES.index(f"next{s}"))
                    project(f"next{s}", ACC, AW, row_source=rows_staged)

        @block.vector
        def _(dve):
            ca, cb, cu = Chain(dve, chain_a), Chain(dve, chain_b), Chain(dve, chain_u)
            link = ca.link

            flat = msg[:, :, :, :].rearrange("p r g c -> p (r g c)")
            dve.memset(flat, 0.0).then_inc(blanked, 1)
            dve.memset(SH[:, :], 0.0).then_inc(blanked, 1)
            dve.wait_ge(blanked, 2)
            dve.memset(flat[:, 0:22 * REC].rearrange("p (j c) -> p j c", c=REC)[:, :, 0], -1.0).then_inc(blanked, 1)
            dve.memset(SH[:, :].rearrange("p (j c) -> p j c", c=2)[:, :, 0], -1.0).then_inc(blanked, 1)

            dve.wait_ge(inputs_in, 16 * 5)
            dve.wait_ge(consts, 6)
            head = header.rearrange("p (j c) -> p j c", c=HW)
            two_ = pair.rearrange("p (j c) -> p j c", c=2)
            link(dve.tensor_scalar(threshold[:, :], IOTA[:, 0:T], float(P), None, ALU.mult))
            link(dve.memset(ones_row, 1.0))
            link(dve.memset(header, 0.0))
            for name in ("dst", "src"):
                link(dve.tensor_copy(key_of[name], raw[name]))
            link(dve.tensor_copy(head[:, :, 1], key_of["src"]))
            link(dve.tensor_copy(head[:, :, 2], weight_in))
            link(dve.tensor_copy(head[:, :, 3], ones_row))
            link(dve.tensor_copy(head[:, :, 4:7], attr_in.rearrange("p (j c) -> p j c", c=3)))
            link(dve.tensor_copy(two_[:, :, 1], key_of["dst"]))

            for which, name in enumerate(("dst", "src")):
                key = key_of[name]
                local = head[:, :, 0] if name == "dst" else two_[:, :, 0]
                link(dve.memset(bucket, 0.0))
                link(dve.memset(rank, 0.0))
                ca.loop(T - 1, 1, lambda t: ca.link(dve.scalar_tensor_tensor(
                    bucket, key, threshold[0:P, bass.ds(t + 1, 1)], bucket, ALU.is_ge, ALU.add)))
                link(dve.scalar_tensor_tensor(local, bucket, -float(P), key, ALU.mult, ALU.add))

                def ranks(t):
                    ca.link(dve.tensor_scalar(mask, bucket, IOTA[0:P, bass.ds(t, 1)], None, ALU.is_equal))
                    ca.link(dve.tensor_tensor_scan(prefix, ones_row, mask, 0.0, ALU.mult, ALU.add))
                    dve.sem_inc(apart, 1)
                    ca.link(dve.tensor_copy(count[:, bass.ds(t, 1)], prefix[:, EC - 1:EC]))
                    ca.link(dve.tensor_tensor(mask, mask, prefix, ALU.mult))
                    ca.link(dve.tensor_tensor(rank, rank, mask, ALU.add))
                ca.loop(T, 5, ranks)
                dve.sem_inc(counted, 1)
                dve.wait_ge(prefixed, which + 1)
                total, below = psum[2][:, 0:T], psum[3][0:P, 0:T]
                link(dve.tensor_scalar(units_i[:, :], total, float(CAP - 1), None, ALU.add))
                link(dve.tensor_scalar(units_i[:, :], units_i[:, :], CAP.bit_length() - 1, None, ALU.logical_shift_right))
                link(dve.tensor_copy(units[:, :], units_i[:, :]))
                link(dve.tensor_tensor_scan(unit_end[:, :], ONES[:, 0:T], units[:, :], 0.0, ALU.mult, ALU.add))
                link(dve.tensor_tensor(unit_start[:, :], unit_end[:, :], units[:, :], ALU.subtract))
                link(dve.scalar_tensor_tensor(base[:, :], unit_start[0:P, :], float(CAP), below, ALU.mult, ALU.add))
                link(dve.tensor_scalar(base[:, :], base[:, :], -1.0, None, ALU.add))

                def places(t):
                    ca.link(dve.tensor_scalar(mask, bucket, IOTA[0:P, bass.ds(t, 1)], base[:, bass.ds(t, 1)],
                                              ALU.is_equal, ALU.mult))
                    ca.link(dve.tensor_tensor(rank, rank, mask, ALU.add))
                ca.loop(T, 2, places)
                link(dve.tensor_copy(place_i, rank))
                link(dve.tensor_scalar(place_j, place_i, 7, None, ALU.logical_shift_right))
                link(dve.tensor_scalar(place_i, place_i, 127, None, ALU.bitwise_and))
                dve.scalar_tensor_tensor(place_of[name], place_i, float(BLOCKS), place_j, ALU.mult,
                                         ALU.add).then_inc(placed, 1)
                link(dve.memset(tile_f[:, :], 0.0))
                ca.loop(T - 1, 1, lambda t: ca.link(dve.scalar_tensor_tensor(
                    tile_f[:, :], IOTA[0:1, 0:UNITS], unit_start[0:1, bass.ds(t + 1, 1)], tile_f[:, :],
                    ALU.is_ge, ALU.add)))
                link(dve.tensor_copy((DTILE if name == "dst" else STILE)[:, :], tile_f[:, :]))

            def mv(t, c):
                return MV[:, bass.ds(t * 2 + c, 1)]

            def stats(A, t, w=D):
                dve.sem_inc(apart, 1)
                ca.link(dve.bn_stats(ST[:, :], tile(A, t, 0, D, w)))
                dve.sem_inc(apart, 1)
                ca.link(dve.bn_aggr(AG[:, :], ST[:, :]))
                dve.sem_inc(apart, 1)
                ca.link(dve.tensor_copy(MV[:, bass.ds(t * 2, 2)], AG[:, :]))

            def rstd(k):
                dve.wait_ge(rooted, k)
                link(dve.reciprocal(RS[:, :], SD[:, :]))

            def normalize(A, t):
                return dve.tensor_scalar(tile(KEEP, t), tile(A, t), mv(t, 0), RS[:, bass.ds(t, 1)],
                                         ALU.subtract, ALU.mult)

            def project(name, make, per_make, draw, per_draw, before=None):
                k = PHASES.index(name) * T
                a0, b0 = ca.n, cb.n

                def step(t, r, on):
                    if make is not None and on(0):
                        ca.at(a0 + t * per_make)
                        make(t).then_inc(made, 1)
                    if on(2):
                        dve.wait_ge(projected, k + t - 1)
                        if before is not None:
                            b, per = before
                            wait_past(dve, rows_out[r], row_dmas(b, r) + 16 * per * laps(t - 2, r, 2))
                        wait_past(dve, drawn, k + t - 2)
                        dve.sem_inc(apart, 1)
                        cb.at(b0 + (t - 2) * per_draw)
                        draw(t - 2, r).then_inc(drawn, 1)
                turns(dve, T, 2, 4, 2, step)
                ca.at(a0 + T * per_make if make is not None else a0)
                cb.at(b0 + T * per_draw)

            def product(r, j):
                return (psum[2 + r][0:P, (j % 2) * D:(j % 2 + 1) * D] if j < 2 else psum[4 + r][0:P, 0:D])

            ca.loop(T, 3, lambda t: stats(X, t))
            dve.sem_inc(moments, 1)
            rstd(1)
            await_init(dve)

            def draw_h(t, r):
                hrow = wide[:, r, 0:D]
                cb.link(dve.tensor_scalar(wide[:, 2, 0:D], product(r, 0), 0.0, None, ALU.max))
                cb.link(dve.scalar_tensor_tensor(hrow, product(r, 0), 0.0, wide[:, 2, 0:D], ALU.min, ALU.add))
                cb.link(dve.tensor_tensor(wide[:, 2, 0:D], hrow, ALR[:, 0:D], ALU.mult))
                dve.sem_inc(apart, 1)
                cb.link(dve.tensor_reduce(HL[:, bass.ds(t * HEADS, HEADS)],
                                          wide[:, 2, 0:D].rearrange("p (h f) -> p h f", h=HEADS), AX_X, ALU.add))
                cb.link(dve.tensor_tensor(wide[:, 2, 0:D], hrow, ALR[:, D:2 * D], ALU.mult))
                return dve.tensor_reduce(wide[:, r, D:AW], wide[:, 2, 0:D].rearrange("p (h f) -> p h f", h=HEADS),
                                         AX_X, ALU.add)
            project("l0", lambda t: normalize(X, t), 0, draw_h, 5, before=(0, 2))

            def load_tile(table, v, most=T - 1):
                return dve.value_load(table[0:1, bass.ds(v, 1)], min_val=0, max_val=most)

            def one_hot(dest, head_, hw, v, r, scale=None):
                for g in range(G):
                    col = (v * G + g) * hw
                    ins = dve.tensor_scalar(dest[:, r, g, 0:P], IOTA[:, 0:P], head_[:, bass.ds(col, 1)],
                                            None if scale is None else scale(v, g), ALU.is_equal,
                                            *([] if scale is None else [ALU.mult]))
                return ins

            def accumulate(q, v, r, table, width, A=ACC, aw=AW):
                dve.wait_ge(part_ready, q + v + 1)
                t = load_tile(table, v)
                wait_past(dve, acc_done, q + v)
                dve.tensor_tensor(A[:, bass.ds(t * aw, width)], psum[6 + r % 2][0:P, 0:width],
                                  A[:, bass.ds(t * aw, width)], ALU.add).then_inc(acc_done, 1)

            def clear():
                dve.memset(ACC[:, :], 0.0).then_inc(accs_clear, 1)

            dve.wait_ge(lists_in["dst"], 16)
            link(dve.tensor_copy(DIDX[:, :], DH[:, :].rearrange("p (b c) -> p b c", c=HW)[:, :, 1]))
            dve.sem_inc(lists_ready["dst"], 1)
            link(dve.memset(CNT[:, :], 0.0))

            def degrees(v, r, on):
                if on(0):
                    one_hot(oh, DH, HW, v, r).then_inc(oh_ready, 1)
                if on(2):
                    accumulate(0, v - 2, (r + 2) % RING, DTILE, 2, CNT, 2)
            turns(dve, UNITS, RING, RING, 2, degrees)

            dve.wait_ge(lists_in["src"], 16)
            link(dve.tensor_copy(SIDX[:, :], SH[:, :].rearrange("p (b c) -> p b c", c=2)[:, :, 1]))
            dve.sem_inc(lists_ready["src"], 1)
            link(dve.memset(MX[:, :], -BIG))

            def maxima(v, r, on):
                if on(0):
                    for g in range(G):
                        ins = dve.tensor_scalar(oh[:, r, g, 0:P], IOTA[:, 0:P], SH[:, bass.ds((v * G + g) * 2, 1)],
                                                -BIG, ALU.not_equal, ALU.mult)
                    ins.then_inc(max_oh, 1)
                if on(3):
                    dve.wait_ge(max_rows, v - 2)
                    wait_past(dve, max_done, v - 3)
                    for k in range(2):
                        ins = dve.tensor_reduce(
                            wide[:, 3, D + 2 * k:D + 2 * k + 2],
                            psum[2 + 2 * ((r + 1) % 2) + k][0:P, :].rearrange("p (h e) -> p h e", h=2), AX_X, ALU.max)
                    cu.at(v - 3)
                    cu.link(ins)
                    dve.sem_inc(apart, 1)
                    t = load_tile(STILE, v - 3)
                    dve.tensor_tensor(MX[:, bass.ds(t * HEADS, HEADS)], wide[:, 3, D:AW],
                                      MX[:, bass.ds(t * HEADS, HEADS)], ALU.max).then_inc(max_done, 1)
            turns(dve, UNITS, RING, RING, 3, maxima)
            dve.wait_ge(max_done, UNITS)
            clear()
            hm = HM[:, :].rearrange("p (t c) -> p t c", c=2 * HEADS)
            hl = HL[:, :].rearrange("p (t h) -> p t h", h=HEADS)
            mx = MX[:, :].rearrange("p (t h) -> p t h", h=HEADS)
            link(dve.tensor_copy(hm[:, :, 0:HEADS], hl))
            link(dve.tensor_tensor(mx, mx, hl, ALU.add))
            link(dve.scalar_tensor_tensor(hm[:, :, HEADS:], mx, ALPHA, mx, ALU.mult, ALU.max))
            dve.sem_inc(hm_ready, 1)

            def attention(v, r, on):
                if on(4):
                    accumulate(UNITS, v - 4, r, STILE, AW)
                if on(0):
                    one_hot(oh, SH, 2, v, r).then_inc(oh_ready, 1)
                if on(3):
                    o = (r + 1) % RING
                    dve.wait_ge(probs, v - 2)
                    for g in range(G):
                        ins = dve.tensor_tensor(
                            msg[:, o, g, 0:D].rearrange("p (h f) -> p h f", h=HEADS),
                            gat[:, o, g, 0:D].rearrange("p (h f) -> p h f", h=HEADS),
                            msg[:, o, g, D:AW].unsqueeze(2).broadcast_to([128, HEADS, HD]), ALU.mult)
                    ins.then_inc(msgs, 1)
                if on(2):
                    o = (r + 2) % RING
                    dve.wait_ge(mid_ready, v - 1)
                    dve.wait_ge(landed[o], (UNITS // RING + laps(v - 2, o, RING) + 1) * 16 * G)
                    cu.at(UNITS + (v - 2) * 3)
                    hs = psum[2 + r % 2][:, 0:G * 8].rearrange("p (g c) -> p g c", g=G)
                    e = small[:, o * 8:o * 8 + 8].rearrange("p (g h) -> p g h", g=G)
                    cu.link(dve.tensor_tensor(e, hs[:, :, 0:HEADS], gat[:, o, :, D:AW], ALU.add))
                    cu.link(dve.scalar_tensor_tensor(e, e, ALPHA, e, ALU.mult, ALU.max))
                    cu.link(dve.tensor_tensor(e, e, hs[:, :, HEADS:], ALU.subtract))
                    dve.tensor_scalar(e, e, 0.0, None, ALU.min).then_inc(scores, 1)
            turns(dve, UNITS, RING, 2 * RING, 4, attention)
            dve.wait_ge(acc_done, 2 * UNITS)

            def acc(t, lo=0, hi=D):
                return tile(ACC, t, lo, hi, AW)

            accs = ACC[:, :].rearrange("p (t c) -> p t c", c=AW)
            rden = RDEN[:, :].rearrange("p (t h) -> p t h", h=HEADS)
            link(dve.tensor_scalar(rden, accs[:, :, D:AW], 1e-16, None, ALU.add))
            link(dve.reciprocal(rden, rden))

            def add_attention(t):
                ca.link(dve.tensor_tensor(acc(t).rearrange("p (h f) -> p h f", h=HEADS),
                                          acc(t).rearrange("p (h f) -> p h f", h=HEADS),
                                          RDEN[:, bass.ds(t * HEADS, HEADS)].unsqueeze(2).broadcast_to([P, HEADS, HD]),
                                          ALU.mult))
                ca.link(dve.tensor_tensor(tile(X, t), tile(X, t), acc(t), ALU.add))
                stats(X, t)
            ca.loop(T, 5, add_attention)

            cnts = CNT[:, :].rearrange("p (t c) -> p t c", c=2)
            link(dve.tensor_scalar(cnts[:, :, 0], cnts[:, :, 0], 1.0, None, ALU.add))
            link(dve.tensor_scalar(RDEN[:, 0:T], cnts[:, :, 0], 0.0, None, ALU.is_gt))
            link(dve.tensor_scalar(cnts[:, :, 0], cnts[:, :, 0], 1e-30, None, ALU.max))
            dve.sem_inc(hm_ready, 1)
            dve.wait_ge(rooted, 2)
            link(dve.reciprocal(DINV[:, :], DINV[:, :]))
            link(dve.tensor_tensor(DINV[:, :], DINV[:, :], RDEN[:, 0:T], ALU.mult))
            dve.sem_inc(moments, 1)
            rstd(3)

            def dinv(t):
                return DINV[:, bass.ds(t, 1)]

            def draw_scaled(t, r):
                return dve.tensor_scalar(tile(Y, t), product(r, 0), dinv(t), None, ALU.mult)
            project("l1a", lambda t: normalize(X, t), 0, draw_scaled, 0)
            clear()

            def weighted(name):
                q = SCATTERS.index(name) * UNITS

                def unit(v, r, on):
                    if on(2):
                        accumulate(q, v - 2, (r + 2) % RING, DTILE, D)
                    if on(0):
                        one_hot(oh, DH, HW, v, r, lambda v, g: DH[:, bass.ds((v * G + g) * HW + 2, 1)]
                                ).then_inc(oh_ready, 1)
                turns(dve, UNITS, RING, RING, 2, unit)
                dve.wait_ge(acc_done, q + UNITS)

            def convolved(t, b, relu):
                link_ = ca.link
                dve.sem_inc(apart, 1)
                link_(dve.tensor_tensor(acc(t), acc(t), tile(Y, t), ALU.add))
                link_(dve.scalar_tensor_tensor(acc(t), acc(t), dinv(t), bias(b), ALU.mult, ALU.add))
                if relu:
                    link_(dve.tensor_scalar(tile(KEEP, t), tile(KEEP, t), 0.0, 0.1, ALU.max, ALU.mult))
                else:
                    link_(dve.tensor_scalar(tile(KEEP, t), tile(KEEP, t), 0.1, None, ALU.mult))
                return dve.scalar_tensor_tensor(tile(KEEP, t), acc(t), 0.9, tile(KEEP, t), ALU.mult, ALU.add)

            weighted("l1a")
            project("l1b", lambda t: convolved(t, 2, True), 3, draw_scaled, 0)
            clear()
            weighted("l1b")

            def add_convolved(t):
                ca.link(convolved(t, 3, False))
                ca.link(dve.tensor_tensor(tile(X, t), tile(X, t), tile(KEEP, t), ALU.add))
                stats(X, t)
            ca.loop(T, 8, add_convolved)
            dve.sem_inc(moments, 1)
            rstd(4)

            def draw_root(t, r):
                cb.link(dve.tensor_tensor(tile(Y, t), product(r, 0), bias(4), ALU.add))
                cb.link(dve.tensor_tensor(tile(X, t), product(r, 1), tile(X, t), ALU.add))
                return dve.tensor_scalar(tile(KEEP, t), tile(KEEP, t), 0.0, None, ALU.max)
            project("l2in", lambda t: normalize(X, t), 0, draw_root, 2)
            clear()

            def edge_messages(v, r, on):
                if on(2):
                    o = (r + 2) % RING
                    dve.wait_ge(mid_ready, UNITS + v - 1)
                    dve.wait_ge(landed[o], (GATHERS.index("l2") * (UNITS // RING) + laps(v - 2, o, RING) + 1) * 16 * G)
                    for g in range(G):
                        ins = dve.tensor_tensor(msg[:, o, g, 0:D], psum[2 + 2 * (o % 2) + g][:, 0:D],
                                                gat[:, o, g, 0:D], ALU.mult)
                    ins.then_inc(msgs, 1)
                if on(3):
                    accumulate(SCATTERS.index("l2") * UNITS, v - 3, (r + 1) % RING, DTILE, D)
                if on(0):
                    one_hot(oh, DH, HW, v, r).then_inc(oh_ready, 1)
            turns(dve, UNITS, RING, 2 * RING, 3, edge_messages)
            dve.wait_ge(acc_done, (SCATTERS.index("l2") + 1) * UNITS)

            def draw_bn(t, r):
                cb.link(dve.tensor_tensor(tile(KEEP, t), product(r, 0), tile(Y, t), ALU.add))
                return dve.tensor_scalar(tile(KEEP, t), tile(KEEP, t), 0.0, None, ALU.max)
            project("l2out", None, 0, draw_bn, 1)
            mean, scale = wide[:, 0, 0:D], wide[:, 1, 0:D]
            dve.wait_ge(bn_sum, 1)
            link(dve.tensor_scalar(mean, psum[6][0:P, 0:D], 1.0 / N, None, ALU.mult))

            def squares(t):
                ca.link(dve.tensor_tensor(tile(KEEP, t), tile(KEEP, t), mean, ALU.subtract))
                dve.tensor_tensor(tile(Y, t), tile(KEEP, t), tile(KEEP, t), ALU.mult).then_inc(bn_sq, 1)
            ca.loop(T, 1, squares)
            dve.wait_ge(bn_sqsum, 1)
            link(dve.tensor_scalar(scale, psum[7][0:P, 0:D], 1.0 / N, None, ALU.mult))
            dve.sem_inc(bn_sqsum, 1)
            dve.wait_ge(rooted, 5)
            link(dve.reciprocal(scale, scale))
            link(dve.tensor_tensor(scale, scale, bias(5), ALU.mult))

            def add_bn(t):
                ca.link(dve.tensor_tensor(tile(KEEP, t), tile(KEEP, t), scale, ALU.mult))
                ca.link(dve.tensor_tensor(tile(KEEP, t), tile(KEEP, t), bias(6), ALU.add))
                ca.link(dve.tensor_tensor(tile(X, t), tile(X, t), tile(KEEP, t), ALU.add))
                stats(X, t)
            ca.loop(T, 6, add_bn)
            dve.sem_inc(finished, 1)
            dve.sem_inc(moments, 1)
            def draw_tables(t, r):
                cb.link(dve.tensor_copy(wide[:, r, 0:D], product(r, 0)))
                cb.link(dve.tensor_tensor(BT[0:P, bass.ds(t * D, D)], product(r, 1), bias(0), ALU.add))
                return dve.tensor_tensor(tile(Y, t), product(r, 2), bias(1), ALU.add)

            rstd(6)
            await_tables(dve, 0)
            project("l3in", lambda t: normalize(X, t), 0, draw_tables, 2, before=(ROWS.index("l3in"), 1))
            for s in range(S3):
                q = SCATTERS.index(f"e{s}") * UNITS
                m0 = MSGS_BEFORE_E + s * UNITS
                clear()

                def edge_net(v, r, on):
                    if on(0):
                        dve.tensor_copy(oh[:, r, :, P:128], DH[:, bass.ds(v * G * HW, G * HW)]
                                        .rearrange("p (g c) -> p g c", g=G)[:, :, 4:7])
                        one_hot(oh, DH, HW, v, r).then_inc(oh_ready, 1)
                    if on(6):
                        accumulate(q, v - 6, (r + 2) % RING, DTILE, D + 2)
                    if on(3):
                        o = (r + 1) % RING
                        dve.wait_ge(msg_relu, s * UNITS + v - 2)
                        for g in range(G):
                            ins = dve.bn_stats(small[:, 16 + g * 6:22 + g * 6], msg[:, o, g, 0:D])
                        cu.at(cu0 + (v - 3))
                        cu.link(ins)
                        dve.sem_inc(apart, 1)
                        for g in range(G):
                            dve.bn_aggr(msg[:, o, g, D:D + 2], small[:, 16 + g * 6:22 + g * 6]).then_inc(msg_stats, 1)
                    if on(4):
                        o = r
                        dve.wait_ge(msg_sd, s * UNITS + v - 3)
                        dve.reciprocal(small[:, 8 + o * 2:8 + o * 2 + 2], small[:, o * 2:o * 2 + 2]).then_inc(recip, 1)
                        dve.wait_ge(recip, s * UNITS + v - 3)
                        for g in range(G):
                            col = ((v - 4) * G + g) * HW
                            ins = dve.tensor_scalar(ohw[:, o % 2, g, :], IOTA[:, 0:P], DH[:, bass.ds(col, 1)],
                                                    small[:, 8 + o * 2 + g:9 + o * 2 + g], ALU.is_equal, ALU.mult)
                        ins.then_inc(ohw_ready, 1)
                    if on(2):
                        o = (r + 2) % RING
                        dve.wait_ge(mid_ready, 2 * UNITS + s * UNITS + v - 1)
                        dve.wait_ge(landed[o], (GATHERS.index(f"e{s}") * (UNITS // RING) + laps(v - 2, o, RING) + 1) * 16 * G)
                        dve.tensor_tensor(msg[:, o, :, 0:D], psum[2 + o % 2][:, :].rearrange("p (g f) -> p g f", g=G),
                                          gat[:, o, :, 0:D], ALU.add).then_inc(msgs, 1)
                cu0 = UNITS * 4 + s * UNITS
                turns(dve, UNITS, RING, 2 * RING, 6, edge_net)
                dve.wait_ge(acc_done, q + UNITS)
                await_nets(dve, s)

                def summed(t):
                    link_ = ca.link
                    dve.sem_inc(apart, 1)
                    link_(dve.tensor_scalar(tile(KEEP, t), acc(t), acc(t, D, D + 1), None, ALU.subtract))
                    link_(dve.tensor_tensor(tile(KEEP, t), tile(KEEP, t), bias(2), ALU.mult))
                    return dve.scalar_tensor_tensor(tile(KEEP, t), bias(3), CNT[:, bass.ds(t * 2 + 1, 1)],
                                                    tile(KEEP, t), ALU.mult, ALU.add)

                def draw_agg(t, r):
                    return dve.scalar_tensor_tensor(acc(t), bias(4), CNT[:, bass.ds(t * 2 + 1, 1)], product(r, 0),
                                                    ALU.mult, ALU.add)
                project(f"agg{s}", summed, 2, draw_agg, 0)

                def draw_mix(t, r):
                    cb.link(dve.tensor_tensor(tile(KEEP, t), product(r, 0), tile(Y, t), ALU.add))
                    cb.link(dve.tensor_scalar(tile(KEEP, t), tile(KEEP, t), 0.0, None, ALU.max))
                    dve.sem_inc(apart, 1)
                    cb.link(dve.bn_stats(ST[:, :], tile(KEEP, t)))
                    dve.sem_inc(apart, 1)
                    cb.link(dve.bn_aggr(AG[:, :], ST[:, :]))
                    dve.sem_inc(apart, 1)
                    return dve.tensor_copy(MV[:, bass.ds(t * 2, 2)], AG[:, :])
                project(f"mix{s}", None, 0, draw_mix, 4)
                dve.wait_ge(drawn, T * (PHASES.index(f"mix{s}") + 1))
                dve.sem_inc(moments, 1)
                rstd(7 + s)

                def normed(t):
                    dve.sem_inc(apart, 1)
                    ca.link(normalize(KEEP, t))
                    ca.link(dve.tensor_tensor(tile(KEEP, t), tile(KEEP, t), bias(5), ALU.mult))
                    return dve.tensor_tensor(tile(KEEP, t), tile(KEEP, t), bias(6), ALU.add)

                def draw_node(t, r):
                    return dve.tensor_tensor(acc(t), product(r, 0), bias(7), ALU.add)

                def draw_last(t, r):
                    cb.link(dve.tensor_tensor(acc(t), product(r, 0), bias(7), ALU.add))
                    return dve.tensor_tensor(tile(X, t), acc(t), tile(X, t), ALU.add)
                if s < S3 - 1:
                    project(f"node{s}", normed, 2, draw_node, 0)
                    await_tables(dve, s + 1)
                    project(f"next{s}", None, 0, draw_tables, 2, before=(ROWS.index(f"next{s}"), 1))
                else:
                    project(f"node{s}", normed, 2, draw_last, 1)
            dve.wait_ge(drawn, T * len(PHASES))
            dve.sem_inc(finished, LAST - 1)

        @block.tensor
        def _(pe):
            pe.wait_ge(consts, 6)
            for which in range(2):
                pe.wait_ge(placed, which) if which else None
                pe.wait_ge(counted, which + 1)
                pe.matmul(psum[2][:, 0:T], ONES[0:P, :], count[:, :], start=True, stop=True)
                pe.matmul(psum[3][0:P, 0:T], LTRI[0:P, 0:P], count[:, :], start=True, stop=True).then_inc(prefixed, 1)

            def project(name, weights, extra=None):
                k = PHASES.index(name) * T

                def step(t, r, on):
                    if on(0):
                        pe.wait_ge(staged_in, k + t + 1)
                        wait_past(pe, turned_in, k + t - 1)
                        for c in range(2):
                            ins = pe.transpose(psum[r][:, c * P:(c + 1) * P], staged[:, r, c * 128:(c + 1) * 128],
                                               IDENT[0:P, 0:P])
                        ins.then_inc(turned, 1)
                    if on(1):
                        o = (r + 1) % 2
                        pe.wait_ge(turned_in, k + t)
                        wait_past(pe, drawn, k + t - 2)
                        for j, W in enumerate(weights):
                            place = psum[2 + o][0:P, j * D:(j + 1) * D] if j < 2 else psum[4 + o][0:P, 0:D]
                            for c in range(2):
                                ins = pe.matmul(place, hT[:, o, c * P:(c + 1) * P], Wc(W, c), start=(c == 0), stop=(c == 1))
                        ins.then_inc(projected, 1)
                    if extra is not None and on(3):
                        pe.wait_ge(drawn, k + t - 2)
                        extra(t - 3)
                turns(pe, T, 2, 4, 3 if extra else 1, step)

            await_init(pe)
            project("l0", [W0])

            def scatter(q, v, r, lhs, rhs, width, ready, value):
                pe.wait_ge(ready, value)
                wait_past(pe, acc_done, q + v - 1)
                for g in range(G):
                    ins = pe.matmul(psum[6 + r % 2][0:P, 0:width], lhs(g), rhs(g), start=(g == 0), stop=(g == G - 1))
                return ins.then_inc(part_ready, 1)

            def await_gather(name, v, r):
                pe.wait_ge(landed[r], (GATHERS.index(name) * (UNITS // RING) + laps(v, r, RING) + 1) * 16 * G)

            def degrees(v, r, on):
                scatter(0, v, r, lambda g: oh[:, r, g, 0:P],
                        lambda g: DH[:, bass.ds((v * G + g) * HW + 2, 2)], 2, oh_ready, v + 1)
            pe.wait_ge(lists_in["dst"], 16)
            turns(pe, UNITS, RING, RING, 0, degrees)

            def maxima(v, r, on):
                pe.wait_ge(max_neg, v + 1)
                wait_past(pe, max_done, v - 1)
                for h in range(HEADS):
                    for g in range(G):
                        ins = pe.transpose(
                            psum[2 + 2 * (r % 2) + h // 2][0:P, (h % 2) * 256 + g * 128:(h % 2) * 256 + g * 128 + 128],
                            cand[:, r % 2, h, g, :], IDENT[:, :])
                ins.then_inc(max_rows, 1)
            turns(pe, UNITS, RING, RING, 0, maxima)

            def turn_one_hot(qt, q, v, r, height):
                pe.wait_ge(oh_ready, q + v + 1)
                wait_past(pe, ohT_ready, qt + v - 1)
                for g in range(G):
                    ins = pe.transpose(psum[r % 2][0:height, g * 128:(g + 1) * 128], oh[:, r, g, 0:height], IDENT[:, :])
                ins.then_inc(oh_turned, 1)

            def attention(v, r, on):
                if on(2):
                    o = (r + 2) % RING
                    pe.wait_ge(ohT_ready, v - 1)
                    t = pe.value_load(STILE[0:1, bass.ds(v - 2, 1)], min_val=0, max_val=T - 1)
                    wait_past(pe, scores, v - 3)
                    for g in range(G):
                        ins = pe.matmul(psum[2 + o % 2][:, g * 8:g * 8 + 8], ohT[0:P, o, g * 128:(g + 1) * 128],
                                        HM[:, bass.ds(t * 2 * HEADS, 2 * HEADS)], start=True, stop=True)
                    ins.then_inc(mid_ready, 1)
                if on(1):
                    turn_one_hot(0, UNITS, v - 1, (r + 3) % RING, P)
                if on(3):
                    o = (r + 1) % RING
                    scatter(UNITS, v - 3, o, lambda g: oh[:, o, g, 0:P], lambda g: msg[:, o, g, :], AW, msgs, v - 2)
            pe.wait_ge(hm_ready, 1)
            turns(pe, UNITS, RING, 2 * RING, 3, attention)
            project("l1a", [WA])

            def weighted(name):
                q = SCATTERS.index(name) * UNITS

                def unit(v, r, on):
                    await_gather(name, v, r)
                    scatter(q, v, r, lambda g: oh[:, r, g, 0:P], lambda g: gat[:, r, g, 0:D], D, oh_ready, q + v + 1)
                turns(pe, UNITS, RING, RING, 0, unit)
            weighted("l1a")
            project("l1b", [WB])
            weighted("l1b")
            project("l2in", [WC, WD])

            def edge_messages(v, r, on):
                if on(0):
                    pe.wait_ge(attrs_in[r], (laps(v, r, RING) + 1) * 16)
                    wait_past(pe, ohT_ready, UNITS + v - 1)
                    pe.transpose(psum[r % 2][:, 0:128], attr_slot(r), IDENT[:, :]).then_inc(oh_turned, 1)
                if on(1):
                    o = (r + 3) % RING
                    pe.wait_ge(ohT_ready, UNITS + v)
                    wait_past(pe, msgs, UNITS + v - 2)
                    for g in range(G):
                        ins = pe.matmul(psum[2 + 2 * (o % 2) + g][:, 0:D], ohT[g * EA:(g + 1) * EA, o, 0:128],
                                        WE[g * EA:(g + 1) * EA, :], start=True, stop=True)
                    ins.then_inc(mid_ready, 1)
                if on(2):
                    o = (r + 2) % RING
                    q = SCATTERS.index("l2") * UNITS
                    pe.wait_ge(oh_ready, q + v - 1)
                    scatter(q, v - 2, o, lambda g: oh[:, o, g, 0:P], lambda g: msg[:, o, g, 0:D], D, msgs, UNITS + v - 1)
            turns(pe, UNITS, RING, 2 * RING, 2, edge_messages)

            def bn_sums(t):
                ins = pe.matmul(psum[6][0:P, 0:D], ONES[0:P, 0:P], tile(KEEP, t), start=isinstance(t, int) and t == 0,
                                stop=isinstance(t, int) and t == T - 1)
                if isinstance(t, int) and t == T - 1:
                    ins.then_inc(bn_sum, 1)
            project("l2out", [WF], bn_sums)

            def bn_squares(t, r, on):
                pe.wait_ge(bn_sq, t + 1)
                ins = pe.matmul(psum[7][0:P, 0:D], ONES[0:P, 0:P], tile(Y, t), start=isinstance(t, int) and t == 0,
                                stop=isinstance(t, int) and t == T - 1)
                if isinstance(t, int) and t == T - 1:
                    ins.then_inc(bn_sqsum, 1)
            turns(pe, T, 2, 2, 0, bn_squares)
            await_tables(pe, 0)
            project("l3in", [W0, WA, WB])
            for s in range(S3):
                q = SCATTERS.index(f"e{s}") * UNITS
                qt = TURNS_BEFORE_E + s * UNITS
                pe.wait_ge(edge_rows_in, 16 * (s + 1))

                def edge_net(v, r, on):
                    if on(2):
                        o = (r + 2) % RING
                        pe.wait_ge(ohT_ready, qt + v - 1)
                        t = pe.value_load(DTILE[0:1, bass.ds(v - 2, 1)], min_val=0, max_val=T - 1)
                        wait_past(pe, msgs, MSGS_BEFORE_E + s * UNITS + v - 3)
                        for g in range(G):
                            ins = pe.matmul(psum[2 + o % 2][:, g * D:(g + 1) * D], ohT[:, o, g * 128:(g + 1) * 128],
                                            BT[:, bass.ds(t * D, D)], start=True, stop=True)
                        ins.then_inc(mid_ready, 1)
                    if on(1):
                        turn_one_hot(qt, q, v - 1, (r + 3) % RING, 128)
                    if on(5):
                        o = (r + 3) % RING
                        scatter(q, v - 5, o, lambda g: ohw[:, o % 2, g, :], lambda g: msg[:, o, g, 0:D + 2], D + 2,
                                ohw_ready, s * UNITS + v - 4)
                turns(pe, UNITS, RING, 2 * RING, 5, edge_net)
                await_nets(pe, s)
                project(f"agg{s}", [WC])
                project(f"mix{s}", [WD])
                project(f"node{s}", [WF])
                if s < S3 - 1:
                    await_tables(pe, s + 1)
                    project(f"next{s}", [W0, WA, WB])


_INS = ["x", "src", "dst", "edge_attr_3", "edge_attr_64", "edge_weight", "L0_gnn_W", "L0_gnn_a_l", "L0_gnn_a_r",
        "L1_gnn_W1", "L1_gnn_b1", "L1_gnn_W2", "L1_gnn_b2", "L2_gnn_W_edge", "L2_gnn_W_rel", "L2_gnn_b_rel",
        "L2_gnn_W_root", "L2_gnn_gamma", "L2_gnn_beta", "L2_gnn_W_res", "L3_gnn_W1e", "L3_gnn_b1e", "L3_gnn_ge",
        "L3_gnn_oe", "L3_gnn_W2e", "L3_gnn_b2e", "L3_gnn_W1n", "L3_gnn_b1n", "L3_gnn_gn", "L3_gnn_on",
        "L3_gnn_W2n", "L3_gnn_b2n"]


def kernel(**inputs):
    import numpy as _np
    import concourse.bacc as _bacc
    from concourse import mybir as _mybir
    from concourse.bass_utils import run_bass_kernel_spmd as _run

    nc = _bacc.Bacc("TRN2", target_bir_lowering=False, num_devices=1)
    arrays, args = {}, []
    for name in _INS:
        a = _np.ascontiguousarray(inputs[name])
        arrays[f"in_{name}"] = a
        args.append(nc.dram_tensor(f"in_{name}", a.shape, _mybir.dt.from_np(a.dtype), kind="ExternalInput").ap())
    args.append(nc.dram_tensor("out_0", (N, D), _mybir.dt.float32, kind="ExternalOutput").ap())
    build(nc, *args)
    r = _run(nc, [arrays], core_ids=[0])
    return r.results[0]["out_0"]
```

```python
from contextlib import ExitStack

import concourse.bass as bass
from concourse import mybir

F32 = mybir.dt.float32
I32 = mybir.dt.int32
BF16 = mybir.dt.bfloat16
ALU = mybir.AluOpType
ACT = mybir.ActivationFunctionType
AX_X = mybir.AxisListType.X

N, D, E = 3125, 256, 50000
P = 125
T = N // P
HEADS = 4
HD = D // HEADS
G = 2
RING = 4
OHS = 2 * RING
CAP = G * 128
MOST = (E + T * (CAP - 1)) // CAP
UNITS = -(-MOST // RING) * RING
BLOCKS = UNITS * G
EC = E // P
HW = 8
EA = 64
AK = 96
REC = HW + EA
CH = 8
AW = D + 4
BIG = 1e30
ALPHA = 0.2
EPS = 1e-5
S3 = 3


def turns(eng, total, ring, head, depth, step):
    assert head % ring == 0 and head >= depth
    end = total - total % ring
    for v in range(head):
        step(v, v % ring, lambda lag: v >= lag)
    with eng.Fori(head // ring, end // ring) as lap:
        for r in range(ring):
            step(lap * ring + r, r, lambda lag: True)
    for v in range(end, total + depth):
        step(v, v % ring, lambda lag: 0 <= v - lag < total)


def wait_past(eng, sem, value):
    if isinstance(value, int) and value <= 0:
        return
    eng.wait_ge(sem, value)


class Chain:

    def __init__(self, eng, sem):
        self.eng, self.sem, self.n = eng, sem, 0

    def link(self, ins):
        ins.then_inc(self.sem, 1)
        self.n = self.n + 1
        self.eng.wait_ge(self.sem, self.n)

    def mark(self, ins):
        ins.then_inc(self.sem, 1)
        self.n = self.n + 1
        return self.n

    def await_(self, n):
        self.eng.wait_ge(self.sem, n)

    def at(self, n):
        self.n = n

    def loop(self, end, per, body):
        base, times = self.n, 5 if end % 5 == 0 else 4
        assert end % times == 0
        with self.eng.Fori(0, end // times) as i:
            for k in range(times):
                self.n = base + (i * times + k) * per
                body(i * times + k)
        self.n = base + per * end


def build(nc, x, src, dst, edge_attr_3, edge_attr_64, edge_weight, L0_gnn_W, L0_gnn_a_l, L0_gnn_a_r,
          L1_gnn_W1, L1_gnn_b1, L1_gnn_W2, L1_gnn_b2, L2_gnn_W_edge, L2_gnn_W_rel, L2_gnn_b_rel,
          L2_gnn_W_root, L2_gnn_gamma, L2_gnn_beta, L2_gnn_W_res, L3_gnn_W1e, L3_gnn_b1e, L3_gnn_ge,
          L3_gnn_oe, L3_gnn_W2e, L3_gnn_b2e, L3_gnn_W1n, L3_gnn_b1n, L3_gnn_gn, L3_gnn_on, L3_gnn_W2n,
          L3_gnn_b2n, out):
    by_dst = nc.dram_tensor("by_dst", (128 * BLOCKS, REC), F32, kind="Internal").ap()
    by_src = nc.dram_tensor("by_src", (128 * BLOCKS, 2), F32, kind="Internal").ap()
    rows_h = nc.dram_tensor("rows_h", (N, AW), F32, kind="Internal").ap()
    rows_hr = nc.dram_tensor("rows_hr", (N, HEADS), F32, kind="Internal").ap()
    rows = nc.dram_tensor("rows", (N, D), F32, kind="Internal").ap()

    with ExitStack() as ctx:
        def sb(name, shape, dt=F32):
            return ctx.enter_context(nc.sbuf_tensor(name, shape, dt))

        def sem(name):
            return ctx.enter_context(nc.semaphore(name))

        X = sb("X", [P, T * D])
        KEEP = sb("KEEP", [P, T * D])
        Y = sb("Y", [P, T * D])
        ACC = sb("ACC", [P, T * AW])
        BT = sb("BT", [128, T * D])
        HL = sb("HL", [P, T * HEADS])
        MX = sb("MX", [P, T * HEADS])
        HM = sb("HM", [P, T * 2 * HEADS])
        CNT = sb("CNT", [P, T * 2])
        DINV = sb("DINV", [P, T])
        RDEN = sb("RDEN", [P, T * HEADS])
        MV = sb("MV", [P, T * 2])
        SD = sb("SD", [P, T])
        RS = sb("RS", [P, T])
        ST = sb("ST", [P, 6])
        AG = sb("AG", [P, 2])
        EPSC = sb("EPSC", [128, 1])

        DH = sb("DH", [128, BLOCKS * HW])
        SH = sb("SH", [128, BLOCKS * 2])
        DIDX = sb("DIDX", [128, BLOCKS], I32)
        SIDX = sb("SIDX", [128, BLOCKS], I32)
        DTILE = sb("DTILE", [1, UNITS], I32)
        STILE = sb("STILE", [1, UNITS], I32)

        IOTA = sb("IOTA", [128, UNITS])
        IOTAB = sb("IOTAB", [128, 128], BF16)
        IDENT = sb("IDENT", [128, 128])
        IDENTB = sb("IDENTB", [128, 128], BF16)
        ONES = sb("ONES", [128, 128])
        LTRI = sb("LTRI", [128, 128])

        W0 = sb("W0", [128, 2 * D])
        WA = sb("WA", [128, 2 * D])
        WB = sb("WB", [128, 2 * D])
        WC = sb("WC", [128, 2 * D])
        WD = sb("WD", [128, 2 * D])
        WF = sb("WF", [128, 2 * D])
        WE = sb("WE", [128, D])
        BIAS = sb("BIAS", [P, 8 * D])
        ALR = BIAS[:, 0:2 * D]

        gidx = sb("gidx", [128, RING * G], I32)
        gat = sb("gat", [128, RING, G, AW])
        oh = sb("oh", [128, RING, G, 128])
        ohw = sb("ohw", [128, 2, G, P])
        ohT = sb("ohT", [128, RING, G * 128])
        msg = sb("msg", [128, RING, G, AW])
        small = sb("small", [128, 64])
        wide = sb("wide", [P, 4, AW])
        staged = sb("staged", [P, 2, D])
        cand = msg[:, :, :, :].rearrange("p r g c -> p (r g c)")[:, 0:2 * HEADS * G * P].rearrange(
            "p (s h g n) -> p s h g n", s=2, h=HEADS, g=G)
        ohb = oh[:, :, :, :].rearrange("p r g n -> p (r g n)").bitcast(BF16)[:, 0:OHS * G * P].rearrange(
            "p (r g n) -> p r g n", r=OHS, g=G)
        flatT = ohT[:, :, :].rearrange("p r n -> p (r n)").bitcast(BF16)
        ohbT = flatT[:, 0:RING * G * 128].rearrange("p (r n) -> p r n", r=RING)
        atT = flatT[0:AK, RING * G * 128:2 * RING * G * 128].rearrange("p (r n) -> p r n", r=RING)
        free_b = SH[:, :].bitcast(BF16)
        atb = free_b[:, 0:RING * G * AK].rearrange("p (r g n) -> p r g n", r=RING, g=G)
        edge_w = free_b[0:AK, RING * G * AK:RING * G * AK + D]
        BTB, KEEPB = BT[:, :].bitcast(BF16), KEEP[:, :].bitcast(BF16)
        edge_in = WE[0:AK, :]
        HMB = staged[:, :, :].rearrange("p s n -> p (s n)").bitcast(BF16)[:, 0:T * 6 * HEADS]
        hT = ohT[:, 0:2, 0:2 * P]

        psum = [ctx.enter_context(nc.psum_tensor(f"ps{k}", [128, 512], F32)) for k in range(8)]
        psum_b = [psum[k][:, :].bitcast(BF16) for k in range(2)]

        key_of = {"dst": Y[:, 0:EC], "src": Y[:, EC:2 * EC]}
        bucket = Y[:, 2 * EC:3 * EC]
        rank = Y[:, 3 * EC:4 * EC]
        mask = Y[:, 4 * EC:5 * EC]
        prefix = Y[:, 5 * EC:6 * EC]
        ones_row = Y[:, 6 * EC:7 * EC]
        raw = {"dst": Y[:, 7 * EC:8 * EC].bitcast(I32), "src": Y[:, 8 * EC:9 * EC].bitcast(I32)}
        weight_in = Y[:, 9 * EC:10 * EC]
        attr_in = Y[:, 10 * EC:13 * EC]
        place_i = Y[:, 13 * EC:14 * EC].bitcast(I32)
        place_j = Y[:, 14 * EC:15 * EC].bitcast(I32)
        header = BT[0:P, 0:HW * EC]
        pair = BT[0:P, HW * EC:(HW + 2) * EC]
        place_of = {"dst": BT[0:P, 10 * EC:11 * EC].bitcast(I32), "src": BT[0:P, 11 * EC:12 * EC].bitcast(I32)}
        record = BT[0:P, 12 * EC:12 * EC + 2 * CH * REC].rearrange("p (s j c) -> p s j c", s=2, c=REC)
        AT = 12 * EC + 2 * CH * REC
        place_now = BT[0:P, AT:AT + 2 * CH].bitcast(I32)
        AT += 2 * CH
        pair_now = BT[0:P, AT:AT + 4 * CH].rearrange("p (s j c) -> p s j c", s=2, c=2)
        AT += 4 * CH
        threshold = BT[:, AT:AT + T]
        count = sb("count", [P, T])
        units_i = BT[:, AT + T:AT + 2 * T].bitcast(I32)
        units = BT[:, AT + 2 * T:AT + 3 * T]
        unit_end = BT[:, AT + 3 * T:AT + 4 * T]
        unit_start = BT[:, AT + 4 * T:AT + 5 * T]
        base = sb("base", [P, T])
        tile_f = Y[0:1, 15 * EC:15 * EC + UNITS]

        inputs_in = sem("inputs_in")
        consts = sem("consts")
        threshold_ready = sem("threshold_ready")
        counted = sem("counted")
        prefixed = sem("prefixed")
        blanked = sem("blanked")
        blank_out = sem("blank_out")
        placed = sem("placed")
        attr_landed = [sem(f"attr_landed{r}") for r in range(2)]
        scattered = [sem(f"scattered{r}") for r in range(2)]
        pairs_out = [sem(f"pairs_out{r}") for r in range(2)]
        turn_ready = sem("turn_ready")
        apart = sem("apart")
        lists_in = {"dst": sem("dst_list_in"), "src": sem("src_list_in")}
        lists_ready = {"dst": sem("dst_list_ready"), "src": sem("src_list_ready")}
        weights_in = sem("weights_in")
        chain_a = sem("chain_a")
        chain_b = sem("chain_b")
        chain_u = sem("chain_u")
        accs_clear = sem("accs_clear")
        moments = sem("moments")
        rooted = sem("rooted")
        made = sem("made")
        staged_in = sem("staged_in")
        turned = sem("turned")
        turned_in = sem("turned_in")
        projected = sem("projected")
        drawn = sem("drawn")
        rows_out = [sem(f"rows_out{r}") for r in range(2)]
        gidx_ready = sem("gidx_ready")
        landed = [sem(f"landed{r}") for r in range(RING)]
        oh_ready = sem("oh_ready")
        part_ready = sem("part_ready")
        acc_done = sem("acc_done")
        max_oh = sem("max_oh")
        max_neg = sem("max_neg")
        max_rows = sem("max_rows")
        max_done = sem("max_done")
        oh_turned = sem("oh_turned")
        ohT_ready = sem("ohT_ready")
        mid_ready = sem("mid_ready")
        scores = sem("scores")
        probs = sem("probs")
        msgs = sem("msgs")
        msg_relu = sem("msg_relu")
        msg_stats = sem("msg_stats")
        msg_sd = sem("msg_sd")
        attrs_in = [sem(f"attrs_in{r}") for r in range(RING)]
        bn_sum = sem("bn_sum")
        bn_sq = sem("bn_sq")
        bn_sqsum = sem("bn_sqsum")
        hm_ready = sem("hm_ready")
        recip = sem("recip")
        ohw_ready = sem("ohw_ready")
        finished = sem("finished")
        out_done = sem("out_done")

        PHASES = ["l0", "l1a", "l1b", "l2in", "l2out", "l3in"]
        for s in range(S3):
            PHASES += [f"agg{s}", f"mix{s}", f"node{s}"] + ([f"next{s}"] if s < S3 - 1 else [])
        MAKES = [p for p in PHASES if p not in ("l2out",) and not p.startswith(("mix", "next"))]
        ROWS = ["l0", "l0", "l1a", "l1b", "l2in", "l3in", "next0", "next1"]
        SCATTERS = ["deg", "l0", "l1a", "l1b", "l2", "e0", "e1", "e2"]
        GATHERS = ["max", "l0", "l1a", "l1b", "l2", "e0", "e1", "e2"]

        def laps(v, r, ring):
            return v // ring if isinstance(v, int) else (v - r) // ring

        def landings(name, v, r):
            return 16 * G * (UNITS // RING * GATHERS.index(name) + 1) + (v - r) * (16 * G // RING)

        class Tiles:

            def __init__(self, engine, table, lag, ring):
                self.engine, self.table, self.lag, self.ring = engine, table, lag, ring

            def load(self, first, n):
                return nc.values_load_multi_w_load_instructions(
                    self.table[0:1, bass.ds(first, n)], engines=[self.engine], min_val=0, max_val=T - 1,
                    skip_runtime_bounds_check_because="the table counts passed thresholds, of which there are T - 1")[1]

            def at(self, v, r):
                if isinstance(v, int):
                    return self.load(v - self.lag, 1)[0]
                if r == 0:
                    self.lap = self.load(v - self.lag, self.ring)
                return self.lap[r]

        def row_dmas(names, r):
            return 16 * names * ((T + 1 - r) // 2)

        def await_rows(eng, phase):
            k = len(ROWS) - 1 - ROWS[::-1].index(phase) + 1
            for r in range(2):
                eng.wait_ge(rows_out[r], row_dmas(k, r))

        def tile(A, t, lo=0, hi=None, w=D):
            return A[:, bass.ds(t * w + lo, (w if hi is None else hi) - lo)]

        def Wc(W, c):
            return W[:, c * D:(c + 1) * D]

        def bias(k):
            return BIAS[:, k * D:(k + 1) * D]

        def hold(eng, s, value):
            wait_past(eng, s, value)
            eng.sem_inc(apart, 1)

        def attr_slot(r):
            return ohT[:, r, 128:128 + G * EA]

        USERS = {"max": (max_neg, 0), "l0": (msgs, 0), "l1a": (part_ready, 2 * UNITS),
                 "l1b": (part_ready, 3 * UNITS), "l2": (msgs, UNITS)}
        USERS.update({f"e{s}": (msgs, (2 + s) * UNITS) for s in range(S3)})
        TURNS_BEFORE_E = MSGS_BEFORE_E = 2 * UNITS
        LAST = 2
        ROWS_TOTAL = [row_dmas(len(ROWS), r) for r in range(2)]

        block = ctx.enter_context(nc.Block())

        def kcn(W):
            return W.rearrange("(c k) n -> k c n", k=128)

        def two(W):
            return W[:, :].rearrange("p (c n) -> p c n", c=2)

        def row(v):
            return v.partition_broadcast(P)

        INIT = [(two(W0), kcn(L0_gnn_W)), (two(WA), kcn(L1_gnn_W1)), (two(WB), kcn(L1_gnn_W2)),
                (two(WC), kcn(L2_gnn_W_root)), (two(WD), kcn(L2_gnn_W_res)), (two(WF), kcn(L2_gnn_W_rel)),
                (WE[0:EA, :], L2_gnn_W_edge), (WE[EA:2 * EA, :], L2_gnn_W_edge),
                (ALR[:, 0:D], row(L0_gnn_a_l.rearrange("a h f -> (a h f)"))),
                (ALR[:, D:2 * D], row(L0_gnn_a_r.rearrange("a h f -> (a h f)"))),
                (bias(2), row(L1_gnn_b1)), (bias(3), row(L1_gnn_b2)), (bias(4), row(L2_gnn_b_rel)),
                (bias(5), row(L2_gnn_gamma)), (bias(6), row(L2_gnn_beta))]

        def table_loads(s):
            return [(two(W0), kcn(L3_gnn_W1e[s, 3:3 + D, :])), (two(WA), kcn(L3_gnn_W1e[s, 3 + D:3 + 2 * D, :])),
                    (two(WB), kcn(L3_gnn_W1n[s, 0:D, :])), (bias(0), row(L3_gnn_b1e[s, :])),
                    (bias(1), row(L3_gnn_b1n[s, :]))]

        def net_loads(s):
            return [(two(WC), kcn(L3_gnn_W2e[s])), (two(WD), kcn(L3_gnn_W1n[s, D:2 * D, :])),
                    (two(WF), kcn(L3_gnn_W2n[s])), (bias(2), row(L3_gnn_ge[s, :])),
                    (bias(3), row(L3_gnn_oe[s, :])), (bias(4), row(L3_gnn_b2e[s, :])),
                    (bias(5), row(L3_gnn_gn[s, :])), (bias(6), row(L3_gnn_on[s, :])),
                    (bias(7), row(L3_gnn_b2n[s, :]))]

        def await_init(eng):
            eng.wait_ge(weights_in, 16 * len(INIT))

        def await_tables(eng, s):
            eng.wait_ge(tables_in, 16 * len(table_loads(s)) * (s + 1))

        def await_nets(eng, s):
            eng.wait_ge(nets_in, 16 * len(net_loads(s)) * (s + 1))

        edge_clear = sem("edge_clear")
        edge_split = sem("edge_split")
        edge_rows_in = sem("edge_rows_in")
        tables_in = sem("tables_in")
        nets_in = sem("nets_in")

        @block.sync
        def _(sp):
            def load(out_, in_, s):
                sp.dma_start(out_, in_).then_inc(s, 16)

            load(raw["dst"], dst.rearrange("(p j) -> p j", p=P), inputs_in)
            load(raw["src"], src.rearrange("(p j) -> p j", p=P), inputs_in)
            load(weight_in, edge_weight.rearrange("(p j) -> p j", p=P), inputs_in)
            load(attr_in, edge_attr_3.rearrange("(p j) c -> p (j c)", p=P), inputs_in)
            load(X[:, :].rearrange("p (t n) -> p t n", t=T), x.rearrange("(t p) n -> p t n", p=P), inputs_in)
            for a, b in INIT:
                load(a, b, weights_in)
            sp.wait_ge(blanked, 4)
            nb = 22
            for k in range(BLOCKS // nb):
                load(by_dst.rearrange("(p b) c -> p (b c)", p=128)[:, k * nb * REC:(k + 1) * nb * REC],
                     msg[:, :, :, :].rearrange("p r g c -> p (r g c)")[:, 0:nb * REC], blank_out)
            load(by_src.rearrange("(p b) c -> p (b c)", p=128), SH[:, :], blank_out)

            def attrs(v, r, on):
                wait_past(sp, scattered[r], laps(v, r, 2) * 16 * CH)
                sp.dma_start(record[:, r, :, HW:REC],
                             edge_attr_64.rearrange("(p j) c -> p j c", p=P)[:, bass.ds(v * CH, CH), :]
                             ).then_inc(attr_landed[r], 16)
            turns(sp, EC // CH, 2, 2, 0, attrs)
            for r in range(2):
                sp.wait_ge(scattered[r], EC // CH // 2 * 16 * CH)
            load(DH[:, :].rearrange("p (b c) -> p b c", c=HW),
                 by_dst.rearrange("(p b) c -> p b c", p=128)[:, :, 0:HW], lists_in["dst"])
            for r in range(2):
                sp.wait_ge(pairs_out[r], EC // CH // 2 * 16 * CH)
            load(SH[:, :], by_src.rearrange("(p b) c -> p (b c)", p=128), lists_in["src"])
            sp.wait_ge(lists_ready["src"], 1)
            def load_edge_rows(s):
                sp.wait_ge(edge_clear, s + 1)
                for k in range(9):
                    at = k // 3 * 32 + k % 3 * 3
                    load(edge_in[at:at + 3, :], L3_gnn_W1e[s, 0:3, :], edge_rows_in)

            sp.wait_ge(projected, T * (PHASES.index("l1b") + 1))
            for a, b in table_loads(0):
                load(a, b, tables_in)

            def unit_attrs(v, r, on):
                if not isinstance(v, int) or v >= RING:
                    sp.wait_ge(oh_turned, UNITS + v - RING + 1)
                sp.dma_start(attr_slot(r).rearrange("p (g c) -> p g c", g=G), by_dst.rearrange("(p b) c -> p b c", p=128)
                             [:, bass.ds(v * G, G), HW:REC]).then_inc(attrs_in[r], 16)
            sp.wait_ge(projected, T * (PHASES.index("l2in") + 1))
            turns(sp, UNITS, RING, RING, 0, unit_attrs)
            for s in range(S3):
                if s == 0:
                    sp.wait_ge(finished, 1)
                    load_edge_rows(0)
                else:
                    sp.wait_ge(drawn, T * (PHASES.index(f"node{s - 1}") + 1))
                for a, b in net_loads(s):
                    load(a, b, nets_in)
                if s < S3 - 1:
                    sp.wait_ge(acc_done, UNITS * (SCATTERS.index(f"e{s}") + 1))
                    load_edge_rows(s + 1)
                    for a, b in table_loads(s + 1):
                        load(a, b, tables_in)
            sp.wait_ge(finished, LAST)
            sp.dma_start(out.rearrange("(t p) n -> p t n", p=P),
                         X[:, :].rearrange("p (t n) -> p t n", t=T)).then_inc(out_done, 16)
            sp.wait_ge(out_done, 16)
            for r in range(2):
                sp.wait_ge(rows_out[r], ROWS_TOTAL[r])

        @block.gpsimd
        def _(pool):
            pool.iota(IOTA[:, :], pattern=[[1, UNITS]], base=0, channel_multiplier=0,
                      allow_small_or_imprecise_dtypes=True).then_inc(consts, 1)
            pool.iota(IOTAB[:, :], pattern=[[1, 128]], base=0, channel_multiplier=0,
                      allow_small_or_imprecise_dtypes=True).then_inc(consts, 1)
            pool.memset(ONES[:, :], 1.0).then_inc(consts, 1)
            pool.memset(IDENT[:, :], 0.0).then_inc(consts, 1)
            pool.memset(EPSC[:, :], EPS).then_inc(consts, 1)
            pool.memset(IDENTB[:, :], 0.0).then_inc(consts, 1)
            pool.wait_ge(consts, 6)
            pool.affine_select(out=IDENTB[:, :], in_=IDENTB[:, :], compare_op=ALU.not_equal, fill=1.0, base=0,
                               pattern=[[-1, 128]], channel_multiplier=1).then_inc(consts, 1)
            pool.affine_select(out=IDENT[:, :], in_=IDENT[:, :], compare_op=ALU.not_equal, fill=1.0, base=0,
                               pattern=[[-1, 128]], channel_multiplier=1).then_inc(consts, 1)
            pool.affine_select(out=LTRI[:, :], in_=ONES[:, :], compare_op=ALU.is_ge, fill=0.0, base=-1,
                               pattern=[[1, 128]], channel_multiplier=-1).then_inc(consts, 1)

            def copies_done(n):
                pool.wait_ge(turn_ready, n)
                pool.sem_inc(apart, 1)

            pool.wait_ge(placed, 1)
            pool.wait_ge(blank_out, 16 * (BLOCKS // 22 + 1))

            def to_dst(v, r, on):
                if not isinstance(v, int) or v >= 2:
                    pool.wait_ge(scattered[r], laps(v, r, 2) * 16 * CH)
                pool.wait_ge(attr_landed[r], (laps(v, r, 2) + 1) * 16)
                pool.sem_inc(apart, 1)
                pool.tensor_copy(record[:, r, :, 0:HW], header[:, bass.ds(v * CH * HW, CH * HW)]
                                 .rearrange("p (j c) -> p j c", c=HW)).then_inc(turn_ready, 1)
                pool.tensor_copy(place_now[:, r * CH:(r + 1) * CH], place_of["dst"][:, bass.ds(v * CH, CH)]
                                 ).then_inc(turn_ready, 1)
                copies_done((v + 1) * 2)
                for j in range(CH):
                    pool.indirect_dma_start(
                        by_dst, bass.IndirectOffsetOnAxis(ap=place_now[:, r * CH + j:r * CH + j + 1], axis=0),
                        record[:, r, j, :], None).then_inc(scattered[r], 16)
            turns(pool, EC // CH, 2, 2, 0, to_dst)
            for r in range(2):
                pool.wait_ge(scattered[r], EC // CH // 2 * 16 * CH)
            pool.wait_ge(placed, 2)

            def to_src(v, r, on):
                wait_past(pool, pairs_out[r], laps(v, r, 2) * 16 * CH)
                pool.sem_inc(apart, 1)
                pool.tensor_copy(pair_now[:, r, :, :], pair[:, bass.ds(v * CH * 2, CH * 2)]
                                 .rearrange("p (j c) -> p j c", c=2)).then_inc(turn_ready, 1)
                pool.tensor_copy(place_now[:, r * CH:(r + 1) * CH], place_of["src"][:, bass.ds(v * CH, CH)]
                                 ).then_inc(turn_ready, 1)
                copies_done(EC // CH * 2 + (v + 1) * 2)
                for j in range(CH):
                    pool.indirect_dma_start(
                        by_src, bass.IndirectOffsetOnAxis(ap=place_now[:, r * CH + j:r * CH + j + 1], axis=0),
                        pair_now[:, r, j, :], None).then_inc(pairs_out[r], 16)
            turns(pool, EC // CH, 2, 2, 0, to_src)

            def gather(name, table, width, index):
                q = GATHERS.index(name)
                used, before = USERS[name]
                if q:
                    last, n = USERS[GATHERS[q - 1]]
                    pool.wait_ge(last, n + UNITS)

                def unit(v, r, on):
                    if not isinstance(v, int) or v >= RING:
                        pool.wait_ge(used, before + v - RING + 1)
                    if r % 2 == 0:
                        for k in range(2):
                            wait_past(pool, landed[r + k], (q * (UNITS // RING) + laps(v, r, RING)) * 16 * G)
                        pool.sem_inc(apart, 1)
                        pool.tensor_copy(gidx[:, r * G:(r + 2) * G], index[:, bass.ds(v * G, 2 * G)]
                                         ).then_inc(gidx_ready, 2)
                        pool.wait_ge(gidx_ready, q * UNITS + v + 2)
                    pool.sem_inc(apart, 1)
                    for g in range(G):
                        pool.indirect_dma_start(
                            gat[:, r, g, AW - width:AW] if width == HEADS else gat[:, r, g, 0:width], None, table,
                            bass.IndirectOffsetOnAxis(ap=gidx[:, r * G + g:r * G + g + 1], axis=0)
                            ).then_inc(landed[r], 16)
                turns(pool, UNITS, RING, RING, 0, unit)

            pool.wait_ge(lists_ready["src"], 1)
            await_rows(pool, "l0")
            gather("max", rows_hr, HEADS, SIDX)
            gather("l0", rows_h, AW, SIDX)
            for name in ("l1a", "l1b"):
                await_rows(pool, name)
                gather(name, rows, D, DIDX)
            await_rows(pool, "l2in")
            gather("l2", rows, D, DIDX)
            for s in range(S3):
                await_rows(pool, "l3in" if s == 0 else f"next{s - 1}")
                gather(f"e{s}", rows, D, DIDX)

        @block.scalar
        def _(act):
            def roots(k):
                act.wait_ge(moments, k)
                act.activation(SD[:, :], MV[:, :].rearrange("p (t c) -> p t c", c=2)[:, :, 1], ACT.Sqrt,
                               bias=EPSC[0:P, :]).then_inc(rooted, 1)

            def project(name, A=KEEP, w=D, func=ACT.Copy, row_source=None):
                k = PHASES.index(name) * T
                km = MAKES.index(name) * T if name in MAKES else 0

                def step(t, r, on):
                    if on(0):
                        if name in MAKES:
                            act.wait_ge(made, km + t + 1)
                        hold(act, turned, k + t - 1)
                        act.activation(staged[:, r, :], tile(A, t, 0, D, w), func).then_inc(staged_in, 1)
                    if on(1):
                        o = (r + 1) % 2
                        act.wait_ge(turned, k + t)
                        wait_past(act, projected, k + t - 2)
                        act.activation(hT[:, o, :], psum[o][:, 0:2 * P], ACT.Copy).then_inc(turned_in, 1)
                    if row_source is not None and on(3):
                        act.wait_ge(drawn, k + t - 2)
                        row_source(t - 3, (r + 1) % 2)
                turns(act, T, 2, 4, 3, step)

            def rows_from(A, w=D):
                def go(t, r):
                    act.dma_start(rows[bass.ds(t * P, P), :], tile(A, t, 0, D, w)).then_inc(rows_out[r], 16)
                return go

            def rows_h_from(t, r):
                act.dma_start(rows_h[bass.ds(t * P, P), :], wide[:, r, :]).then_inc(rows_out[r], 16)
                act.dma_start(rows_hr[bass.ds(t * P, P), :], wide[:, r, D:AW]).then_inc(rows_out[r], 16)

            def rows_staged(t, r):
                act.dma_start(rows[bass.ds(t * P, P), :], wide[:, r, 0:D]).then_inc(rows_out[r], 16)

            act.wait_ge(consts, 9)
            roots(1)
            project("l0", func=ACT.Relu, row_source=rows_h_from)

            def candidates(v, r, on):
                act.wait_ge(max_oh, v + 1)
                act.wait_ge(landed[r], (laps(v, r, RING) + 1) * 16 * G)
                wait_past(act, max_rows, v - 1)
                for h in range(HEADS):
                    for g in range(G):
                        ins = act.activation(cand[:, r % 2, h, g, :], oh[:, r, g, 0:P], ACT.Identity,
                                             bias=gat[:, r, g, D + h:D + h + 1])
                ins.then_inc(max_neg, 1)
            turns(act, UNITS, RING, RING, 0, candidates)

            def attend(v, r, on):
                if on(1):
                    o = (r + 3) % RING
                    act.wait_ge(oh_turned, v)
                    act.activation(ohbT[0:P, o, :], psum_b[o % 2][0:P, 0:G * 128], ACT.Copy).then_inc(ohT_ready, 1)
                if on(3):
                    o = (r + 1) % RING
                    act.wait_ge(scores, v - 2)
                    act.activation(msg[:, o, :, D:AW], small[:, o * 8:o * 8 + 8].rearrange("p (g h) -> p g h", g=G),
                                   ACT.Exp).then_inc(probs, 1)
                if on(4):
                    wait_past(act, part_ready, UNITS + v - 5)
                    act.activation(ohw[:, r % 2, :, :], ohb[:, (r + 4) % OHS, :, :], ACT.Copy).then_inc(ohw_ready, 1)
            turns(act, UNITS, OHS, OHS, 4, attend)
            act.wait_ge(hm_ready, 2)
            act.activation(DINV[:, :], CNT[:, :].rearrange("p (t c) -> p t c", c=2)[:, :, 0], ACT.Sqrt
                           ).then_inc(rooted, 1)
            roots(2)
            project("l1a", func=ACT.Relu, row_source=rows_from(Y))
            project("l1b", row_source=rows_from(Y))
            roots(3)
            project("l2in", func=ACT.Relu, row_source=rows_from(KEEP))

            def attrs_in_sbuf(v, r, on):
                act.wait_ge(oh_turned, UNITS + v + 1)
                act.activation(ohT[:, r, 0:128], psum[r % 2][:, 0:128], ACT.Copy).then_inc(ohT_ready, 1)
            turns(act, UNITS, RING, RING, 0, attrs_in_sbuf)
            act.wait_ge(acc_done, UNITS * (SCATTERS.index("l2") + 1))
            project("l2out", ACC, AW)
            act.wait_ge(bn_sqsum, 2)
            act.activation(wide[:, 1, 0:D], wide[:, 1, 0:D], ACT.Sqrt, bias=EPSC[0:P, :]).then_inc(rooted, 1)
            roots(4)
            project("l3in", func=ACT.Relu, row_source=rows_staged)
            for s in range(S3):
                q = TURNS_BEFORE_E + s * UNITS

                def edge_net(v, r, on):
                    if on(1):
                        o = (r + 3) % RING
                        act.wait_ge(oh_turned, q + v)
                        act.activation(ohbT[0:P, o, :], psum_b[o % 2][0:P, 0:G * 128], ACT.Copy)
                        act.activation(atT[:, o, :], psum_b[o % 2][0:AK, G * 128:2 * G * 128], ACT.Copy
                                       ).then_inc(ohT_ready, 1)
                    if on(5):
                        o = (r + 3) % RING
                        act.wait_ge(recip, s * UNITS + v - 4)
                        wait_past(act, part_ready, SCATTERS.index(f"e{s}") * UNITS + v - 6)
                        for g in range(G):
                            ins = act.activation(ohw[:, o % 2, g, :], ohb[:, (r + 3) % OHS, g, :], ACT.Copy,
                                                 scale=small[:, 8 + o * 2 + g:9 + o * 2 + g])
                        ins.then_inc(ohw_ready, 1)
                    if on(3):
                        o = (r + 1) % RING
                        act.wait_ge(msgs, MSGS_BEFORE_E + s * UNITS + v - 2)
                        act.activation(msg[:, o, :, 0:D], msg[:, o, :, 0:D], ACT.Relu).then_inc(msg_relu, 1)
                    if on(4):
                        o = r % RING
                        act.wait_ge(msg_stats, (s * UNITS + v - 3) * 2)
                        act.activation(small[:, o * 2:o * 2 + 2], msg[:, o, :, D + 1], ACT.Sqrt,
                                       bias=EPSC[:, :]).then_inc(msg_sd, 1)
                turns(act, UNITS, OHS, OHS, 5, edge_net)
                project(f"agg{s}")
                act.wait_ge(drawn, T * PHASES.index(f"mix{s}"))
                project(f"mix{s}", ACC, AW)
                roots(5 + s)
                project(f"node{s}")
                if s < S3 - 1:
                    act.wait_ge(drawn, T * PHASES.index(f"next{s}"))
                    project(f"next{s}", ACC, AW, row_source=rows_staged)

        @block.vector
        def _(dve):
            ca, cb, cu = Chain(dve, chain_a), Chain(dve, chain_b), Chain(dve, chain_u)
            link = ca.link

            flat = msg[:, :, :, :].rearrange("p r g c -> p (r g c)")
            dve.memset(flat, 0.0).then_inc(blanked, 1)
            dve.memset(SH[:, :], 0.0).then_inc(blanked, 1)
            dve.wait_ge(blanked, 2)
            dve.memset(flat[:, 0:22 * REC].rearrange("p (j c) -> p j c", c=REC)[:, :, 0], -1.0).then_inc(blanked, 1)
            dve.memset(SH[:, :].rearrange("p (j c) -> p j c", c=2)[:, :, 0], -1.0).then_inc(blanked, 1)

            dve.wait_ge(inputs_in, 16 * 5)
            dve.wait_ge(consts, 9)
            head = header.rearrange("p (j c) -> p j c", c=HW)
            two_ = pair.rearrange("p (j c) -> p j c", c=2)
            link(dve.tensor_scalar(threshold[:, :], IOTA[:, 0:T], float(P), None, ALU.mult))
            link(dve.memset(ones_row, 1.0))
            link(dve.memset(header, 0.0))
            for name in ("dst", "src"):
                link(dve.tensor_copy(key_of[name], raw[name]))
            link(dve.tensor_copy(head[:, :, 1], key_of["src"]))
            link(dve.tensor_copy(head[:, :, 2], weight_in))
            link(dve.tensor_copy(head[:, :, 3], ones_row))
            link(dve.tensor_copy(head[:, :, 4:7], attr_in.rearrange("p (j c) -> p j c", c=3)))
            link(dve.tensor_copy(two_[:, :, 1], key_of["dst"]))

            for which, name in enumerate(("dst", "src")):
                key = key_of[name]
                local = head[:, :, 0] if name == "dst" else two_[:, :, 0]
                link(dve.memset(bucket, 0.0))
                link(dve.memset(rank, 0.0))
                ca.loop(T - 1, 1, lambda t: ca.link(dve.scalar_tensor_tensor(
                    bucket, key, threshold[0:P, bass.ds(t + 1, 1)], bucket, ALU.is_ge, ALU.add)))
                link(dve.scalar_tensor_tensor(local, bucket, -float(P), key, ALU.mult, ALU.add))

                def ranks(t):
                    ca.link(dve.tensor_scalar(mask, bucket, IOTA[0:P, bass.ds(t, 1)], None, ALU.is_equal))
                    ca.link(dve.tensor_tensor_scan(prefix, ones_row, mask, 0.0, ALU.mult, ALU.add))
                    dve.sem_inc(apart, 1)
                    ca.link(dve.tensor_copy(count[:, bass.ds(t, 1)], prefix[:, EC - 1:EC]))
                    ca.link(dve.tensor_tensor(mask, mask, prefix, ALU.mult))
                    ca.link(dve.tensor_tensor(rank, rank, mask, ALU.add))
                ca.loop(T, 5, ranks)
                dve.sem_inc(counted, 1)
                dve.wait_ge(prefixed, which + 1)
                total, below = psum[2][:, 0:T], psum[3][0:P, 0:T]
                link(dve.tensor_scalar(units_i[:, :], total, float(CAP - 1), None, ALU.add))
                link(dve.tensor_scalar(units_i[:, :], units_i[:, :], CAP.bit_length() - 1, None, ALU.logical_shift_right))
                link(dve.tensor_copy(units[:, :], units_i[:, :]))
                link(dve.tensor_tensor_scan(unit_end[:, :], ONES[:, 0:T], units[:, :], 0.0, ALU.mult, ALU.add))
                link(dve.tensor_tensor(unit_start[:, :], unit_end[:, :], units[:, :], ALU.subtract))
                link(dve.scalar_tensor_tensor(base[:, :], unit_start[0:P, :], float(CAP), below, ALU.mult, ALU.add))
                link(dve.tensor_scalar(base[:, :], base[:, :], -1.0, None, ALU.add))

                def places(t):
                    ca.link(dve.tensor_scalar(mask, bucket, IOTA[0:P, bass.ds(t, 1)], base[:, bass.ds(t, 1)],
                                              ALU.is_equal, ALU.mult))
                    ca.link(dve.tensor_tensor(rank, rank, mask, ALU.add))
                ca.loop(T, 2, places)
                link(dve.tensor_copy(place_i, rank))
                link(dve.tensor_scalar(place_j, place_i, 7, None, ALU.logical_shift_right))
                link(dve.tensor_scalar(place_i, place_i, 127, None, ALU.bitwise_and))
                dve.scalar_tensor_tensor(place_of[name], place_i, float(BLOCKS), place_j, ALU.mult,
                                         ALU.add).then_inc(placed, 1)
                link(dve.memset(tile_f[:, :], 0.0))
                ca.loop(T - 1, 1, lambda t: ca.link(dve.scalar_tensor_tensor(
                    tile_f[:, :], IOTA[0:1, 0:UNITS], unit_start[0:1, bass.ds(t + 1, 1)], tile_f[:, :],
                    ALU.is_ge, ALU.add)))
                link(dve.tensor_copy((DTILE if name == "dst" else STILE)[:, :], tile_f[:, :]))

            def mv(t, c):
                return MV[:, bass.ds(t * 2 + c, 1)]

            def stats(A, t, w=D):
                dve.sem_inc(apart, 1)
                ca.link(dve.bn_stats(ST[:, :], tile(A, t, 0, D, w)))
                dve.sem_inc(apart, 1)
                ca.link(dve.bn_aggr(AG[:, :], ST[:, :]))
                dve.sem_inc(apart, 1)
                ca.link(dve.tensor_copy(MV[:, bass.ds(t * 2, 2)], AG[:, :]))

            def rstd(k):
                dve.wait_ge(rooted, k)
                link(dve.reciprocal(RS[:, :], SD[:, :]))

            def normalize(A, t):
                return dve.tensor_scalar(tile(KEEP, t), tile(A, t), mv(t, 0), RS[:, bass.ds(t, 1)],
                                         ALU.subtract, ALU.mult)

            def project(name, make, per_make, draw, per_draw, before=None):
                k = PHASES.index(name) * T
                a0, b0 = ca.n, cb.n

                def step(t, r, on):
                    if make is not None and on(0):
                        ca.at(a0 + t * per_make)
                        make(t).then_inc(made, 1)
                    if on(2):
                        dve.wait_ge(projected, k + t - 1)
                        if before is not None:
                            b, per = before
                            wait_past(dve, rows_out[r], row_dmas(b, r) + 16 * per * laps(t - 2, r, 2))
                        wait_past(dve, drawn, k + t - 2)
                        dve.sem_inc(apart, 1)
                        cb.at(b0 + (t - 2) * per_draw)
                        draw(t - 2, r).then_inc(drawn, 1)
                turns(dve, T, 2, 4, 2, step)
                ca.at(a0 + T * per_make if make is not None else a0)
                cb.at(b0 + T * per_draw)

            def product(r, j):
                return (psum[2 + r][0:P, (j % 2) * D:(j % 2 + 1) * D] if j < 2 else psum[4 + r][0:P, 0:D])

            ca.loop(T, 3, lambda t: stats(X, t))
            dve.sem_inc(moments, 1)
            rstd(1)
            await_init(dve)

            def draw_h(t, r):
                hrow = wide[:, r, 0:D]
                cb.link(dve.tensor_scalar(wide[:, 2, 0:D], product(r, 0), 0.0, None, ALU.max))
                cb.link(dve.scalar_tensor_tensor(hrow, product(r, 0), 0.0, wide[:, 2, 0:D], ALU.min, ALU.add))
                cb.link(dve.tensor_tensor(wide[:, 2, 0:D], hrow, ALR[:, 0:D], ALU.mult))
                dve.sem_inc(apart, 1)
                cb.link(dve.tensor_reduce(HL[:, bass.ds(t * HEADS, HEADS)],
                                          wide[:, 2, 0:D].rearrange("p (h f) -> p h f", h=HEADS), AX_X, ALU.add))
                cb.link(dve.tensor_tensor(wide[:, 2, 0:D], hrow, ALR[:, D:2 * D], ALU.mult))
                return dve.tensor_reduce(wide[:, r, D:AW], wide[:, 2, 0:D].rearrange("p (h f) -> p h f", h=HEADS),
                                         AX_X, ALU.add)
            project("l0", lambda t: normalize(X, t), 0, draw_h, 5, before=(0, 2))

            def split(link_, A, parts, rest):
                link_(dve.tensor_copy(parts[0], A))
                link_(dve.tensor_tensor(rest, A, parts[0], ALU.subtract))
                link_(dve.tensor_copy(parts[1], rest))
                return dve.tensor_tensor(parts[2], rest, parts[1], ALU.subtract)

            def one_hot(dest, head_, hw, v, r, scale=None):
                for g in range(G):
                    col = (v * G + g) * hw
                    ins = dve.tensor_scalar(dest[:, r, g, 0:P], (IOTAB if dest is ohb else IOTA)[:, 0:P], head_[:, bass.ds(col, 1)],
                                            None if scale is None else scale(v, g), ALU.is_equal,
                                            *([] if scale is None else [ALU.mult]))
                return ins

            def tiles_of(table, lag, ring=RING):
                return Tiles(mybir.EngineType.DVE, table, lag, ring)

            def accumulate(q, v, r, t, width, A=ACC, aw=AW):
                dve.wait_ge(part_ready, q + v + 1)
                wait_past(dve, acc_done, q + v)
                dve.tensor_tensor(A[:, bass.ds(t * aw, width)], psum[6 + r % 2][0:P, 0:width],
                                  A[:, bass.ds(t * aw, width)], ALU.add).then_inc(acc_done, 1)

            def clear():
                dve.memset(ACC[:, :], 0.0).then_inc(accs_clear, 1)

            dve.wait_ge(lists_in["dst"], 16)
            link(dve.tensor_copy(DIDX[:, :], DH[:, :].rearrange("p (b c) -> p b c", c=HW)[:, :, 1]))
            dve.sem_inc(lists_ready["dst"], 1)
            link(dve.memset(CNT[:, :], 0.0))

            def degrees(v, r, on):
                if on(0):
                    one_hot(oh, DH, HW, v, r).then_inc(oh_ready, 1)
                if on(2):
                    accumulate(0, v - 2, (r + 2) % RING, tiles.at(v, r), 2, CNT, 2)
            tiles = tiles_of(DTILE, 2)
            turns(dve, UNITS, RING, RING, 2, degrees)

            dve.wait_ge(lists_in["src"], 16)
            link(dve.tensor_copy(SIDX[:, :], SH[:, :].rearrange("p (b c) -> p b c", c=2)[:, :, 1]))
            dve.sem_inc(lists_ready["src"], 1)
            link(dve.memset(MX[:, :], -BIG))

            def maxima(v, r, on):
                if on(0):
                    for g in range(G):
                        ins = dve.tensor_scalar(oh[:, r, g, 0:P], IOTA[:, 0:P], SH[:, bass.ds((v * G + g) * 2, 1)],
                                                -BIG, ALU.not_equal, ALU.mult)
                    ins.then_inc(max_oh, 1)
                if on(3):
                    dve.wait_ge(max_rows, v - 2)
                    wait_past(dve, max_done, v - 3)
                    for k in range(2):
                        ins = dve.tensor_reduce(
                            wide[:, 3, D + 2 * k:D + 2 * k + 2],
                            psum[2 + 2 * ((r + 1) % 2) + k][0:P, :].rearrange("p (h e) -> p h e", h=2), AX_X, ALU.max)
                    cu.at(v - 3)
                    cu.link(ins)
                    dve.sem_inc(apart, 1)
                    t = tiles.at(v, r)
                    dve.tensor_tensor(MX[:, bass.ds(t * HEADS, HEADS)], wide[:, 3, D:AW],
                                      MX[:, bass.ds(t * HEADS, HEADS)], ALU.max).then_inc(max_done, 1)
            tiles = tiles_of(STILE, 3)
            turns(dve, UNITS, RING, RING, 3, maxima)
            dve.wait_ge(max_done, UNITS)
            clear()
            hm = HM[:, :].rearrange("p (t c) -> p t c", c=2 * HEADS)
            hl = HL[:, :].rearrange("p (t h) -> p t h", h=HEADS)
            mx = MX[:, :].rearrange("p (t h) -> p t h", h=HEADS)
            link(dve.tensor_copy(hm[:, :, 0:HEADS], hl))
            link(dve.tensor_tensor(mx, mx, hl, ALU.add))
            link(dve.scalar_tensor_tensor(hm[:, :, HEADS:], mx, ALPHA, mx, ALU.mult, ALU.max))
            parts = HMB.rearrange("p (k n) -> p k n", k=3)
            link(split(link, HM[:, :], [parts[:, k, :] for k in range(3)], wide[:, 0, 0:T * 2 * HEADS]))
            dve.sem_inc(hm_ready, 1)

            def attention(v, r, on):
                if on(6):
                    accumulate(UNITS, v - 6, (r + 2) % RING, tiles.at(v, r), AW)
                if on(3):
                    o = (r + 1) % RING
                    dve.wait_ge(mid_ready, v - 2)
                    dve.wait_ge(landed[o], landings("l0", v - 3, o))
                    cu.at(UNITS + (v - 3) * 3)
                    hs = psum[2 + o % 2][:, 0:G * 8].rearrange("p (g c) -> p g c", g=G)
                    e = small[:, o * 8:o * 8 + 8].rearrange("p (g h) -> p g h", g=G)
                    summed = cu.mark(dve.tensor_tensor(e, hs[:, :, 0:HEADS], gat[:, o, :, D:AW], ALU.add))
                if on(0):
                    one_hot(ohb, SH, 2, v, r).then_inc(oh_ready, 1)
                if on(3):
                    cu.await_(summed)
                    leaked = cu.mark(dve.scalar_tensor_tensor(e, e, ALPHA, e, ALU.mult, ALU.max))

                def weigh(g):
                    k = r % RING
                    return dve.tensor_tensor(
                        msg[:, k, g, 0:D].rearrange("p (h f) -> p h f", h=HEADS),
                        gat[:, k, g, 0:D].rearrange("p (h f) -> p h f", h=HEADS),
                        msg[:, k, g, D:AW].unsqueeze(2).broadcast_to([128, HEADS, HD]), ALU.mult)
                if on(4):
                    dve.wait_ge(probs, v - 3)
                    weigh(0)
                if on(3):
                    cu.await_(leaked)
                    lowered = cu.mark(dve.tensor_tensor(e, e, hs[:, :, HEADS:], ALU.subtract))
                if on(4):
                    weigh(1).then_inc(msgs, 1)
                if on(3):
                    cu.await_(lowered)
                    dve.tensor_scalar(e, e, 0.0, None, ALU.min).then_inc(scores, 1)
            tiles = tiles_of(STILE, 6, OHS)
            turns(dve, UNITS, OHS, OHS, 6, attention)
            dve.wait_ge(acc_done, 2 * UNITS)

            def acc(t, lo=0, hi=D):
                return tile(ACC, t, lo, hi, AW)

            accs = ACC[:, :].rearrange("p (t c) -> p t c", c=AW)
            rden = RDEN[:, :].rearrange("p (t h) -> p t h", h=HEADS)
            link(dve.tensor_scalar(rden, accs[:, :, D:AW], 1e-16, None, ALU.add))
            link(dve.reciprocal(rden, rden))

            def add_attention(t):
                ca.link(dve.tensor_tensor(acc(t).rearrange("p (h f) -> p h f", h=HEADS),
                                          acc(t).rearrange("p (h f) -> p h f", h=HEADS),
                                          RDEN[:, bass.ds(t * HEADS, HEADS)].unsqueeze(2).broadcast_to([P, HEADS, HD]),
                                          ALU.mult))
                ca.link(dve.tensor_tensor(tile(X, t), tile(X, t), acc(t), ALU.add))
                stats(X, t)
            ca.loop(T, 5, add_attention)

            cnts = CNT[:, :].rearrange("p (t c) -> p t c", c=2)
            link(dve.tensor_scalar(cnts[:, :, 0], cnts[:, :, 0], 1.0, None, ALU.add))
            link(dve.tensor_scalar(RDEN[:, 0:T], cnts[:, :, 0], 0.0, None, ALU.is_gt))
            link(dve.tensor_scalar(cnts[:, :, 0], cnts[:, :, 0], 1e-30, None, ALU.max))
            dve.sem_inc(hm_ready, 1)
            dve.wait_ge(rooted, 2)
            link(dve.reciprocal(DINV[:, :], DINV[:, :]))
            link(dve.tensor_tensor(DINV[:, :], DINV[:, :], RDEN[:, 0:T], ALU.mult))
            dve.sem_inc(moments, 1)
            rstd(3)

            def dinv(t):
                return DINV[:, bass.ds(t, 1)]

            def draw_scaled(t, r):
                return dve.tensor_scalar(tile(Y, t), product(r, 0), dinv(t), None, ALU.mult)
            project("l1a", lambda t: normalize(X, t), 0, draw_scaled, 0)
            clear()

            def weighted(name):
                q = SCATTERS.index(name) * UNITS

                def unit(v, r, on):
                    if on(2):
                        accumulate(q, v - 2, (r + 2) % RING, tiles.at(v, r), D)
                    if on(0):
                        one_hot(oh, DH, HW, v, r, lambda v, g: DH[:, bass.ds((v * G + g) * HW + 2, 1)]
                                ).then_inc(oh_ready, 1)
                tiles = tiles_of(DTILE, 2)
                turns(dve, UNITS, RING, RING, 2, unit)
                dve.wait_ge(acc_done, q + UNITS)

            def convolved(t, b, relu):
                link_ = ca.link
                dve.sem_inc(apart, 1)
                link_(dve.tensor_tensor(acc(t), acc(t), tile(Y, t), ALU.add))
                link_(dve.scalar_tensor_tensor(acc(t), acc(t), dinv(t), bias(b), ALU.mult, ALU.add))
                if relu:
                    link_(dve.tensor_scalar(tile(KEEP, t), tile(KEEP, t), 0.0, 0.1, ALU.max, ALU.mult))
                else:
                    link_(dve.tensor_scalar(tile(KEEP, t), tile(KEEP, t), 0.1, None, ALU.mult))
                return dve.scalar_tensor_tensor(tile(KEEP, t), acc(t), 0.9, tile(KEEP, t), ALU.mult, ALU.add)

            weighted("l1a")
            project("l1b", lambda t: convolved(t, 2, True), 3, draw_scaled, 0)
            clear()
            weighted("l1b")

            def add_convolved(t):
                ca.link(convolved(t, 3, False))
                ca.link(dve.tensor_tensor(tile(X, t), tile(X, t), tile(KEEP, t), ALU.add))
                stats(X, t)
            ca.loop(T, 8, add_convolved)
            dve.sem_inc(moments, 1)
            rstd(4)

            def draw_root(t, r):
                cb.link(dve.tensor_tensor(tile(Y, t), product(r, 0), bias(4), ALU.add))
                cb.link(dve.tensor_tensor(tile(X, t), product(r, 1), tile(X, t), ALU.add))
                return dve.tensor_scalar(tile(KEEP, t), tile(KEEP, t), 0.0, None, ALU.max)
            project("l2in", lambda t: normalize(X, t), 0, draw_root, 2)
            clear()

            def edge_messages(v, r, on):
                if on(2):
                    o = (r + 2) % RING
                    dve.wait_ge(mid_ready, UNITS + v - 1)
                    dve.wait_ge(landed[o], (GATHERS.index("l2") * (UNITS // RING) + laps(v - 2, o, RING) + 1) * 16 * G)
                    for g in range(G):
                        ins = dve.tensor_tensor(msg[:, o, g, 0:D], psum[2 + 2 * (o % 2) + g][:, 0:D],
                                                gat[:, o, g, 0:D], ALU.mult)
                    ins.then_inc(msgs, 1)
                if on(3):
                    accumulate(SCATTERS.index("l2") * UNITS, v - 3, (r + 1) % RING, tiles.at(v, r), D)
                if on(0):
                    one_hot(oh, DH, HW, v, r).then_inc(oh_ready, 1)
            tiles = tiles_of(DTILE, 3)
            turns(dve, UNITS, RING, 2 * RING, 3, edge_messages)
            dve.wait_ge(acc_done, (SCATTERS.index("l2") + 1) * UNITS)

            def draw_bn(t, r):
                cb.link(dve.tensor_tensor(tile(KEEP, t), product(r, 0), tile(Y, t), ALU.add))
                return dve.tensor_scalar(tile(KEEP, t), tile(KEEP, t), 0.0, None, ALU.max)
            project("l2out", None, 0, draw_bn, 1)
            mean, scale = wide[:, 0, 0:D], wide[:, 1, 0:D]
            dve.wait_ge(bn_sum, 1)
            link(dve.tensor_scalar(mean, psum[6][0:P, 0:D], 1.0 / N, None, ALU.mult))

            def squares(t):
                ca.link(dve.tensor_tensor(tile(KEEP, t), tile(KEEP, t), mean, ALU.subtract))
                dve.tensor_tensor(tile(Y, t), tile(KEEP, t), tile(KEEP, t), ALU.mult).then_inc(bn_sq, 1)
            ca.loop(T, 1, squares)
            dve.wait_ge(bn_sqsum, 1)
            link(dve.tensor_scalar(scale, psum[7][0:P, 0:D], 1.0 / N, None, ALU.mult))
            dve.sem_inc(bn_sqsum, 1)
            dve.wait_ge(rooted, 5)
            link(dve.reciprocal(scale, scale))
            link(dve.tensor_tensor(scale, scale, bias(5), ALU.mult))

            def add_bn(t):
                ca.link(dve.tensor_tensor(tile(KEEP, t), tile(KEEP, t), scale, ALU.mult))
                ca.link(dve.tensor_tensor(tile(KEEP, t), tile(KEEP, t), bias(6), ALU.add))
                ca.link(dve.tensor_tensor(tile(X, t), tile(X, t), tile(KEEP, t), ALU.add))
                stats(X, t)
            ca.loop(T, 6, add_bn)
            dve.sem_inc(finished, 1)
            dve.sem_inc(moments, 1)
            heads = DH[:, :].rearrange("p (b c) -> p b c", c=HW)
            a_f, r_f = (BT[:, k * 3 * BLOCKS:(k + 1) * 3 * BLOCKS].rearrange("p (b c) -> p b c", c=3)
                        for k in range(2))
            heads_b = DH[:, :].bitcast(BF16).rearrange("p (b c) -> p b c", c=2 * HW)
            link(dve.tensor_copy(a_f, heads[:, :, 4:7]))
            link(split(link, a_f, [heads_b[:, :, 6 + 3 * k:9 + 3 * k] for k in range(3)], r_f))
            link(dve.memset(free_b[:, 0:RING * G * AK], 0.0))
            link(dve.memset(edge_in, 0.0))
            dve.sem_inc(edge_clear, 1)

            def edge_weights(s):
                dve.wait_ge(edge_rows_in, 16 * 9 * (s + 1))
                rest = wide[0:AK, 2, 0:D]
                link(dve.tensor_copy(edge_w, edge_in))
                link(dve.tensor_tensor(rest, edge_in, edge_w, ALU.subtract))
                link(dve.tensor_copy(edge_w[32:64, :], rest[32:64, :]))
                link(dve.tensor_copy(edge_w[64:AK, :], rest[64:AK, :]))
                link(dve.tensor_tensor(edge_w[64:AK, :], rest[64:AK, :], edge_w[64:AK, :], ALU.subtract))
                dve.sem_inc(edge_split, 1)
                if s < S3 - 1:
                    dve.sem_inc(edge_clear, 1)

            def own(t, k):
                if k < 2:
                    return BTB[0:P, bass.ds(t * 2 * D + k * D, D)]
                return KEEPB[:, bass.ds(t * 2 * D, D)]

            def draw_tables(t, r):
                rest = wide[:, 3, 0:D]
                own_sum = cb.mark(dve.tensor_tensor(wide[:, 2, 0:D], product(r, 1), bias(0), ALU.add))
                cb.mark(dve.tensor_copy(wide[:, r, 0:D], product(r, 0)))
                cb.await_(own_sum)
                dve.sem_inc(apart, 1)
                hi = cb.mark(dve.tensor_copy(own(t, 0), wide[:, 2, 0:D]))
                cb.mark(dve.tensor_tensor(tile(Y, t), product(r, 2), bias(1), ALU.add))
                cb.await_(hi)
                cb.link(dve.tensor_tensor(rest, wide[:, 2, 0:D], own(t, 0), ALU.subtract))
                dve.sem_inc(apart, 1)
                cb.link(dve.tensor_copy(own(t, 1), rest))
                return dve.tensor_tensor(own(t, 2), rest, own(t, 1), ALU.subtract)

            rstd(6)
            await_tables(dve, 0)
            project("l3in", lambda t: normalize(X, t), 0, draw_tables, 6, before=(ROWS.index("l3in"), 1))
            for s in range(S3):
                q = SCATTERS.index(f"e{s}") * UNITS
                m0 = MSGS_BEFORE_E + s * UNITS
                clear()
                edge_weights(s)

                def edge_net(v, r, on):
                    if on(7):
                        accumulate(q, v - 7, (r + 1) % RING, tiles.at(v, r), D + 2)
                    if on(0):
                        dve.tensor_copy(
                            atb[:, r % RING, :, :].rearrange("p g (q c) -> p g q c", q=3)[:, :, :, 0:9],
                            DH[:, bass.ds(v * G * HW, G * HW)].bitcast(BF16).rearrange("p (g c) -> p g c", g=G)
                            [:, :, 6:15].unsqueeze(2).broadcast_to([128, G, 3, 9]))
                        one_hot(ohb, DH, HW, v, r).then_inc(oh_ready, 1)
                    if on(5):
                        o = (r + 3) % RING
                        dve.wait_ge(msg_sd, s * UNITS + v - 4)
                        dve.reciprocal(small[:, 8 + o * 2:8 + o * 2 + 2], small[:, o * 2:o * 2 + 2]).then_inc(recip, 1)
                    if on(4):
                        o = r % RING
                        dve.wait_ge(msg_relu, s * UNITS + v - 3)
                        for g in range(G):
                            ins = dve.bn_stats(small[:, 16 + g * 6:22 + g * 6], msg[:, o, g, 0:D])
                        cu.at(cu0 + (v - 4))
                        taken = cu.mark(ins)
                    if on(3):
                        o = (r + 1) % RING
                        dve.wait_ge(mid_ready, 2 * UNITS + s * UNITS + v - 2)
                        dve.wait_ge(landed[o], landings(f"e{s}", v - 3, o))
                        dve.tensor_tensor(msg[:, o, :, 0:D], psum[2 + o % 2][:, :].rearrange("p (g f) -> p g f", g=G),
                                          gat[:, o, :, 0:D], ALU.add).then_inc(msgs, 1)
                    if on(4):
                        o = r % RING
                        cu.await_(taken)
                        dve.sem_inc(apart, 1)
                        for g in range(G):
                            dve.bn_aggr(msg[:, o, g, D:D + 2], small[:, 16 + g * 6:22 + g * 6]).then_inc(msg_stats, 1)
                cu0 = UNITS * 4 + s * UNITS
                tiles = tiles_of(DTILE, 7, OHS)
                turns(dve, UNITS, OHS, OHS, 7, edge_net)
                dve.wait_ge(acc_done, q + UNITS)
                await_nets(dve, s)

                def summed(t):
                    link_ = ca.link
                    dve.sem_inc(apart, 1)
                    link_(dve.tensor_scalar(tile(KEEP, t), acc(t), acc(t, D, D + 1), None, ALU.subtract))
                    link_(dve.tensor_tensor(tile(KEEP, t), tile(KEEP, t), bias(2), ALU.mult))
                    return dve.scalar_tensor_tensor(tile(KEEP, t), bias(3), CNT[:, bass.ds(t * 2 + 1, 1)],
                                                    tile(KEEP, t), ALU.mult, ALU.add)

                def draw_agg(t, r):
                    return dve.scalar_tensor_tensor(acc(t), bias(4), CNT[:, bass.ds(t * 2 + 1, 1)], product(r, 0),
                                                    ALU.mult, ALU.add)
                project(f"agg{s}", summed, 2, draw_agg, 0)

                def draw_mix(t, r):
                    cb.link(dve.tensor_tensor(tile(KEEP, t), product(r, 0), tile(Y, t), ALU.add))
                    cb.link(dve.tensor_scalar(tile(KEEP, t), tile(KEEP, t), 0.0, None, ALU.max))
                    dve.sem_inc(apart, 1)
                    cb.link(dve.bn_stats(ST[:, :], tile(KEEP, t)))
                    dve.sem_inc(apart, 1)
                    cb.link(dve.bn_aggr(AG[:, :], ST[:, :]))
                    dve.sem_inc(apart, 1)
                    return dve.tensor_copy(MV[:, bass.ds(t * 2, 2)], AG[:, :])
                project(f"mix{s}", None, 0, draw_mix, 4)
                dve.wait_ge(drawn, T * (PHASES.index(f"mix{s}") + 1))
                dve.sem_inc(moments, 1)
                rstd(7 + s)

                def normed(t):
                    dve.sem_inc(apart, 1)
                    ca.link(normalize(KEEP, t))
                    ca.link(dve.tensor_tensor(tile(KEEP, t), tile(KEEP, t), bias(5), ALU.mult))
                    return dve.tensor_tensor(tile(KEEP, t), tile(KEEP, t), bias(6), ALU.add)

                def draw_node(t, r):
                    return dve.tensor_tensor(acc(t), product(r, 0), bias(7), ALU.add)

                def draw_last(t, r):
                    cb.link(dve.tensor_tensor(acc(t), product(r, 0), bias(7), ALU.add))
                    return dve.tensor_tensor(tile(X, t), acc(t), tile(X, t), ALU.add)
                if s < S3 - 1:
                    project(f"node{s}", normed, 2, draw_node, 0)
                    await_tables(dve, s + 1)
                    project(f"next{s}", None, 0, draw_tables, 6, before=(ROWS.index(f"next{s}"), 1))
                else:
                    project(f"node{s}", normed, 2, draw_last, 1)
            dve.wait_ge(drawn, T * len(PHASES))
            dve.sem_inc(finished, LAST - 1)

        @block.tensor
        def _(pe):
            pe.wait_ge(consts, 9)
            for which in range(2):
                pe.wait_ge(placed, which) if which else None
                pe.wait_ge(counted, which + 1)
                pe.matmul(psum[2][:, 0:T], ONES[0:P, :], count[:, :], start=True, stop=True)
                pe.matmul(psum[3][0:P, 0:T], LTRI[0:P, 0:P], count[:, :], start=True, stop=True).then_inc(prefixed, 1)

            def project(name, weights, extra=None):
                k = PHASES.index(name) * T

                def step(t, r, on):
                    if on(0):
                        pe.wait_ge(staged_in, k + t + 1)
                        wait_past(pe, turned_in, k + t - 1)
                        for c in range(2):
                            ins = pe.transpose(psum[r][:, c * P:(c + 1) * P], staged[:, r, c * 128:(c + 1) * 128],
                                               IDENT[0:P, 0:P])
                        ins.then_inc(turned, 1)
                    if on(1):
                        o = (r + 1) % 2
                        pe.wait_ge(turned_in, k + t)
                        wait_past(pe, drawn, k + t - 2)
                        for j, W in enumerate(weights):
                            place = psum[2 + o][0:P, j * D:(j + 1) * D] if j < 2 else psum[4 + o][0:P, 0:D]
                            for c in range(2):
                                ins = pe.matmul(place, hT[:, o, c * P:(c + 1) * P], Wc(W, c), start=(c == 0), stop=(c == 1))
                        ins.then_inc(projected, 1)
                    if extra is not None and on(3):
                        pe.wait_ge(drawn, k + t - 2)
                        extra(t - 3)
                turns(pe, T, 2, 4, 3 if extra else 1, step)

            await_init(pe)
            project("l0", [W0])

            def scatter(q, v, r, lhs, rhs, width, ready, value):
                pe.wait_ge(ready, value)
                wait_past(pe, acc_done, q + v - 1)
                for g in range(G):
                    ins = pe.matmul(psum[6 + r % 2][0:P, 0:width], lhs(g), rhs(g), start=(g == 0), stop=(g == G - 1))
                return ins.then_inc(part_ready, 1)

            def await_gather(name, v, r):
                pe.wait_ge(landed[r], (GATHERS.index(name) * (UNITS // RING) + laps(v, r, RING) + 1) * 16 * G)

            def degrees(v, r, on):
                scatter(0, v, r, lambda g: oh[:, r, g, 0:P],
                        lambda g: DH[:, bass.ds((v * G + g) * HW + 2, 2)], 2, oh_ready, v + 1)
            pe.wait_ge(lists_in["dst"], 16)
            turns(pe, UNITS, RING, RING, 0, degrees)

            def maxima(v, r, on):
                pe.wait_ge(max_neg, v + 1)
                wait_past(pe, max_done, v - 1)
                for h in range(HEADS):
                    for g in range(G):
                        ins = pe.transpose(
                            psum[2 + 2 * (r % 2) + h // 2][0:P, (h % 2) * 256 + g * 128:(h % 2) * 256 + g * 128 + 128],
                            cand[:, r % 2, h, g, :], IDENT[:, :])
                ins.then_inc(max_rows, 1)
            turns(pe, UNITS, RING, RING, 0, maxima)

            def turn_one_hot(qt, q, v, r, attrs):
                pe.wait_ge(oh_ready, q + v + 1)
                wait_past(pe, ohT_ready, qt + v - 1)
                for g in range(G):
                    ins = pe.transpose(psum_b[r % 2][0:P, g * 128:(g + 1) * 128], ohb[:, r, g, :], IDENTB[:, :])
                    if attrs:
                        ins = pe.transpose(psum_b[r % 2][0:AK, (G + g) * 128:(G + g + 1) * 128], atb[:, r % RING, g, :],
                                           IDENTB[:, :])
                ins.then_inc(oh_turned, 1)

            def attention(v, r, on):
                if on(2):
                    o = (r + 2) % RING
                    pe.wait_ge(ohT_ready, v - 1)
                    t = tiles.at(v, r)
                    wait_past(pe, scores, v - 3)
                    for g in range(G):
                        for k in range(3):
                            ins = pe.matmul(psum[2 + o % 2][:, g * 8:g * 8 + 8], ohbT[0:P, o, g * 128:(g + 1) * 128],
                                            HMB[:, bass.ds(k * T * 8 + t * 8, 8)], start=(k == 0), stop=(k == 2))
                    ins.then_inc(mid_ready, 1)
                if on(1):
                    turn_one_hot(0, UNITS, v - 1, (r + 7) % OHS, False)
                if on(5):
                    o = (r + 3) % RING
                    pe.wait_ge(ohw_ready, v - 4)
                    scatter(UNITS, v - 5, o, lambda g: ohw[:, o % 2, g, :], lambda g: msg[:, o, g, :], AW, msgs, v - 4)
            pe.wait_ge(hm_ready, 1)
            tiles = Tiles(mybir.EngineType.PE, STILE, 2, OHS)
            turns(pe, UNITS, OHS, OHS, 5, attention)
            project("l1a", [WA])

            def weighted(name):
                q = SCATTERS.index(name) * UNITS

                def unit(v, r, on):
                    await_gather(name, v, r)
                    scatter(q, v, r, lambda g: oh[:, r, g, 0:P], lambda g: gat[:, r, g, 0:D], D, oh_ready, q + v + 1)
                turns(pe, UNITS, RING, RING, 0, unit)
            weighted("l1a")
            project("l1b", [WB])
            weighted("l1b")
            project("l2in", [WC, WD])

            def edge_messages(v, r, on):
                if on(0):
                    pe.wait_ge(attrs_in[r], (laps(v, r, RING) + 1) * 16)
                    wait_past(pe, ohT_ready, UNITS + v - 1)
                    pe.transpose(psum[r % 2][:, 0:128], attr_slot(r), IDENT[:, :]).then_inc(oh_turned, 1)
                if on(1):
                    o = (r + 3) % RING
                    pe.wait_ge(ohT_ready, UNITS + v)
                    wait_past(pe, msgs, UNITS + v - 2)
                    for g in range(G):
                        ins = pe.matmul(psum[2 + 2 * (o % 2) + g][:, 0:D], ohT[g * EA:(g + 1) * EA, o, 0:128],
                                        WE[g * EA:(g + 1) * EA, :], start=True, stop=True)
                    ins.then_inc(mid_ready, 1)
                if on(2):
                    o = (r + 2) % RING
                    q = SCATTERS.index("l2") * UNITS
                    pe.wait_ge(oh_ready, q + v - 1)
                    scatter(q, v - 2, o, lambda g: oh[:, o, g, 0:P], lambda g: msg[:, o, g, 0:D], D, msgs, UNITS + v - 1)
            turns(pe, UNITS, RING, 2 * RING, 2, edge_messages)

            def bn_sums(t):
                ins = pe.matmul(psum[6][0:P, 0:D], ONES[0:P, 0:P], tile(KEEP, t), start=isinstance(t, int) and t == 0,
                                stop=isinstance(t, int) and t == T - 1)
                if isinstance(t, int) and t == T - 1:
                    ins.then_inc(bn_sum, 1)
            project("l2out", [WF], bn_sums)

            def bn_squares(t, r, on):
                pe.wait_ge(bn_sq, t + 1)
                ins = pe.matmul(psum[7][0:P, 0:D], ONES[0:P, 0:P], tile(Y, t), start=isinstance(t, int) and t == 0,
                                stop=isinstance(t, int) and t == T - 1)
                if isinstance(t, int) and t == T - 1:
                    ins.then_inc(bn_sqsum, 1)
            turns(pe, T, 2, 2, 0, bn_squares)
            await_tables(pe, 0)
            project("l3in", [W0, WA, WB])
            for s in range(S3):
                q = SCATTERS.index(f"e{s}") * UNITS
                qt = TURNS_BEFORE_E + s * UNITS
                pe.wait_ge(edge_split, s + 1)

                def edge_net(v, r, on):
                    if on(2):
                        o = (r + 2) % RING
                        pe.wait_ge(ohT_ready, qt + v - 1)
                        t = tiles.at(v, r)
                        wait_past(pe, msgs, MSGS_BEFORE_E + s * UNITS + v - 3)
                        for g in range(G):
                            place = psum[2 + o % 2][:, g * D:(g + 1) * D]
                            own_T = ohbT[0:P, o, g * 128:(g + 1) * 128]
                            pe.matmul(place, own_T, BTB[0:P, bass.ds(t * 2 * D, D)], start=True, stop=False)
                            pe.matmul(place, own_T, BTB[0:P, bass.ds(t * 2 * D + D, D)], start=False, stop=False)
                            pe.matmul(place, own_T, KEEPB[:, bass.ds(t * 2 * D, D)], start=False, stop=False)
                            ins = pe.matmul(place, atT[:, o, g * 128:(g + 1) * 128], edge_w, start=False, stop=True)
                        ins.then_inc(mid_ready, 1)
                    if on(1):
                        turn_one_hot(qt, q, v - 1, (r + 7) % OHS, True)
                    if on(6):
                        o = (r + 2) % RING
                        scatter(q, v - 6, o, lambda g: ohw[:, o % 2, g, :], lambda g: msg[:, o, g, 0:D + 2], D + 2,
                                ohw_ready, (s + 1) * UNITS + v - 5)
                tiles = Tiles(mybir.EngineType.PE, DTILE, 2, OHS)
                turns(pe, UNITS, OHS, OHS, 6, edge_net)
                await_nets(pe, s)
                project(f"agg{s}", [WC])
                project(f"mix{s}", [WD])
                project(f"node{s}", [WF])
                if s < S3 - 1:
                    await_tables(pe, s + 1)
                    project(f"next{s}", [W0, WA, WB])


_INS = ["x", "src", "dst", "edge_attr_3", "edge_attr_64", "edge_weight", "L0_gnn_W", "L0_gnn_a_l", "L0_gnn_a_r",
        "L1_gnn_W1", "L1_gnn_b1", "L1_gnn_W2", "L1_gnn_b2", "L2_gnn_W_edge", "L2_gnn_W_rel", "L2_gnn_b_rel",
        "L2_gnn_W_root", "L2_gnn_gamma", "L2_gnn_beta", "L2_gnn_W_res", "L3_gnn_W1e", "L3_gnn_b1e", "L3_gnn_ge",
        "L3_gnn_oe", "L3_gnn_W2e", "L3_gnn_b2e", "L3_gnn_W1n", "L3_gnn_b1n", "L3_gnn_gn", "L3_gnn_on",
        "L3_gnn_W2n", "L3_gnn_b2n"]


def kernel(**inputs):
    import numpy as _np
    import concourse.bacc as _bacc
    from concourse import mybir as _mybir
    from concourse.bass_utils import run_bass_kernel_spmd as _run

    nc = _bacc.Bacc("TRN2", target_bir_lowering=False, num_devices=1)
    arrays, args = {}, []
    for name in _INS:
        a = _np.ascontiguousarray(inputs[name])
        arrays[f"in_{name}"] = a
        args.append(nc.dram_tensor(f"in_{name}", a.shape, _mybir.dt.from_np(a.dtype), kind="ExternalInput").ap())
    args.append(nc.dram_tensor("out_0", (N, D), _mybir.dt.float32, kind="ExternalOutput").ap())
    build(nc, *args)
    r = _run(nc, [arrays], core_ids=[0])
    return r.results[0]["out_0"]
```

```python
from contextlib import ExitStack

import concourse.bass as bass
from concourse import mybir

F32 = mybir.dt.float32
I32 = mybir.dt.int32
BF16 = mybir.dt.bfloat16
ALU = mybir.AluOpType
ACT = mybir.ActivationFunctionType
AX_X = mybir.AxisListType.X

N, D, E = 3125, 256, 50000
P = 125
T = N // P
CT = 5
HEADS = 4
HD = D // HEADS
G = 2
RING = 4
OHS = 2 * RING
CAP = G * 128
MOST = (E + T * (CAP - 1)) // CAP
UNITS = -(-MOST // RING) * RING
BLOCKS = UNITS * G
EC = E // P
HW = 8
EA = 64
AK = 96
REC = HW + EA
CH = 8
AW = D + 4
BIG = 1e30
ALPHA = 0.2
EPS = 1e-5
S3 = 3
FOLDS = S3 + 3 * (S3 - 1)


def turns(eng, total, ring, head, depth, step):
    assert head % ring == 0 and head >= depth
    end = total - total % ring
    for v in range(head):
        step(v, v % ring, lambda lag: v >= lag)
    with eng.Fori(head // ring, end // ring) as lap:
        for r in range(ring):
            step(lap * ring + r, r, lambda lag: True)
    for v in range(end, total + depth):
        step(v, v % ring, lambda lag: 0 <= v - lag < total)


def wait_past(eng, sem, value):
    if isinstance(value, int) and value <= 0:
        return
    eng.wait_ge(sem, value)


class Chain:

    def __init__(self, eng, sem):
        self.eng, self.sem, self.n = eng, sem, 0

    def link(self, ins):
        ins.then_inc(self.sem, 1)
        self.n = self.n + 1
        self.eng.wait_ge(self.sem, self.n)

    def mark(self, ins):
        ins.then_inc(self.sem, 1)
        self.n = self.n + 1
        return self.n

    def await_(self, n):
        self.eng.wait_ge(self.sem, n)

    def at(self, n):
        self.n = n

    def loop(self, end, per, body):
        base, times = self.n, 5 if end % 5 == 0 else 4
        assert end % times == 0
        with self.eng.Fori(0, end // times) as i:
            for k in range(times):
                self.n = base + (i * times + k) * per
                body(i * times + k)
        self.n = base + per * end


def build(nc, x, src, dst, edge_attr_3, edge_attr_64, edge_weight, L0_gnn_W, L0_gnn_a_l, L0_gnn_a_r,
          L1_gnn_W1, L1_gnn_b1, L1_gnn_W2, L1_gnn_b2, L2_gnn_W_edge, L2_gnn_W_rel, L2_gnn_b_rel,
          L2_gnn_W_root, L2_gnn_gamma, L2_gnn_beta, L2_gnn_W_res, L3_gnn_W1e, L3_gnn_b1e, L3_gnn_ge,
          L3_gnn_oe, L3_gnn_W2e, L3_gnn_b2e, L3_gnn_W1n, L3_gnn_b1n, L3_gnn_gn, L3_gnn_on, L3_gnn_W2n,
          L3_gnn_b2n, out):
    by_dst = nc.dram_tensor("by_dst", (128 * BLOCKS, REC), F32, kind="Internal").ap()
    by_src = nc.dram_tensor("by_src", (128 * BLOCKS, 2), F32, kind="Internal").ap()
    rows_h = nc.dram_tensor("rows_h", (N, AW), F32, kind="Internal").ap()
    rows_hr = nc.dram_tensor("rows_hr", (N, HEADS), F32, kind="Internal").ap()
    rows = nc.dram_tensor("rows", (N, D), F32, kind="Internal").ap()
    folded_w = nc.dram_tensor("folded_w", (FOLDS, D, D), F32, kind="Internal").ap()
    folded_b = nc.dram_tensor("folded_b", (FOLDS, D), F32, kind="Internal").ap()

    with ExitStack() as ctx:
        def sb(name, shape, dt=F32):
            return ctx.enter_context(nc.sbuf_tensor(name, shape, dt))

        def sem(name):
            return ctx.enter_context(nc.semaphore(name))

        X = sb("X", [P, T * D])
        KEEP = sb("KEEP", [P, T * D])
        Y = sb("Y", [P, T * D])
        ACC = sb("ACC", [P, T * AW])
        BT = sb("BT", [128, T * D])
        HL = sb("HL", [P, T * HEADS])
        MX = sb("MX", [P, T * HEADS])
        HM = sb("HM", [P, T * 2 * HEADS])
        CNT = sb("CNT", [P, T * 2])
        DINV = sb("DINV", [P, T])
        RDEN = sb("RDEN", [P, T * HEADS])
        MV = sb("MV", [P, T * 2])
        SD = sb("SD", [P, T])
        RS = sb("RS", [P, T])
        ST = sb("ST", [P, 6 * CT])
        AG = sb("AG", [P, 2 * CT])
        EPSC = sb("EPSC", [128, 1])

        DH = sb("DH", [128, BLOCKS * HW])
        SH = sb("SH", [128, BLOCKS * 2])
        DIDX = sb("DIDX", [128, BLOCKS], I32)
        SIDX = sb("SIDX", [128, BLOCKS], I32)
        DTILE = sb("DTILE", [1, UNITS], I32)
        STILE = sb("STILE", [1, UNITS], I32)

        IOTA = sb("IOTA", [128, UNITS])
        IOTAB = sb("IOTAB", [128, 128], BF16)
        IDENT = sb("IDENT", [128, 128])
        IDENTB = sb("IDENTB", [128, 128], BF16)
        ONES = sb("ONES", [128, 128])
        LTRI = sb("LTRI", [128, 128])

        W0 = sb("W0", [128, 2 * D])
        WA = sb("WA", [128, 2 * D])
        WB = sb("WB", [128, 2 * D])
        WC = sb("WC", [128, 2 * D])
        WD = sb("WD", [128, 2 * D])
        WF = sb("WF", [128, 2 * D])
        WE = sb("WE", [128, D])
        BIAS = sb("BIAS", [P, 8 * D])
        ALR = BIAS[:, 0:2 * D]

        gidx = sb("gidx", [128, RING * G], I32)
        gat = sb("gat", [128, RING, G, AW])
        oh = sb("oh", [128, RING, G, 128])
        ohw = sb("ohw", [128, 2, G, P])
        ohT = sb("ohT", [128, RING, G * 128])
        msg = sb("msg", [128, RING, G, AW])
        small = sb("small", [128, 64])
        wide = sb("wide", [P, 4, AW])
        staged = sb("staged", [P, 2, D])
        cand = msg[:, :, :, :].rearrange("p r g c -> p (r g c)")[:, 0:2 * HEADS * G * P].rearrange(
            "p (s h g n) -> p s h g n", s=2, h=HEADS, g=G)
        ohb = oh[:, :, :, :].rearrange("p r g n -> p (r g n)").bitcast(BF16)[:, 0:OHS * G * P].rearrange(
            "p (r g n) -> p r g n", r=OHS, g=G)
        flatT = ohT[:, :, :].rearrange("p r n -> p (r n)").bitcast(BF16)
        ohbT = flatT[:, 0:RING * G * 128].rearrange("p (r n) -> p r n", r=RING)
        atT = flatT[0:AK, RING * G * 128:2 * RING * G * 128].rearrange("p (r n) -> p r n", r=RING)
        free_b = SH[:, :].bitcast(BF16)
        atb = free_b[:, 0:RING * G * AK].rearrange("p (r g n) -> p r g n", r=RING, g=G)
        edge_w = free_b[0:AK, RING * G * AK:RING * G * AK + D]
        BTB, KEEPB = BT[:, :].bitcast(BF16), KEEP[:, :].bitcast(BF16)
        edge_in = WE[0:AK, :]
        HMB = staged[:, :, :].rearrange("p s n -> p (s n)").bitcast(BF16)[:, 0:T * 6 * HEADS]
        hT = ohT[:, 0:2, 0:2 * P]

        psum = [ctx.enter_context(nc.psum_tensor(f"ps{k}", [128, 512], F32)) for k in range(8)]
        psum_b = [psum[k][:, :].bitcast(BF16) for k in range(2)]

        key_of = {"dst": Y[:, 0:EC], "src": Y[:, EC:2 * EC]}
        bucket = Y[:, 2 * EC:3 * EC]
        rank = Y[:, 3 * EC:4 * EC]
        mask = Y[:, 4 * EC:5 * EC]
        prefix = Y[:, 5 * EC:6 * EC]
        ones_row = Y[:, 6 * EC:7 * EC]
        raw = {"dst": Y[:, 7 * EC:8 * EC].bitcast(I32), "src": Y[:, 8 * EC:9 * EC].bitcast(I32)}
        weight_in = Y[:, 9 * EC:10 * EC]
        attr_in = Y[:, 10 * EC:13 * EC]
        place_i = Y[:, 13 * EC:14 * EC].bitcast(I32)
        place_j = Y[:, 14 * EC:15 * EC].bitcast(I32)
        header = BT[0:P, 0:HW * EC]
        pair = BT[0:P, HW * EC:(HW + 2) * EC]
        place_of = {"dst": BT[0:P, 10 * EC:11 * EC].bitcast(I32), "src": BT[0:P, 11 * EC:12 * EC].bitcast(I32)}
        record = BT[0:P, 12 * EC:12 * EC + 2 * CH * REC].rearrange("p (s j c) -> p s j c", s=2, c=REC)
        AT = 12 * EC + 2 * CH * REC
        place_now = BT[0:P, AT:AT + 2 * CH].bitcast(I32)
        AT += 2 * CH
        pair_now = BT[0:P, AT:AT + 4 * CH].rearrange("p (s j c) -> p s j c", s=2, c=2)
        AT += 4 * CH
        threshold = BT[:, AT:AT + T]
        count = sb("count", [P, T])
        units_i = BT[:, AT + T:AT + 2 * T].bitcast(I32)
        units = BT[:, AT + 2 * T:AT + 3 * T]
        unit_end = BT[:, AT + 3 * T:AT + 4 * T]
        unit_start = BT[:, AT + 4 * T:AT + 5 * T]
        base = sb("base", [P, T])
        tile_f = Y[0:1, 15 * EC:15 * EC + UNITS]

        inputs_in = sem("inputs_in")
        consts = sem("consts")
        counted = sem("counted")
        prefixed = sem("prefixed")
        blanked = sem("blanked")
        blank_out = sem("blank_out")
        placed = sem("placed")
        attr_landed = [sem(f"attr_landed{r}") for r in range(2)]
        scattered = [sem(f"scattered{r}") for r in range(2)]
        pairs_out = [sem(f"pairs_out{r}") for r in range(2)]
        turn_ready = sem("turn_ready")
        apart = sem("apart")
        lists_in = {"dst": sem("dst_list_in"), "src": sem("src_list_in")}
        lists_ready = {"dst": sem("dst_list_ready"), "src": sem("src_list_ready")}
        weights_in = sem("weights_in")
        chain_a = sem("chain_a")
        chain_b = sem("chain_b")
        chain_u = sem("chain_u")
        accs_clear = sem("accs_clear")
        moments = sem("moments")
        rooted = sem("rooted")
        made = sem("made")
        staged_in = sem("staged_in")
        turned = sem("turned")
        turned_in = sem("turned_in")
        projected = sem("projected")
        drawn = sem("drawn")
        rows_out = [sem(f"rows_out{r}") for r in range(2)]
        gidx_ready = sem("gidx_ready")
        landed = [sem(f"landed{r}") for r in range(RING)]
        oh_ready = sem("oh_ready")
        part_ready = sem("part_ready")
        acc_done = sem("acc_done")
        max_oh = sem("max_oh")
        max_neg = sem("max_neg")
        max_rows = sem("max_rows")
        max_done = sem("max_done")
        oh_turned = sem("oh_turned")
        ohT_ready = sem("ohT_ready")
        mid_ready = sem("mid_ready")
        scores = sem("scores")
        probs = sem("probs")
        msgs = sem("msgs")
        msg_relu = sem("msg_relu")
        msg_stats = sem("msg_stats")
        msg_sd = sem("msg_sd")
        attrs_in = [sem(f"attrs_in{r}") for r in range(RING)]
        bn_sum = sem("bn_sum")
        bn_sq = sem("bn_sq")
        bn_sqsum = sem("bn_sqsum")
        hm_ready = sem("hm_ready")
        recip = sem("recip")
        ohw_ready = sem("ohw_ready")
        finished = sem("finished")
        out_done = sem("out_done")

        PHASES = ["l0", "l1a", "l1b", "l2in", "l2out", "l3in"]
        for s in range(S3):
            PHASES += [f"mix{s}", f"next{s}"]
        MAKES = [p for p in PHASES if p != "l2out"]
        ROWS = ["l0", "l0", "l1a", "l1b", "l2in", "l3in", "next0", "next1"]
        SCATTERS = ["deg", "l0", "l1a", "l1b", "l2", "e0", "e1", "e2"]
        GATHERS = ["max", "l0", "l1a", "l1b", "l2", "e0", "e1", "e2"]

        def laps(v, r, ring):
            return v // ring if isinstance(v, int) else (v - r) // ring

        def landings(name, v, r):
            return 16 * G * (UNITS // RING * GATHERS.index(name) + 1) + (v - r) * (16 * G // RING)

        class Tiles:

            def __init__(self, engine, table, lag, ring):
                self.engine, self.table, self.lag, self.ring = engine, table, lag, ring

            def load(self, first, n):
                return nc.values_load_multi_w_load_instructions(
                    self.table[0:1, bass.ds(first, n)], engines=[self.engine], min_val=0, max_val=T - 1,
                    skip_runtime_bounds_check_because="the table counts passed thresholds, of which there are T - 1")[1]

            def at(self, v, r):
                if isinstance(v, int):
                    return self.load(v - self.lag, 1)[0]
                if r == 0:
                    self.lap = self.load(v - self.lag, self.ring)
                return self.lap[r]

        def row_dmas(names, r):
            return 16 * names * ((T + 1 - r) // 2)

        def await_rows(eng, phase):
            k = len(ROWS) - 1 - ROWS[::-1].index(phase) + 1
            for r in range(2):
                eng.wait_ge(rows_out[r], row_dmas(k, r))

        def tile(A, t, lo=0, hi=None, w=D):
            return A[:, bass.ds(t * w + lo, (w if hi is None else hi) - lo)]

        def Wc(W, c):
            return W[:, c * D:(c + 1) * D]

        def bias(k):
            return BIAS[:, k * D:(k + 1) * D]

        def hold(eng, s, value):
            wait_past(eng, s, value)
            eng.sem_inc(apart, 1)

        def attr_slot(r):
            return ohT[:, r, 128:128 + G * EA]

        USERS = {"max": (max_neg, 0), "l0": (msgs, 0), "l1a": (part_ready, 2 * UNITS),
                 "l1b": (part_ready, 3 * UNITS), "l2": (msgs, UNITS)}
        USERS.update({f"e{s}": (msgs, (2 + s) * UNITS) for s in range(S3)})
        TURNS_BEFORE_E = MSGS_BEFORE_E = 2 * UNITS
        LAST = 2
        ROWS_TOTAL = [row_dmas(len(ROWS), r) for r in range(2)]

        block = ctx.enter_context(nc.Block())

        def kcn(W):
            return W.rearrange("(c k) n -> k c n", k=128)

        def two(W):
            return W[:, :].rearrange("p (c n) -> p c n", c=2)

        def two_of(V):
            return V.rearrange("p (c n) -> p c n", c=2)

        def row(v):
            return v.partition_broadcast(P)

        INIT = [(two(W0), kcn(L0_gnn_W)), (two(WA), kcn(L1_gnn_W1)), (two(WB), kcn(L1_gnn_W2)),
                (two(WC), kcn(L2_gnn_W_root)), (two(WD), kcn(L2_gnn_W_res)), (two(WF), kcn(L2_gnn_W_rel)),
                (WE[0:EA, :], L2_gnn_W_edge), (WE[EA:2 * EA, :], L2_gnn_W_edge),
                (ALR[:, 0:D], row(L0_gnn_a_l.rearrange("a h f -> (a h f)"))),
                (ALR[:, D:2 * D], row(L0_gnn_a_r.rearrange("a h f -> (a h f)"))),
                (bias(2), row(L1_gnn_b1)), (bias(3), row(L1_gnn_b2)), (bias(4), row(L2_gnn_b_rel)),
                (bias(5), row(L2_gnn_gamma)), (bias(6), row(L2_gnn_beta))]

        def column(v):
            return v.rearrange("(c k) -> k c", k=128)

        FOLDED = []
        for s in range(S3):
            FOLDED.append((L3_gnn_W2e[s], L3_gnn_ge[s, :], L3_gnn_oe[s, :], L3_gnn_b2e[s, :],
                           [(L3_gnn_W1n[s, D:2 * D, :], None, s)]))
        for s in range(S3 - 1):
            FOLDED.append((L3_gnn_W2n[s], L3_gnn_gn[s, :], L3_gnn_on[s, :], L3_gnn_b2n[s, :],
                           [(L3_gnn_W1e[s + 1, 3:3 + D, :], None, S3 + 3 * s),
                            (L3_gnn_W1e[s + 1, 3 + D:3 + 2 * D, :], L3_gnn_b1e[s + 1:s + 2, :], S3 + 3 * s + 1),
                            (L3_gnn_W1n[s + 1, 0:D, :], L3_gnn_b1n[s + 1:s + 2, :], S3 + 3 * s + 2)]))
        gat_flat = gat[:, :, :, :].rearrange("p r g c -> p (r g c)")
        fold_A, fold_AT, fold_B, fold_F = (gat_flat[:, k * 2 * D:(k + 1) * 2 * D] for k in range(4))
        fold_gain, fold_offset, fold_bias, fold_mid = (gat_flat[:, 8 * D + 2 * k:8 * D + 2 * k + 2] for k in range(4))
        fold_row, fold_rowB = wide[0:1, 2, 0:D], wide[0:1, 3, 0:D]

        def table_loads(s):
            if s:
                k = S3 + 3 * (s - 1)
                return [(two(W), kcn(folded_w[k + j])) for j, W in enumerate((W0, WA, WB))] + [
                    (bias(b), row(folded_b[k + j, :])) for j, b in enumerate((7, 0, 1))]
            return [(two(W0), kcn(L3_gnn_W1e[s, 3:3 + D, :])), (two(WA), kcn(L3_gnn_W1e[s, 3 + D:3 + 2 * D, :])),
                    (two(WB), kcn(L3_gnn_W1n[s, 0:D, :])), (bias(0), row(L3_gnn_b1e[s, :])),
                    (bias(1), row(L3_gnn_b1n[s, :]))]

        def net_loads(s):
            mix = [(two(WD), kcn(folded_w[s])), (bias(4), row(folded_b[s, :]))]
            return mix if s < S3 - 1 else mix + [
                (two(WF), kcn(L3_gnn_W2n[s])), (bias(5), row(L3_gnn_gn[s, :])),
                (bias(6), row(L3_gnn_on[s, :])), (bias(7), row(L3_gnn_b2n[s, :]))]

        def await_init(eng):
            eng.wait_ge(weights_in, 16 * len(INIT))

        def await_tables(eng, s):
            eng.wait_ge(tables_in, 16 * sum(len(table_loads(k)) for k in range(s + 1)))

        def await_nets(eng, s):
            eng.wait_ge(nets_in, 16 * sum(len(net_loads(k)) for k in range(s + 1)))

        fold_A_in = sem("fold_A_in")
        fold_B_in = sem("fold_B_in")
        fold_scaled = sem("fold_scaled")
        fold_turned = sem("fold_turned")
        fold_turned_in = sem("fold_turned_in")
        fold_done = sem("fold_done")
        fold_drawn = sem("fold_drawn")
        fold_out = sem("fold_out")
        edge_clear = sem("edge_clear")
        edge_split = sem("edge_split")
        edge_rows_in = sem("edge_rows_in")
        tables_in = sem("tables_in")
        nets_in = sem("nets_in")

        @block.sync
        def _(sp):
            def load(out_, in_, s):
                sp.dma_start(out_, in_).then_inc(s, 16)

            load(raw["dst"], dst.rearrange("(p j) -> p j", p=P), inputs_in)
            load(raw["src"], src.rearrange("(p j) -> p j", p=P), inputs_in)
            load(weight_in, edge_weight.rearrange("(p j) -> p j", p=P), inputs_in)
            load(attr_in, edge_attr_3.rearrange("(p j) c -> p (j c)", p=P), inputs_in)
            load(X[:, :].rearrange("p (t n) -> p t n", t=T), x.rearrange("(t p) n -> p t n", p=P), inputs_in)
            for a, b in INIT:
                load(a, b, weights_in)
            sp.wait_ge(blanked, 4)
            nb = 22
            for k in range(BLOCKS // nb):
                load(by_dst.rearrange("(p b) c -> p (b c)", p=128)[:, k * nb * REC:(k + 1) * nb * REC],
                     msg[:, :, :, :].rearrange("p r g c -> p (r g c)")[:, 0:nb * REC], blank_out)
            load(by_src.rearrange("(p b) c -> p (b c)", p=128), SH[:, :], blank_out)

            def attrs(v, r, on):
                wait_past(sp, scattered[r], laps(v, r, 2) * 16 * CH)
                sp.dma_start(record[:, r, :, HW:REC],
                             edge_attr_64.rearrange("(p j) c -> p j c", p=P)[:, bass.ds(v * CH, CH), :]
                             ).then_inc(attr_landed[r], 16)
            turns(sp, EC // CH, 2, 2, 0, attrs)
            for r in range(2):
                sp.wait_ge(scattered[r], EC // CH // 2 * 16 * CH)
            load(DH[:, :].rearrange("p (b c) -> p b c", c=HW),
                 by_dst.rearrange("(p b) c -> p b c", p=128)[:, :, 0:HW], lists_in["dst"])
            for r in range(2):
                sp.wait_ge(pairs_out[r], EC // CH // 2 * 16 * CH)
            load(SH[:, :], by_src.rearrange("(p b) c -> p (b c)", p=128), lists_in["src"])
            sp.wait_ge(lists_ready["src"], 1)
            def load_edge_rows(s):
                sp.wait_ge(edge_clear, s + 1)
                for k in range(9):
                    at = k // 3 * 32 + k % 3 * 3
                    load(edge_in[at:at + 3, :], L3_gnn_W1e[s, 0:3, :], edge_rows_in)

            sp.wait_ge(projected, T * (PHASES.index("l1b") + 1))
            for a, b in table_loads(0):
                load(a, b, tables_in)

            def unit_attrs(v, r, on):
                if not isinstance(v, int) or v >= RING:
                    sp.wait_ge(oh_turned, UNITS + v - RING + 1)
                sp.dma_start(attr_slot(r).rearrange("p (g c) -> p g c", g=G), by_dst.rearrange("(p b) c -> p b c", p=128)
                             [:, bass.ds(v * G, G), HW:REC]).then_inc(attrs_in[r], 16)
            sp.wait_ge(projected, T * (PHASES.index("l2in") + 1))
            turns(sp, UNITS, RING, RING, 0, unit_attrs)
            for s in range(S3):
                sp.wait_ge(fold_out, 32 * FOLDS)
                if s == 0:
                    sp.wait_ge(finished, 1)
                    load_edge_rows(0)
                else:
                    sp.wait_ge(drawn, T * (PHASES.index(f"next{s - 1}") + 1))
                for a, b in net_loads(s):
                    load(a, b, nets_in)
                if s < S3 - 1:
                    sp.wait_ge(acc_done, UNITS * (SCATTERS.index(f"e{s}") + 1))
                    load_edge_rows(s + 1)
                    for a, b in table_loads(s + 1):
                        load(a, b, tables_in)
            sp.wait_ge(finished, LAST)
            sp.dma_start(out.rearrange("(t p) n -> p t n", p=P),
                         X[:, :].rearrange("p (t n) -> p t n", t=T)).then_inc(out_done, 16)
            sp.wait_ge(out_done, 16)
            for r in range(2):
                sp.wait_ge(rows_out[r], ROWS_TOTAL[r])

        @block.gpsimd
        def _(pool):
            pool.iota(IOTA[:, :], pattern=[[1, UNITS]], base=0, channel_multiplier=0,
                      allow_small_or_imprecise_dtypes=True).then_inc(consts, 1)
            pool.iota(IOTAB[:, :], pattern=[[1, 128]], base=0, channel_multiplier=0,
                      allow_small_or_imprecise_dtypes=True).then_inc(consts, 1)
            pool.memset(ONES[:, :], 1.0).then_inc(consts, 1)
            pool.memset(IDENT[:, :], 0.0).then_inc(consts, 1)
            pool.memset(EPSC[:, :], EPS).then_inc(consts, 1)
            pool.memset(IDENTB[:, :], 0.0).then_inc(consts, 1)
            pool.wait_ge(consts, 6)
            pool.affine_select(out=IDENTB[:, :], in_=IDENTB[:, :], compare_op=ALU.not_equal, fill=1.0, base=0,
                               pattern=[[-1, 128]], channel_multiplier=1).then_inc(consts, 1)
            pool.affine_select(out=IDENT[:, :], in_=IDENT[:, :], compare_op=ALU.not_equal, fill=1.0, base=0,
                               pattern=[[-1, 128]], channel_multiplier=1).then_inc(consts, 1)
            pool.affine_select(out=LTRI[:, :], in_=ONES[:, :], compare_op=ALU.is_ge, fill=0.0, base=-1,
                               pattern=[[1, 128]], channel_multiplier=-1).then_inc(consts, 1)

            def copies_done(n):
                pool.wait_ge(turn_ready, n)
                pool.sem_inc(apart, 1)

            pool.wait_ge(placed, 1)
            pool.wait_ge(blank_out, 16 * (BLOCKS // 22 + 1))

            def to_dst(v, r, on):
                if not isinstance(v, int) or v >= 2:
                    pool.wait_ge(scattered[r], laps(v, r, 2) * 16 * CH)
                pool.wait_ge(attr_landed[r], (laps(v, r, 2) + 1) * 16)
                pool.sem_inc(apart, 1)
                pool.tensor_copy(record[:, r, :, 0:HW], header[:, bass.ds(v * CH * HW, CH * HW)]
                                 .rearrange("p (j c) -> p j c", c=HW)).then_inc(turn_ready, 1)
                pool.tensor_copy(place_now[:, r * CH:(r + 1) * CH], place_of["dst"][:, bass.ds(v * CH, CH)]
                                 ).then_inc(turn_ready, 1)
                copies_done((v + 1) * 2)
                for j in range(CH):
                    pool.indirect_dma_start(
                        by_dst, bass.IndirectOffsetOnAxis(ap=place_now[:, r * CH + j:r * CH + j + 1], axis=0),
                        record[:, r, j, :], None).then_inc(scattered[r], 16)
            turns(pool, EC // CH, 2, 2, 0, to_dst)
            for r in range(2):
                pool.wait_ge(scattered[r], EC // CH // 2 * 16 * CH)
            pool.wait_ge(placed, 2)

            def to_src(v, r, on):
                wait_past(pool, pairs_out[r], laps(v, r, 2) * 16 * CH)
                pool.sem_inc(apart, 1)
                pool.tensor_copy(pair_now[:, r, :, :], pair[:, bass.ds(v * CH * 2, CH * 2)]
                                 .rearrange("p (j c) -> p j c", c=2)).then_inc(turn_ready, 1)
                pool.tensor_copy(place_now[:, r * CH:(r + 1) * CH], place_of["src"][:, bass.ds(v * CH, CH)]
                                 ).then_inc(turn_ready, 1)
                copies_done(EC // CH * 2 + (v + 1) * 2)
                for j in range(CH):
                    pool.indirect_dma_start(
                        by_src, bass.IndirectOffsetOnAxis(ap=place_now[:, r * CH + j:r * CH + j + 1], axis=0),
                        pair_now[:, r, j, :], None).then_inc(pairs_out[r], 16)
            turns(pool, EC // CH, 2, 2, 0, to_src)

            def gather(name, table, width, index):
                q = GATHERS.index(name)
                used, before = USERS[name]
                if q:
                    last, n = USERS[GATHERS[q - 1]]
                    pool.wait_ge(last, n + UNITS)

                def unit(v, r, on):
                    if not isinstance(v, int) or v >= RING:
                        pool.wait_ge(used, before + v - RING + 1)
                    if r % 2 == 0:
                        for k in range(2):
                            wait_past(pool, landed[r + k], (q * (UNITS // RING) + laps(v, r, RING)) * 16 * G)
                        pool.sem_inc(apart, 1)
                        pool.tensor_copy(gidx[:, r * G:(r + 2) * G], index[:, bass.ds(v * G, 2 * G)]
                                         ).then_inc(gidx_ready, 2)
                        pool.wait_ge(gidx_ready, q * UNITS + v + 2)
                    pool.sem_inc(apart, 1)
                    for g in range(G):
                        pool.indirect_dma_start(
                            gat[:, r, g, AW - width:AW] if width == HEADS else gat[:, r, g, 0:width], None, table,
                            bass.IndirectOffsetOnAxis(ap=gidx[:, r * G + g:r * G + g + 1], axis=0)
                            ).then_inc(landed[r], 16)
                turns(pool, UNITS, RING, RING, 0, unit)

            pool.wait_ge(lists_ready["src"], 1)
            await_rows(pool, "l0")
            pool.wait_ge(fold_out, 32 * FOLDS)
            gather("max", rows_hr, HEADS, SIDX)
            gather("l0", rows_h, AW, SIDX)
            for name in ("l1a", "l1b"):
                await_rows(pool, name)
                gather(name, rows, D, DIDX)
            await_rows(pool, "l2in")
            gather("l2", rows, D, DIDX)
            for s in range(S3):
                await_rows(pool, "l3in" if s == 0 else f"next{s - 1}")
                gather(f"e{s}", rows, D, DIDX)

        @block.scalar
        def _(act):
            def roots(k):
                act.wait_ge(moments, k)
                act.activation(SD[:, :], MV[:, :].rearrange("p (t c) -> p t c", c=2)[:, :, 1], ACT.Sqrt,
                               bias=EPSC[0:P, :]).then_inc(rooted, 1)

            def project(name, A=KEEP, w=D, func=ACT.Copy, row_source=None):
                k = PHASES.index(name) * T
                km = MAKES.index(name) * T if name in MAKES else 0

                def step(t, r, on):
                    if on(1):
                        o = (r + 1) % 2
                        act.wait_ge(turned, k + t)
                        wait_past(act, projected, k + t - 2)
                        act.activation(hT[:, o, :], psum[o][:, 0:2 * P], ACT.Copy).then_inc(turned_in, 1)
                    if on(0):
                        if name in MAKES:
                            act.wait_ge(made, km + t + 1)
                        hold(act, turned, k + t - 1)
                        act.activation(staged[:, r, :], tile(A, t, 0, D, w), func).then_inc(staged_in, 1)
                    if row_source is not None and on(3):
                        act.wait_ge(drawn, k + t - 2)
                        row_source(t - 3, (r + 1) % 2)
                turns(act, T, 2, 4, 3, step)

            def rows_from(A, w=D):
                def go(t, r):
                    act.dma_start(rows[bass.ds(t * P, P), :], tile(A, t, 0, D, w)).then_inc(rows_out[r], 16)
                return go

            def rows_h_from(t, r):
                act.dma_start(rows_h[bass.ds(t * P, P), :], wide[:, r, :]).then_inc(rows_out[r], 16)
                act.dma_start(rows_hr[bass.ds(t * P, P), :], wide[:, r, D:AW]).then_inc(rows_out[r], 16)

            def rows_staged(t, r):
                act.dma_start(rows[bass.ds(t * P, P), :], wide[:, r, 0:D]).then_inc(rows_out[r], 16)

            act.wait_ge(consts, 9)
            roots(1)
            project("l0", func=ACT.Relu, row_source=rows_h_from)

            n = 0
            await_rows(act, "l0")
            for A, gain, offset, b, products in FOLDED:
                wait_past(act, fold_drawn, n)
                act.dma_start(two_of(fold_A), kcn(A)).then_inc(fold_A_in, 16)
                for out_, in_ in ((fold_gain, column(gain)), (fold_offset, column(offset)), (fold_bias, column(b))):
                    act.dma_start(out_, in_, allow_slow_non_contiguous=True).then_inc(fold_A_in, 16)
                for B, b1, k in products:
                    wait_past(act, fold_drawn, n)
                    act.dma_start(two_of(fold_B), kcn(B)).then_inc(fold_B_in, 16)
                    if b1 is not None:
                        act.dma_start(fold_rowB, b1).then_inc(fold_B_in, 16)
                    n = n + 1
                    act.wait_ge(fold_drawn, n)
                    act.dma_start(kcn(folded_w[k]), two_of(fold_F)).then_inc(fold_out, 16)
                    act.dma_start(folded_b[k:k + 1, :], fold_row).then_inc(fold_out, 16)

            def candidates(v, r, on):
                act.wait_ge(max_oh, v + 1)
                act.wait_ge(landed[r], (laps(v, r, RING) + 1) * 16 * G)
                wait_past(act, max_rows, v - 1)
                for h in range(HEADS):
                    for g in range(G):
                        ins = act.activation(cand[:, r % 2, h, g, :], oh[:, r, g, 0:P], ACT.Identity,
                                             bias=gat[:, r, g, D + h:D + h + 1])
                ins.then_inc(max_neg, 1)
            turns(act, UNITS, RING, RING, 0, candidates)

            def attend(v, r, on):
                if on(1):
                    o = (r + 3) % RING
                    act.wait_ge(oh_turned, v)
                    act.activation(ohbT[0:P, o, :], psum_b[o % 2][0:P, 0:G * 128], ACT.Copy).then_inc(ohT_ready, 1)
                if on(3):
                    o = (r + 1) % RING
                    act.wait_ge(scores, v - 2)
                    act.activation(msg[:, o, :, D:AW], small[:, o * 8:o * 8 + 8].rearrange("p (g h) -> p g h", g=G),
                                   ACT.Exp).then_inc(probs, 1)
                if on(4):
                    wait_past(act, part_ready, UNITS + v - 5)
                    act.activation(ohw[:, r % 2, :, :], ohb[:, (r + 4) % OHS, :, :], ACT.Copy).then_inc(ohw_ready, 1)
            turns(act, UNITS, OHS, OHS, 4, attend)
            act.wait_ge(hm_ready, 2)
            act.activation(DINV[:, :], CNT[:, :].rearrange("p (t c) -> p t c", c=2)[:, :, 0], ACT.Sqrt
                           ).then_inc(rooted, 1)
            roots(2)
            project("l1a", func=ACT.Relu, row_source=rows_from(Y))
            project("l1b", row_source=rows_from(Y))
            roots(3)
            project("l2in", func=ACT.Relu, row_source=rows_from(KEEP))

            def attrs_in_sbuf(v, r, on):
                act.wait_ge(oh_turned, UNITS + v + 1)
                act.activation(ohT[:, r, 0:128], psum[r % 2][:, 0:128], ACT.Copy).then_inc(ohT_ready, 1)
            turns(act, UNITS, RING, RING, 0, attrs_in_sbuf)
            act.wait_ge(acc_done, UNITS * (SCATTERS.index("l2") + 1))
            project("l2out", ACC, AW)
            act.wait_ge(bn_sqsum, 2)
            act.activation(wide[:, 1, 0:D], wide[:, 1, 0:D], ACT.Sqrt, bias=EPSC[0:P, :]).then_inc(rooted, 1)
            roots(4)
            project("l3in", func=ACT.Relu, row_source=rows_staged)
            for s in range(S3):
                q = TURNS_BEFORE_E + s * UNITS

                def edge_net(v, r, on):
                    if on(1):
                        o = (r + 3) % RING
                        act.wait_ge(oh_turned, q + v)
                        act.activation(ohbT[0:P, o, :], psum_b[o % 2][0:P, 0:G * 128], ACT.Copy)
                        act.activation(atT[:, o, :], psum_b[o % 2][0:AK, G * 128:2 * G * 128], ACT.Copy
                                       ).then_inc(ohT_ready, 1)
                    if on(5):
                        o = (r + 3) % RING
                        act.wait_ge(recip, s * UNITS + v - 4)
                        wait_past(act, part_ready, SCATTERS.index(f"e{s}") * UNITS + v - 6)
                        for g in range(G):
                            ins = act.activation(ohw[:, o % 2, g, :], ohb[:, (r + 3) % OHS, g, :], ACT.Copy,
                                                 scale=small[:, 8 + o * 2 + g:9 + o * 2 + g])
                        ins.then_inc(ohw_ready, 1)
                    if on(3):
                        o = (r + 1) % RING
                        act.wait_ge(msgs, MSGS_BEFORE_E + s * UNITS + v - 2)
                        act.activation(msg[:, o, :, 0:D], msg[:, o, :, 0:D], ACT.Relu).then_inc(msg_relu, 1)
                    if on(4):
                        o = r % RING
                        act.wait_ge(msg_stats, (s * UNITS + v - 3) * 2)
                        act.activation(small[:, o * 2:o * 2 + 2], msg[:, o, :, D + 1], ACT.Sqrt,
                                       bias=EPSC[:, :]).then_inc(msg_sd, 1)
                turns(act, UNITS, OHS, OHS, 5, edge_net)
                project(f"mix{s}")
                roots(5 + s)
                project(f"next{s}", row_source=rows_staged if s < S3 - 1 else None)

        @block.vector
        def _(dve):
            ca, cb, cu = Chain(dve, chain_a), Chain(dve, chain_b), Chain(dve, chain_u)
            link = ca.link

            flat = msg[:, :, :, :].rearrange("p r g c -> p (r g c)")
            dve.memset(flat, 0.0).then_inc(blanked, 1)
            dve.memset(SH[:, :], 0.0).then_inc(blanked, 1)
            dve.wait_ge(blanked, 2)
            dve.memset(flat[:, 0:22 * REC].rearrange("p (j c) -> p j c", c=REC)[:, :, 0], -1.0).then_inc(blanked, 1)
            dve.memset(SH[:, :].rearrange("p (j c) -> p j c", c=2)[:, :, 0], -1.0).then_inc(blanked, 1)

            dve.wait_ge(inputs_in, 16 * 5)
            dve.wait_ge(consts, 9)
            head = header.rearrange("p (j c) -> p j c", c=HW)
            two_ = pair.rearrange("p (j c) -> p j c", c=2)
            link(dve.tensor_scalar(threshold[:, :], IOTA[:, 0:T], float(P), None, ALU.mult))
            link(dve.memset(ones_row, 1.0))
            link(dve.memset(header, 0.0))
            for name in ("dst", "src"):
                link(dve.tensor_copy(key_of[name], raw[name]))
            link(dve.tensor_copy(head[:, :, 1], key_of["src"]))
            link(dve.tensor_copy(head[:, :, 2], weight_in))
            link(dve.tensor_copy(head[:, :, 3], ones_row))
            link(dve.tensor_copy(head[:, :, 4:7], attr_in.rearrange("p (j c) -> p j c", c=3)))
            link(dve.tensor_copy(two_[:, :, 1], key_of["dst"]))

            for which, name in enumerate(("dst", "src")):
                key = key_of[name]
                local = head[:, :, 0] if name == "dst" else two_[:, :, 0]
                link(dve.memset(bucket, 0.0))
                link(dve.memset(rank, 0.0))
                ca.loop(T - 1, 1, lambda t: ca.link(dve.scalar_tensor_tensor(
                    bucket, key, threshold[0:P, bass.ds(t + 1, 1)], bucket, ALU.is_ge, ALU.add)))
                link(dve.scalar_tensor_tensor(local, bucket, -float(P), key, ALU.mult, ALU.add))

                def ranks(t):
                    ca.link(dve.tensor_scalar(mask, bucket, IOTA[0:P, bass.ds(t, 1)], None, ALU.is_equal))
                    ca.link(dve.tensor_tensor_scan(prefix, ones_row, mask, 0.0, ALU.mult, ALU.add))
                    dve.sem_inc(apart, 1)
                    ca.link(dve.tensor_copy(count[:, bass.ds(t, 1)], prefix[:, EC - 1:EC]))
                    ca.link(dve.tensor_tensor(mask, mask, prefix, ALU.mult))
                    ca.link(dve.tensor_tensor(rank, rank, mask, ALU.add))
                ca.loop(T, 5, ranks)
                dve.sem_inc(counted, 1)
                dve.wait_ge(prefixed, which + 1)
                total, below = psum[2][:, 0:T], psum[3][0:P, 0:T]
                link(dve.tensor_scalar(units_i[:, :], total, float(CAP - 1), None, ALU.add))
                link(dve.tensor_scalar(units_i[:, :], units_i[:, :], CAP.bit_length() - 1, None, ALU.logical_shift_right))
                link(dve.tensor_copy(units[:, :], units_i[:, :]))
                link(dve.tensor_tensor_scan(unit_end[:, :], ONES[:, 0:T], units[:, :], 0.0, ALU.mult, ALU.add))
                link(dve.tensor_tensor(unit_start[:, :], unit_end[:, :], units[:, :], ALU.subtract))
                link(dve.scalar_tensor_tensor(base[:, :], unit_start[0:P, :], float(CAP), below, ALU.mult, ALU.add))
                link(dve.tensor_scalar(base[:, :], base[:, :], -1.0, None, ALU.add))

                def places(t):
                    ca.link(dve.tensor_scalar(mask, bucket, IOTA[0:P, bass.ds(t, 1)], base[:, bass.ds(t, 1)],
                                              ALU.is_equal, ALU.mult))
                    ca.link(dve.tensor_tensor(rank, rank, mask, ALU.add))
                ca.loop(T, 2, places)
                link(dve.tensor_copy(place_i, rank))
                link(dve.tensor_scalar(place_j, place_i, 7, None, ALU.logical_shift_right))
                link(dve.tensor_scalar(place_i, place_i, 127, None, ALU.bitwise_and))
                dve.scalar_tensor_tensor(place_of[name], place_i, float(BLOCKS), place_j, ALU.mult,
                                         ALU.add).then_inc(placed, 1)
                link(dve.memset(tile_f[:, :], 0.0))
                ca.loop(T - 1, 1, lambda t: ca.link(dve.scalar_tensor_tensor(
                    tile_f[:, :], IOTA[0:1, 0:UNITS], unit_start[0:1, bass.ds(t + 1, 1)], tile_f[:, :],
                    ALU.is_ge, ALU.add)))
                link(dve.tensor_copy((DTILE if name == "dst" else STILE)[:, :], tile_f[:, :]))

            def mv(t, c):
                return MV[:, bass.ds(t * 2 + c, 1)]

            def stats(A, i):
                t = i * CT
                dve.sem_inc(apart, 1)
                for k in range(CT):
                    ins = dve.bn_stats(ST[:, 6 * k:6 * k + 6], tile(A, t + k))
                ca.link(ins)
                dve.sem_inc(apart, 1)
                for k in range(CT):
                    ins = dve.bn_aggr(AG[:, 2 * k:2 * k + 2], ST[:, 6 * k:6 * k + 6])
                ca.link(ins)
                ca.link(dve.tensor_scalar(MV[:, bass.ds(t * 2, 2 * CT)], AG[:, :], 1.0, None, ALU.mult))

            def chunk(A, i, w=D):
                return A[:, bass.ds(i * (CT * w), CT * w)].rearrange("p (t c) -> p t c", t=CT)[:, :, 0:D]

            def over_tiles(V):
                return V.unsqueeze(1).broadcast_to([P, CT, D])

            def chunks(per, body):
                base = ca.n
                with dve.Fori(0, T // CT) as i:
                    ca.at(base + i * per)
                    body(i)
                ca.at(base + per * (T // CT))

            def rstd(k):
                dve.wait_ge(rooted, k)
                link(dve.reciprocal(RS[:, :], SD[:, :]))

            def normalize(A, t):
                return dve.tensor_scalar(tile(KEEP, t), tile(A, t), mv(t, 0), RS[:, bass.ds(t, 1)],
                                         ALU.subtract, ALU.mult)

            def project(name, make, per_make, draw, per_draw, before=None):
                k = PHASES.index(name) * T
                a0, b0 = ca.n, cb.n

                def step(t, r, on):
                    if make is not None and on(0):
                        ca.at(a0 + t * per_make)
                        make(t).then_inc(made, 1)
                    if on(3):
                        o = (r + 1) % 2
                        dve.wait_ge(projected, k + t - 2)
                        if before is not None:
                            b, per = before
                            wait_past(dve, rows_out[o], row_dmas(b, o) + 16 * per * laps(t - 3, o, 2))
                        wait_past(dve, drawn, k + t - 3)
                        dve.sem_inc(apart, 1)
                        cb.at(b0 + (t - 3) * per_draw)
                        draw(t - 3, o).then_inc(drawn, 1)
                turns(dve, T, 2, 4, 3, step)
                ca.at(a0 + T * per_make if make is not None else a0)
                cb.at(b0 + T * per_draw)

            def product(r, j):
                return (psum[2 + r][0:P, (j % 2) * D:(j % 2 + 1) * D] if j < 2 else psum[4 + r][0:P, 0:D])

            chunks(3, lambda i: stats(X, i))
            dve.sem_inc(moments, 1)
            rstd(1)
            await_init(dve)

            def draw_h(t, r):
                hrow = wide[:, r, 0:D]
                cb.link(dve.tensor_scalar(wide[:, 2, 0:D], product(r, 0), 0.0, None, ALU.max))
                cb.link(dve.scalar_tensor_tensor(hrow, product(r, 0), 0.0, wide[:, 2, 0:D], ALU.min, ALU.add))
                cb.link(dve.tensor_tensor(wide[:, 2, 0:D], hrow, ALR[:, 0:D], ALU.mult))
                dve.sem_inc(apart, 1)
                cb.link(dve.tensor_reduce(HL[:, bass.ds(t * HEADS, HEADS)],
                                          wide[:, 2, 0:D].rearrange("p (h f) -> p h f", h=HEADS), AX_X, ALU.add))
                cb.link(dve.tensor_tensor(wide[:, 2, 0:D], hrow, ALR[:, D:2 * D], ALU.mult))
                return dve.tensor_reduce(wide[:, r, D:AW], wide[:, 2, 0:D].rearrange("p (h f) -> p h f", h=HEADS),
                                         AX_X, ALU.add)
            project("l0", lambda t: normalize(X, t), 0, draw_h, 5, before=(0, 2))

            n, landed_B = 0, 0
            for i, (A, gain, offset, b, products) in enumerate(FOLDED):
                dve.wait_ge(fold_A_in, 64 * (i + 1))
                wait_past(dve, fold_out, 32 * n)
                for c in range(2):
                    ins = dve.tensor_scalar(Wc(fold_F, c), Wc(fold_A, c), fold_gain[:, c:c + 1], None, ALU.mult)
                ins.then_inc(fold_scaled, 1)
                dve.wait_ge(fold_turned, i + 1)
                dve.tensor_copy(fold_AT, psum[4][:, :])
                dve.tensor_tensor(fold_mid, psum[5][:, 0:2], fold_bias, ALU.add).then_inc(fold_turned_in, 1)
                for B, b1, k in products:
                    landed_B += 16 if b1 is None else 32
                    dve.wait_ge(fold_done, n + 1)
                    wait_past(dve, fold_out, 32 * n)
                    dve.wait_ge(fold_B_in, landed_B)
                    if b1 is None:
                        dve.tensor_copy(fold_row, psum[3][0:1, 0:D])
                    else:
                        dve.tensor_tensor(fold_row, psum[3][0:1, 0:D], fold_rowB, ALU.add)
                    dve.tensor_copy(fold_F, psum[2][:, :]).then_inc(fold_drawn, 1)
                    n = n + 1

            def split(link_, A, parts, rest):
                link_(dve.tensor_copy(parts[0], A))
                link_(dve.tensor_tensor(rest, A, parts[0], ALU.subtract))
                link_(dve.tensor_copy(parts[1], rest))
                return dve.tensor_tensor(parts[2], rest, parts[1], ALU.subtract)

            def one_hot(dest, head_, hw, v, r, scale=None):
                for g in range(G):
                    col = (v * G + g) * hw
                    ins = dve.tensor_scalar(dest[:, r, g, 0:P], (IOTAB if dest is ohb else IOTA)[:, 0:P], head_[:, bass.ds(col, 1)],
                                            None if scale is None else scale(v, g), ALU.is_equal,
                                            *([] if scale is None else [ALU.mult]))
                return ins

            def tiles_of(table, lag, ring=RING):
                return Tiles(mybir.EngineType.DVE, table, lag, ring)

            def accumulate(q, v, r, t, width, A=ACC, aw=AW):
                dve.wait_ge(part_ready, q + v + 1)
                wait_past(dve, acc_done, q + v)
                dve.tensor_tensor(A[:, bass.ds(t * aw, width)], psum[6 + r % 2][0:P, 0:width],
                                  A[:, bass.ds(t * aw, width)], ALU.add).then_inc(acc_done, 1)

            def clear():
                dve.memset(ACC[:, :], 0.0).then_inc(accs_clear, 1)

            dve.wait_ge(lists_in["dst"], 16)
            link(dve.tensor_copy(DIDX[:, :], DH[:, :].rearrange("p (b c) -> p b c", c=HW)[:, :, 1]))
            dve.sem_inc(lists_ready["dst"], 1)
            link(dve.memset(CNT[:, :], 0.0))

            def degrees(v, r, on):
                if on(0):
                    one_hot(oh, DH, HW, v, r).then_inc(oh_ready, 1)
                if on(2):
                    accumulate(0, v - 2, (r + 2) % RING, tiles.at(v, r), 2, CNT, 2)
            tiles = tiles_of(DTILE, 2)
            turns(dve, UNITS, RING, RING, 2, degrees)

            dve.wait_ge(lists_in["src"], 16)
            link(dve.tensor_copy(SIDX[:, :], SH[:, :].rearrange("p (b c) -> p b c", c=2)[:, :, 1]))
            dve.sem_inc(lists_ready["src"], 1)
            link(dve.memset(MX[:, :], -BIG))

            def maxima(v, r, on):
                if on(0):
                    for g in range(G):
                        ins = dve.tensor_scalar(oh[:, r, g, 0:P], IOTA[:, 0:P], SH[:, bass.ds((v * G + g) * 2, 1)],
                                                -BIG, ALU.not_equal, ALU.mult)
                    ins.then_inc(max_oh, 1)
                if on(3):
                    dve.wait_ge(max_rows, v - 2)
                    wait_past(dve, max_done, v - 3)
                    for k in range(2):
                        ins = dve.tensor_reduce(
                            wide[:, 3, D + 2 * k:D + 2 * k + 2],
                            psum[2 + 2 * ((r + 1) % 2) + k][0:P, :].rearrange("p (h e) -> p h e", h=2), AX_X, ALU.max)
                    cu.at(v - 3)
                    cu.link(ins)
                    dve.sem_inc(apart, 1)
                    t = tiles.at(v, r)
                    dve.tensor_tensor(MX[:, bass.ds(t * HEADS, HEADS)], wide[:, 3, D:AW],
                                      MX[:, bass.ds(t * HEADS, HEADS)], ALU.max).then_inc(max_done, 1)
            tiles = tiles_of(STILE, 3)
            turns(dve, UNITS, RING, RING, 3, maxima)
            dve.wait_ge(max_done, UNITS)
            clear()
            hm = HM[:, :].rearrange("p (t c) -> p t c", c=2 * HEADS)
            hl = HL[:, :].rearrange("p (t h) -> p t h", h=HEADS)
            mx = MX[:, :].rearrange("p (t h) -> p t h", h=HEADS)
            link(dve.tensor_copy(hm[:, :, 0:HEADS], hl))
            link(dve.tensor_tensor(mx, mx, hl, ALU.add))
            link(dve.scalar_tensor_tensor(hm[:, :, HEADS:], mx, ALPHA, mx, ALU.mult, ALU.max))
            parts = HMB.rearrange("p (k n) -> p k n", k=3)
            link(split(link, HM[:, :], [parts[:, k, :] for k in range(3)], wide[:, 0, 0:T * 2 * HEADS]))
            dve.sem_inc(hm_ready, 1)

            def attention(v, r, on):
                if on(6):
                    accumulate(UNITS, v - 6, (r + 2) % RING, tiles.at(v, r), AW)
                if on(3):
                    o = (r + 1) % RING
                    dve.wait_ge(mid_ready, v - 2)
                    dve.wait_ge(landed[o], landings("l0", v - 3, o))
                    cu.at(UNITS + (v - 3) * 3)
                    hs = psum[2 + o % 2][:, 0:G * 8].rearrange("p (g c) -> p g c", g=G)
                    e = small[:, o * 8:o * 8 + 8].rearrange("p (g h) -> p g h", g=G)
                    summed = cu.mark(dve.tensor_tensor(e, hs[:, :, 0:HEADS], gat[:, o, :, D:AW], ALU.add))
                if on(0):
                    one_hot(ohb, SH, 2, v, r).then_inc(oh_ready, 1)
                if on(3):
                    cu.await_(summed)
                    leaked = cu.mark(dve.scalar_tensor_tensor(e, e, ALPHA, e, ALU.mult, ALU.max))

                def weigh(g):
                    k = r % RING
                    return dve.tensor_tensor(
                        msg[:, k, g, 0:D].rearrange("p (h f) -> p h f", h=HEADS),
                        gat[:, k, g, 0:D].rearrange("p (h f) -> p h f", h=HEADS),
                        msg[:, k, g, D:AW].unsqueeze(2).broadcast_to([128, HEADS, HD]), ALU.mult)
                if on(4):
                    dve.wait_ge(probs, v - 3)
                    weigh(0)
                if on(3):
                    cu.await_(leaked)
                    lowered = cu.mark(dve.tensor_tensor(e, e, hs[:, :, HEADS:], ALU.subtract))
                if on(4):
                    weigh(1).then_inc(msgs, 1)
                if on(3):
                    cu.await_(lowered)
                    dve.tensor_scalar(e, e, 0.0, None, ALU.min).then_inc(scores, 1)
            tiles = tiles_of(STILE, 6, OHS)
            turns(dve, UNITS, OHS, OHS, 6, attention)
            dve.wait_ge(acc_done, 2 * UNITS)

            def acc(t, lo=0, hi=D):
                return tile(ACC, t, lo, hi, AW)

            accs = ACC[:, :].rearrange("p (t c) -> p t c", c=AW)
            rden = RDEN[:, :].rearrange("p (t h) -> p t h", h=HEADS)
            link(dve.tensor_scalar(rden, accs[:, :, D:AW], 1e-16, None, ALU.add))
            link(dve.reciprocal(rden, rden))

            def add_attention(i):
                sums = chunk(ACC, i, AW)
                heads_of = sums.rearrange("p t (h f) -> p t h f", h=HEADS)
                parts = RDEN[:, bass.ds(i * (CT * HEADS), CT * HEADS)].rearrange("p (t h) -> p t h", t=CT)
                ca.link(dve.tensor_tensor(heads_of, heads_of, parts.unsqueeze(3).broadcast_to([P, CT, HEADS, HD]),
                                          ALU.mult))
                ca.link(dve.tensor_tensor(chunk(X, i), chunk(X, i), sums, ALU.add))
                stats(X, i)
            chunks(5, add_attention)

            cnts = CNT[:, :].rearrange("p (t c) -> p t c", c=2)
            link(dve.tensor_scalar(cnts[:, :, 0], cnts[:, :, 0], 1.0, None, ALU.add))
            link(dve.tensor_scalar(RDEN[:, 0:T], cnts[:, :, 0], 0.0, None, ALU.is_gt))
            link(dve.tensor_scalar(cnts[:, :, 0], cnts[:, :, 0], 1e-30, None, ALU.max))
            dve.sem_inc(hm_ready, 1)
            dve.wait_ge(rooted, 2)
            link(dve.reciprocal(DINV[:, :], DINV[:, :]))
            link(dve.tensor_tensor(DINV[:, :], DINV[:, :], RDEN[:, 0:T], ALU.mult))
            dve.sem_inc(moments, 1)
            rstd(3)

            def dinv(t):
                return DINV[:, bass.ds(t, 1)]

            def draw_scaled(t, r):
                return dve.tensor_scalar(tile(Y, t), product(r, 0), dinv(t), None, ALU.mult)
            project("l1a", lambda t: normalize(X, t), 0, draw_scaled, 0)
            clear()

            def weighted(name):
                q = SCATTERS.index(name) * UNITS

                def unit(v, r, on):
                    if on(2):
                        accumulate(q, v - 2, (r + 2) % RING, tiles.at(v, r), D)
                    if on(0):
                        one_hot(oh, DH, HW, v, r, lambda v, g: DH[:, bass.ds((v * G + g) * HW + 2, 1)]
                                ).then_inc(oh_ready, 1)
                tiles = tiles_of(DTILE, 2)
                turns(dve, UNITS, RING, RING, 2, unit)
                dve.wait_ge(acc_done, q + UNITS)

            def convolved(t, b):
                link_ = ca.link
                dve.sem_inc(apart, 1)
                link_(dve.tensor_tensor(acc(t), acc(t), tile(Y, t), ALU.add))
                link_(dve.scalar_tensor_tensor(acc(t), acc(t), dinv(t), bias(b), ALU.mult, ALU.add))
                link_(dve.tensor_scalar(tile(KEEP, t), tile(KEEP, t), 0.0, 0.1, ALU.max, ALU.mult))
                return dve.scalar_tensor_tensor(tile(KEEP, t), acc(t), 0.9, tile(KEEP, t), ALU.mult, ALU.add)

            weighted("l1a")
            project("l1b", lambda t: convolved(t, 2), 3, draw_scaled, 0)
            clear()
            weighted("l1b")

            def add_convolved(i):
                sums = chunk(ACC, i, AW)
                ca.link(dve.tensor_tensor(sums, sums, chunk(Y, i), ALU.add))
                ca.link(dve.tensor_tensor(sums, sums, DINV[:, bass.ds(i * CT, CT)].unsqueeze(2).broadcast_to([P, CT, D]),
                                          ALU.mult))
                ca.link(dve.tensor_tensor(sums, sums, over_tiles(bias(3)), ALU.add))
                ca.link(dve.scalar_tensor_tensor(chunk(X, i), sums, 0.9, chunk(X, i), ALU.mult, ALU.add))
                ca.link(dve.scalar_tensor_tensor(chunk(X, i), chunk(KEEP, i), 0.1, chunk(X, i), ALU.mult, ALU.add))
                stats(X, i)
            chunks(8, add_convolved)
            dve.sem_inc(moments, 1)
            rstd(4)

            def draw_root(t, r):
                cb.link(dve.tensor_tensor(tile(Y, t), product(r, 0), bias(4), ALU.add))
                cb.link(dve.tensor_tensor(tile(X, t), product(r, 1), tile(X, t), ALU.add))
                return dve.tensor_scalar(tile(KEEP, t), tile(KEEP, t), 0.0, None, ALU.max)
            project("l2in", lambda t: normalize(X, t), 0, draw_root, 2)
            clear()

            def edge_messages(v, r, on):
                if on(2):
                    o = (r + 2) % RING
                    dve.wait_ge(mid_ready, UNITS + v - 1)
                    dve.wait_ge(landed[o], (GATHERS.index("l2") * (UNITS // RING) + laps(v - 2, o, RING) + 1) * 16 * G)
                    for g in range(G):
                        ins = dve.tensor_tensor(msg[:, o, g, 0:D], psum[2 + 2 * (o % 2) + g][:, 0:D],
                                                gat[:, o, g, 0:D], ALU.mult)
                    ins.then_inc(msgs, 1)
                if on(3):
                    accumulate(SCATTERS.index("l2") * UNITS, v - 3, (r + 1) % RING, tiles.at(v, r), D)
                if on(0):
                    one_hot(oh, DH, HW, v, r).then_inc(oh_ready, 1)
            tiles = tiles_of(DTILE, 3)
            turns(dve, UNITS, RING, 2 * RING, 3, edge_messages)
            dve.wait_ge(acc_done, (SCATTERS.index("l2") + 1) * UNITS)

            def draw_bn(t, r):
                cb.link(dve.tensor_tensor(tile(KEEP, t), product(r, 0), tile(Y, t), ALU.add))
                return dve.tensor_scalar(tile(KEEP, t), tile(KEEP, t), 0.0, None, ALU.max)
            project("l2out", None, 0, draw_bn, 1)
            mean, scale = wide[:, 0, 0:D], wide[:, 1, 0:D]
            dve.wait_ge(bn_sum, 1)
            link(dve.tensor_scalar(mean, psum[6][0:P, 0:D], 1.0 / N, None, ALU.mult))

            def squares(i):
                ca.link(dve.tensor_tensor(chunk(KEEP, i), chunk(KEEP, i), over_tiles(mean), ALU.subtract))
                dve.tensor_tensor(chunk(Y, i), chunk(KEEP, i), chunk(KEEP, i), ALU.mult).then_inc(bn_sq, CT)
            chunks(1, squares)
            dve.wait_ge(bn_sqsum, 1)
            link(dve.tensor_scalar(scale, psum[7][0:P, 0:D], 1.0 / N, None, ALU.mult))
            dve.sem_inc(bn_sqsum, 1)
            dve.wait_ge(rooted, 5)
            link(dve.reciprocal(scale, scale))
            link(dve.tensor_tensor(scale, scale, bias(5), ALU.mult))

            def add_bn(i):
                ca.link(dve.tensor_tensor(chunk(KEEP, i), chunk(KEEP, i), over_tiles(scale), ALU.mult))
                ca.link(dve.tensor_tensor(chunk(KEEP, i), chunk(KEEP, i), over_tiles(bias(6)), ALU.add))
                ca.link(dve.tensor_tensor(chunk(X, i), chunk(X, i), chunk(KEEP, i), ALU.add))
                stats(X, i)
            chunks(6, add_bn)
            dve.sem_inc(finished, 1)
            dve.sem_inc(moments, 1)
            heads = DH[:, :].rearrange("p (b c) -> p b c", c=HW)
            a_f, r_f = (BT[:, k * 3 * BLOCKS:(k + 1) * 3 * BLOCKS].rearrange("p (b c) -> p b c", c=3)
                        for k in range(2))
            heads_b = DH[:, :].bitcast(BF16).rearrange("p (b c) -> p b c", c=2 * HW)
            link(dve.tensor_copy(a_f, heads[:, :, 4:7]))
            link(split(link, a_f, [heads_b[:, :, 6 + 3 * k:9 + 3 * k] for k in range(3)], r_f))
            link(dve.memset(free_b[:, 0:RING * G * AK], 0.0))
            link(dve.memset(edge_in, 0.0))
            dve.sem_inc(edge_clear, 1)

            def edge_weights(s):
                dve.wait_ge(edge_rows_in, 16 * 9 * (s + 1))
                rest = wide[0:AK, 2, 0:D]
                link(dve.tensor_copy(edge_w, edge_in))
                link(dve.tensor_tensor(rest, edge_in, edge_w, ALU.subtract))
                link(dve.tensor_copy(edge_w[32:64, :], rest[32:64, :]))
                link(dve.tensor_copy(edge_w[64:AK, :], rest[64:AK, :]))
                link(dve.tensor_tensor(edge_w[64:AK, :], rest[64:AK, :], edge_w[64:AK, :], ALU.subtract))
                dve.sem_inc(edge_split, 1)
                if s < S3 - 1:
                    dve.sem_inc(edge_clear, 1)

            def own(t, k):
                if k < 2:
                    return BTB[0:P, bass.ds(t * 2 * D + k * D, D)]
                return KEEPB[:, bass.ds(t * 2 * D, D)]

            def draw_tables(t, r):
                rest = wide[:, 3, 0:D]
                own_sum = cb.mark(dve.tensor_tensor(wide[:, 2, 0:D], product(r, 1), bias(0), ALU.add))
                cb.mark(dve.tensor_tensor(wide[:, r, 0:D], product(r, 0), bias(7), ALU.add))
                cb.await_(own_sum)
                hi = cb.mark(dve.tensor_scalar(own(t, 0), wide[:, 2, 0:D], 1.0, None, ALU.mult))
                cb.mark(dve.tensor_tensor(tile(Y, t), product(r, 2), bias(1), ALU.add))
                cb.await_(hi)
                cb.link(dve.tensor_tensor(rest, wide[:, 2, 0:D], own(t, 0), ALU.subtract))
                cb.link(dve.tensor_scalar(own(t, 1), rest, 1.0, None, ALU.mult))
                return dve.tensor_tensor(own(t, 2), rest, own(t, 1), ALU.subtract)

            rstd(6)
            link(dve.memset(bias(7), 0.0))
            await_tables(dve, 0)
            project("l3in", lambda t: normalize(X, t), 0, draw_tables, 6, before=(ROWS.index("l3in"), 1))
            for s in range(S3):
                q = SCATTERS.index(f"e{s}") * UNITS
                m0 = MSGS_BEFORE_E + s * UNITS
                clear()
                edge_weights(s)

                def edge_net(v, r, on):
                    if on(7):
                        accumulate(q, v - 7, (r + 1) % RING, tiles.at(v, r), D + 2)
                    if on(0):
                        dve.tensor_copy(
                            atb[:, r % RING, :, :].rearrange("p g (q c) -> p g q c", q=3)[:, :, :, 0:9],
                            DH[:, bass.ds(v * G * HW, G * HW)].bitcast(BF16).rearrange("p (g c) -> p g c", g=G)
                            [:, :, 6:15].unsqueeze(2).broadcast_to([128, G, 3, 9]))
                        one_hot(ohb, DH, HW, v, r).then_inc(oh_ready, 1)
                    if on(5):
                        o = (r + 3) % RING
                        dve.wait_ge(msg_sd, s * UNITS + v - 4)
                        dve.reciprocal(small[:, 8 + o * 2:8 + o * 2 + 2], small[:, o * 2:o * 2 + 2]).then_inc(recip, 1)
                    if on(4):
                        o = r % RING
                        dve.wait_ge(msg_relu, s * UNITS + v - 3)
                        for g in range(G):
                            ins = dve.bn_stats(small[:, 16 + g * 6:22 + g * 6], msg[:, o, g, 0:D])
                        cu.at(cu0 + (v - 4))
                        taken = cu.mark(ins)
                    if on(3):
                        o = (r + 1) % RING
                        dve.wait_ge(mid_ready, 2 * UNITS + s * UNITS + v - 2)
                        dve.wait_ge(landed[o], landings(f"e{s}", v - 3, o))
                        dve.tensor_tensor(msg[:, o, :, 0:D], psum[2 + o % 2][:, :].rearrange("p (g f) -> p g f", g=G),
                                          gat[:, o, :, 0:D], ALU.add).then_inc(msgs, 1)
                    if on(4):
                        o = r % RING
                        cu.await_(taken)
                        dve.sem_inc(apart, 1)
                        for g in range(G):
                            dve.bn_aggr(msg[:, o, g, D:D + 2], small[:, 16 + g * 6:22 + g * 6]).then_inc(msg_stats, 1)
                cu0 = UNITS * 4 + s * UNITS
                tiles = tiles_of(DTILE, 7, OHS)
                turns(dve, UNITS, OHS, OHS, 7, edge_net)
                dve.wait_ge(acc_done, q + UNITS)
                await_nets(dve, s)

                def summed(t):
                    dve.sem_inc(apart, 1)
                    return dve.tensor_scalar(tile(KEEP, t), acc(t), acc(t, D, D + 1), None, ALU.subtract)

                def draw_mix(t, r):
                    cb.link(dve.scalar_tensor_tensor(tile(KEEP, t), bias(4), CNT[:, bass.ds(t * 2 + 1, 1)],
                                                     product(r, 0), ALU.mult, ALU.add))
                    cb.link(dve.tensor_tensor(tile(KEEP, t), tile(KEEP, t), tile(Y, t), ALU.add))
                    return dve.tensor_scalar(tile(KEEP, t), tile(KEEP, t), 0.0, None, ALU.max)
                project(f"mix{s}", summed, 0, draw_mix, 2)
                dve.wait_ge(drawn, T * (PHASES.index(f"mix{s}") + 1))
                chunks(3, lambda i: stats(KEEP, i))
                dve.sem_inc(moments, 1)
                rstd(7 + s)

                def normed(t):
                    dve.sem_inc(apart, 1)
                    ca.link(normalize(KEEP, t))
                    ca.link(dve.tensor_tensor(tile(KEEP, t), tile(KEEP, t), bias(5), ALU.mult))
                    return dve.tensor_tensor(tile(KEEP, t), tile(KEEP, t), bias(6), ALU.add)

                def draw_last(t, r):
                    cb.link(dve.tensor_tensor(acc(t), product(r, 0), bias(7), ALU.add))
                    return dve.tensor_tensor(tile(X, t), acc(t), tile(X, t), ALU.add)
                if s < S3 - 1:
                    await_tables(dve, s + 1)
                    project(f"next{s}", lambda t: normalize(KEEP, t), 0, draw_tables, 6,
                            before=(ROWS.index(f"next{s}"), 1))
                else:
                    project(f"next{s}", normed, 2, draw_last, 1)
            dve.wait_ge(drawn, T * len(PHASES))
            dve.sem_inc(finished, LAST - 1)

        @block.tensor
        def _(pe):
            pe.wait_ge(consts, 9)
            for which in range(2):
                pe.wait_ge(placed, which) if which else None
                pe.wait_ge(counted, which + 1)
                pe.matmul(psum[2][:, 0:T], ONES[0:P, :], count[:, :], start=True, stop=True)
                pe.matmul(psum[3][0:P, 0:T], LTRI[0:P, 0:P], count[:, :], start=True, stop=True).then_inc(prefixed, 1)

            def project(name, weights, extra=None):
                k = PHASES.index(name) * T

                def step(t, r, on):
                    if on(0):
                        pe.wait_ge(staged_in, k + t + 1)
                        wait_past(pe, turned_in, k + t - 1)
                        for c in range(2):
                            ins = pe.transpose(psum[r][:, c * P:(c + 1) * P], staged[:, r, c * 128:(c + 1) * 128],
                                               IDENT[0:P, 0:P])
                        ins.then_inc(turned, 1)
                    if on(1):
                        o = (r + 1) % 2
                        pe.wait_ge(turned_in, k + t)
                        wait_past(pe, drawn, k + t - 2)
                        for j, W in enumerate(weights):
                            place = psum[2 + o][0:P, j * D:(j + 1) * D] if j < 2 else psum[4 + o][0:P, 0:D]
                            for c in range(2):
                                ins = pe.matmul(place, hT[:, o, c * P:(c + 1) * P], Wc(W, c), start=(c == 0), stop=(c == 1))
                        ins.then_inc(projected, 1)
                    if extra is not None and on(3):
                        pe.wait_ge(drawn, k + t - 2)
                        extra(t - 3)
                turns(pe, T, 2, 4, 3 if extra else 1, step)

            await_init(pe)
            project("l0", [W0])

            n, landed_B = 0, 0
            for i, (A, gain, offset, b, products) in enumerate(FOLDED):
                pe.wait_ge(fold_A_in, 64 * (i + 1))
                for m in range(2):
                    for c in range(2):
                        pe.matmul(psum[5][:, m:m + 1], fold_A[:, c * D + m * 128:c * D + (m + 1) * 128],
                                  fold_offset[:, c:c + 1], start=(c == 0), stop=(c == 1))
                pe.wait_ge(fold_scaled, i + 1)
                for m in range(2):
                    for c in range(2):
                        ins = pe.transpose(psum[4][:, m * D + c * 128:m * D + (c + 1) * 128],
                                           fold_F[:, c * D + m * 128:c * D + (m + 1) * 128], IDENT[:, :])
                ins.then_inc(fold_turned, 1)
                pe.wait_ge(fold_turned_in, i + 1)
                for B, b1, k in products:
                    landed_B += 16 if b1 is None else 32
                    pe.wait_ge(fold_B_in, landed_B)
                    wait_past(pe, fold_drawn, n)
                    for m in range(2):
                        pe.matmul(psum[3][0:1, 0:D], fold_mid[:, m:m + 1], Wc(fold_B, m), start=(m == 0), stop=(m == 1))
                    for c in range(2):
                        for m in range(2):
                            ins = pe.matmul(psum[2][:, c * D:(c + 1) * D], fold_AT[:, m * D + c * 128:m * D + (c + 1) * 128],
                                            Wc(fold_B, m), start=(m == 0), stop=(m == 1))
                    ins.then_inc(fold_done, 1)
                    n = n + 1

            def scatter(q, v, r, lhs, rhs, width, ready, value):
                pe.wait_ge(ready, value)
                wait_past(pe, acc_done, q + v - 1)
                for g in range(G):
                    ins = pe.matmul(psum[6 + r % 2][0:P, 0:width], lhs(g), rhs(g), start=(g == 0), stop=(g == G - 1))
                return ins.then_inc(part_ready, 1)

            def await_gather(name, v, r):
                pe.wait_ge(landed[r], (GATHERS.index(name) * (UNITS // RING) + laps(v, r, RING) + 1) * 16 * G)

            def degrees(v, r, on):
                scatter(0, v, r, lambda g: oh[:, r, g, 0:P],
                        lambda g: DH[:, bass.ds((v * G + g) * HW + 2, 2)], 2, oh_ready, v + 1)
            pe.wait_ge(lists_in["dst"], 16)
            turns(pe, UNITS, RING, RING, 0, degrees)

            def maxima(v, r, on):
                pe.wait_ge(max_neg, v + 1)
                wait_past(pe, max_done, v - 1)
                for h in range(HEADS):
                    for g in range(G):
                        ins = pe.transpose(
                            psum[2 + 2 * (r % 2) + h // 2][0:P, (h % 2) * 256 + g * 128:(h % 2) * 256 + g * 128 + 128],
                            cand[:, r % 2, h, g, :], IDENT[:, :])
                ins.then_inc(max_rows, 1)
            turns(pe, UNITS, RING, RING, 0, maxima)

            def turn_one_hot(qt, q, v, r, attrs):
                pe.wait_ge(oh_ready, q + v + 1)
                wait_past(pe, ohT_ready, qt + v - 1)
                for g in range(G):
                    ins = pe.transpose(psum_b[r % 2][0:P, g * 128:(g + 1) * 128], ohb[:, r, g, :], IDENTB[:, :])
                    if attrs:
                        ins = pe.transpose(psum_b[r % 2][0:AK, (G + g) * 128:(G + g + 1) * 128], atb[:, r % RING, g, :],
                                           IDENTB[:, :])
                ins.then_inc(oh_turned, 1)

            def attention(v, r, on):
                if on(2):
                    o = (r + 2) % RING
                    pe.wait_ge(ohT_ready, v - 1)
                    t = tiles.at(v, r)
                    wait_past(pe, scores, v - 3)
                    for g in range(G):
                        for k in range(3):
                            ins = pe.matmul(psum[2 + o % 2][:, g * 8:g * 8 + 8], ohbT[0:P, o, g * 128:(g + 1) * 128],
                                            HMB[:, bass.ds(k * T * 8 + t * 8, 8)], start=(k == 0), stop=(k == 2))
                    ins.then_inc(mid_ready, 1)
                if on(1):
                    turn_one_hot(0, UNITS, v - 1, (r + 7) % OHS, False)
                if on(5):
                    o = (r + 3) % RING
                    pe.wait_ge(ohw_ready, v - 4)
                    scatter(UNITS, v - 5, o, lambda g: ohw[:, o % 2, g, :], lambda g: msg[:, o, g, :], AW, msgs, v - 4)
            pe.wait_ge(hm_ready, 1)
            tiles = Tiles(mybir.EngineType.PE, STILE, 2, OHS)
            turns(pe, UNITS, OHS, OHS, 5, attention)
            project("l1a", [WA])

            def weighted(name):
                q = SCATTERS.index(name) * UNITS

                def unit(v, r, on):
                    await_gather(name, v, r)
                    scatter(q, v, r, lambda g: oh[:, r, g, 0:P], lambda g: gat[:, r, g, 0:D], D, oh_ready, q + v + 1)
                turns(pe, UNITS, RING, RING, 0, unit)
            weighted("l1a")
            project("l1b", [WB])
            weighted("l1b")
            project("l2in", [WC, WD])

            def edge_messages(v, r, on):
                if on(0):
                    pe.wait_ge(attrs_in[r], (laps(v, r, RING) + 1) * 16)
                    wait_past(pe, ohT_ready, UNITS + v - 1)
                    pe.transpose(psum[r % 2][:, 0:128], attr_slot(r), IDENT[:, :]).then_inc(oh_turned, 1)
                if on(1):
                    o = (r + 3) % RING
                    pe.wait_ge(ohT_ready, UNITS + v)
                    wait_past(pe, msgs, UNITS + v - 2)
                    for g in range(G):
                        ins = pe.matmul(psum[2 + 2 * (o % 2) + g][:, 0:D], ohT[g * EA:(g + 1) * EA, o, 0:128],
                                        WE[g * EA:(g + 1) * EA, :], start=True, stop=True)
                    ins.then_inc(mid_ready, 1)
                if on(2):
                    o = (r + 2) % RING
                    q = SCATTERS.index("l2") * UNITS
                    pe.wait_ge(oh_ready, q + v - 1)
                    scatter(q, v - 2, o, lambda g: oh[:, o, g, 0:P], lambda g: msg[:, o, g, 0:D], D, msgs, UNITS + v - 1)
            turns(pe, UNITS, RING, 2 * RING, 2, edge_messages)

            def bn_sums(t):
                ins = pe.matmul(psum[6][0:P, 0:D], ONES[0:P, 0:P], tile(KEEP, t), start=isinstance(t, int) and t == 0,
                                stop=isinstance(t, int) and t == T - 1)
                if isinstance(t, int) and t == T - 1:
                    ins.then_inc(bn_sum, 1)
            project("l2out", [WF], bn_sums)

            def bn_squares(t, r, on):
                pe.wait_ge(bn_sq, t + 1)
                ins = pe.matmul(psum[7][0:P, 0:D], ONES[0:P, 0:P], tile(Y, t), start=isinstance(t, int) and t == 0,
                                stop=isinstance(t, int) and t == T - 1)
                if isinstance(t, int) and t == T - 1:
                    ins.then_inc(bn_sqsum, 1)
            turns(pe, T, 2, 2, 0, bn_squares)
            await_tables(pe, 0)
            project("l3in", [W0, WA, WB])
            for s in range(S3):
                q = SCATTERS.index(f"e{s}") * UNITS
                qt = TURNS_BEFORE_E + s * UNITS
                pe.wait_ge(edge_split, s + 1)

                def edge_net(v, r, on):
                    if on(2):
                        o = (r + 2) % RING
                        pe.wait_ge(ohT_ready, qt + v - 1)
                        t = tiles.at(v, r)
                        wait_past(pe, msgs, MSGS_BEFORE_E + s * UNITS + v - 3)
                        for g in range(G):
                            place = psum[2 + o % 2][:, g * D:(g + 1) * D]
                            own_T = ohbT[0:P, o, g * 128:(g + 1) * 128]
                            pe.matmul(place, own_T, BTB[0:P, bass.ds(t * 2 * D, D)], start=True, stop=False)
                            pe.matmul(place, own_T, BTB[0:P, bass.ds(t * 2 * D + D, D)], start=False, stop=False)
                            pe.matmul(place, own_T, KEEPB[:, bass.ds(t * 2 * D, D)], start=False, stop=False)
                            ins = pe.matmul(place, atT[:, o, g * 128:(g + 1) * 128], edge_w, start=False, stop=True)
                        ins.then_inc(mid_ready, 1)
                    if on(1):
                        turn_one_hot(qt, q, v - 1, (r + 7) % OHS, True)
                    if on(6):
                        o = (r + 2) % RING
                        scatter(q, v - 6, o, lambda g: ohw[:, o % 2, g, :], lambda g: msg[:, o, g, 0:D + 2], D + 2,
                                ohw_ready, (s + 1) * UNITS + v - 5)
                tiles = Tiles(mybir.EngineType.PE, DTILE, 2, OHS)
                turns(pe, UNITS, OHS, OHS, 6, edge_net)
                await_nets(pe, s)
                project(f"mix{s}", [WD])
                if s < S3 - 1:
                    await_tables(pe, s + 1)
                    project(f"next{s}", [W0, WA, WB])
                else:
                    project(f"next{s}", [WF])


_INS = ["x", "src", "dst", "edge_attr_3", "edge_attr_64", "edge_weight", "L0_gnn_W", "L0_gnn_a_l", "L0_gnn_a_r",
        "L1_gnn_W1", "L1_gnn_b1", "L1_gnn_W2", "L1_gnn_b2", "L2_gnn_W_edge", "L2_gnn_W_rel", "L2_gnn_b_rel",
        "L2_gnn_W_root", "L2_gnn_gamma", "L2_gnn_beta", "L2_gnn_W_res", "L3_gnn_W1e", "L3_gnn_b1e", "L3_gnn_ge",
        "L3_gnn_oe", "L3_gnn_W2e", "L3_gnn_b2e", "L3_gnn_W1n", "L3_gnn_b1n", "L3_gnn_gn", "L3_gnn_on",
        "L3_gnn_W2n", "L3_gnn_b2n"]


def kernel(**inputs):
    import numpy as _np
    import concourse.bacc as _bacc
    from concourse import mybir as _mybir
    from concourse.bass_utils import run_bass_kernel_spmd as _run

    nc = _bacc.Bacc("TRN2", target_bir_lowering=False, num_devices=1)
    arrays, args = {}, []
    for name in _INS:
        a = _np.ascontiguousarray(inputs[name])
        arrays[f"in_{name}"] = a
        args.append(nc.dram_tensor(f"in_{name}", a.shape, _mybir.dt.from_np(a.dtype), kind="ExternalInput").ap())
    args.append(nc.dram_tensor("out_0", (N, D), _mybir.dt.float32, kind="ExternalOutput").ap())
    build(nc, *args)
    r = _run(nc, [arrays], core_ids=[0])
    return r.results[0]["out_0"]
```
